# Optimizing a Trainium2 kernel written in Bass

```python
import numpy as np
import jax
import jax.numpy as jnp

def _softmax(x, axis=-1):
    return jax.nn.softmax(x, axis=axis)

def _gelu(x):
    return jax.nn.gelu(x, approximate=True)

def _silu(x):
    return jax.nn.silu(x)

def _sigmoid(x):
    return jax.nn.sigmoid(x)

def _layernorm(x, axis=-1, eps=1e-05):
    m = jnp.mean(x, axis=axis, keepdims=True)
    v = jnp.var(x, axis=axis, keepdims=True)
    return (x - m) / jnp.sqrt(v + eps)

def _scatter_add(tgt, idx, src, axis=0):
    return tgt.at[idx].add(src)

def _segment_sum(src, seg, n):
    return jax.ops.segment_sum(src, seg, n)
kernel_name = 'mk_flamingo_gated_d2_seqx_r4_776502'

def setup_inputs(seed: int=0):
    np.random.seed(seed)
    _w = jnp.asarray

    def _rec_inputs():
        import jax
        import jax.numpy as jnp
        _rk = jax.random.key(seed)
        x = -0.000125 + 0.9999 * jax.random.normal(jax.random.fold_in(_rk, 1), (32, 128, 256), jnp.float32)
        _lenS = 128 - jax.random.randint(jax.random.fold_in(_rk, 7), (32,), 0, max(1, 128 // 4) + 1, jnp.int32)
        _lenS2 = 128 - jax.random.randint(jax.random.fold_in(_rk, 8), (32,), 0, max(1, 128 // 4) + 1, jnp.int32)
        _ctx_1024P = jax.random.normal(jax.random.fold_in(_rk, 11), (32, 16, 256), jnp.float32)
        _ctx_1024c = jax.random.dirichlet(jax.random.fold_in(_rk, 511), 0.3 * jnp.ones((16,), jnp.float32), (32, 128))
        _ctx_1024t = jnp.einsum('bsk,bkd->bsd', _ctx_1024c, _ctx_1024P)
        _ctx_1024t = _ctx_1024t * jax.lax.rsqrt(jnp.mean(jnp.square(_ctx_1024t)) + 1e-12) * 0.953939
        ctx_1024 = -1.52775e-05 + 0.999936 * (_ctx_1024t + 0.3 * jax.random.normal(jax.random.fold_in(_rk, 611), (32, 128, 256), jnp.float32))
        _validS = jnp.arange(128)[None, :] < _lenS[:, None]
        _validS2 = jnp.arange(128)[None, :] < _lenS2[:, None]
        _causal = jnp.tril(jnp.ones((128, 128), dtype=bool))
        mask_BxS2_ik0 = jnp.where(jnp.broadcast_to(_validS2[:, :], (32, 128)), 0, 1).astype(jnp.int32)
        _g = jax.random.normal(jax.random.fold_in(_rk, 9001), (2, 2), jnp.float32)
        _g = jnp.sign(_g) * jnp.maximum(jnp.abs(_g), 1.0) + (_g == 0) * 1.0
        g_xattn = _g[0]
        g_ffn = _g[1]
        return (x, ctx_1024, mask_BxS2_ik0, g_xattn, g_ffn)
    x, ctx_1024, mask_BxS2_ik0, g_xattn, g_ffn = _rec_inputs()

    def _L0_xattn_setup():
        import jax, jax.numpy as jnp
        import numpy as np
        DECAY = 0.9
        key = jax.random.key(seed)
        k1, k2, k3 = jax.random.split(key, 3)
        B, S, D = (8, 1024, 256)
        q = jax.random.normal(k1, (B, S, D), dtype=jnp.float32)
        k = jax.random.normal(k2, (B, S, D), dtype=jnp.float32)
        v = jax.random.normal(k3, (B, S, D), dtype=jnp.float32)
        return {'q': q, 'k': k, 'v': v}
    _L0_xattn_all = _L0_xattn_setup()
    _L0_xattn_in = {k: v for k, v in _L0_xattn_all.items() if k in ()}
    del _L0_xattn_all

    def _L0_ffn_setup():
        import jax, jax.numpy as jnp
        import numpy as np
        B, C, D, O = (4, 1024, 256, 256)
        PROJ = 64
        RANKS = [1, 2, 4, 8]
        E = len(RANKS)
        CLAMP_MAX = float(np.log(1.0 / 0.01))

        def _l2norm(v, axis):
            return v / jnp.maximum(jnp.linalg.norm(v, axis=axis, keepdims=True), 1e-12)
        key = jax.random.key(seed)
        ks = jax.random.split(key, 16)
        inp = {'x': jax.random.normal(ks[0], (B, C, D), dtype=jnp.float32), 'W': jax.random.normal(ks[1], (O, D), dtype=jnp.float32) / np.sqrt(D), 'Wp': jax.random.normal(ks[2], (PROJ, D), dtype=jnp.float32) / np.sqrt(D), 'bp': jnp.zeros((PROJ,), dtype=jnp.float32), 'sim': jax.random.normal(ks[3], (PROJ, E), dtype=jnp.float32) * 0.01, 'temp': jnp.full((1,), np.log(1.0 / 0.5), dtype=jnp.float32)}
        for i, r in enumerate(RANKS):
            inp[f'Wd{i}'] = jax.random.normal(ks[4 + 2 * i], (r, D), dtype=jnp.float32) / r
            inp[f'Wu{i}'] = jax.random.normal(ks[5 + 2 * i], (O, r), dtype=jnp.float32) * 0.01
        return inp
    _L0_ffn_all = _L0_ffn_setup()
    _L0_ffn_in = {k: v for k, v in _L0_ffn_all.items() if k in ('W', 'Wp', 'bp', 'sim', 'temp', 'Wd0', 'Wu0', 'Wd1', 'Wu1', 'Wd2', 'Wu2', 'Wd3', 'Wu3')}
    del _L0_ffn_all

    def _L1_xattn_setup():
        import jax, jax.numpy as jnp
        import numpy as np
        BSZ, QLEN, KLEN = (2, 256, 512)
        QD = KD = VD = HID = 256
        NH = 16
        HD = HID // NH
        SCALE = 1.0 / HD ** 0.5
        NEG_INF = -1e+30
        key = jax.random.key(seed)
        ks = jax.random.split(key, 8)
        query = jax.random.normal(ks[0], (BSZ, QLEN, QD), dtype=jnp.float32)
        k_in = jax.random.normal(ks[1], (BSZ, KLEN, KD), dtype=jnp.float32)
        v_in = jax.random.normal(ks[2], (BSZ, KLEN, VD), dtype=jnp.float32)
        attn_mask = jax.random.randint(ks[3], (BSZ, KLEN), 0, 2, dtype=jnp.int32)

        def xavier(k, fan_in, fan_out):
            lim = (6.0 / (fan_in + fan_out)) ** 0.5
            return jax.random.uniform(k, (fan_in, fan_out), jnp.float32, -lim, lim)
        Wq = xavier(ks[4], QD, HID)
        Wk = xavier(ks[5], KD, HID)
        Wv = xavier(ks[6], VD, HID)
        Wo = xavier(ks[7], HID, QD)
        return {'query': query, 'key': k_in, 'value': v_in, 'attn_mask': attn_mask, 'Wq': Wq, 'Wk': Wk, 'Wv': Wv, 'Wo': Wo}
    _L1_xattn_all = _L1_xattn_setup()
    _L1_xattn_in = {k: v for k, v in _L1_xattn_all.items() if k in ('Wq', 'Wk', 'Wv', 'Wo')}
    del _L1_xattn_all

    def _L1_ffn_setup():
        import jax, jax.numpy as jnp
        import numpy as np
        D, H, E, K = (256, 256, 8, 2)

        def _moe(x, router_w, w_in, b_in, w_out, b_out):
            B, S, Dm = x.shape
            T = B * S
            x2 = x.reshape(T, Dm)
            logits = x2 @ router_w
            probs = jax.nn.softmax(logits, axis=-1)
            top_p, top_e = jax.lax.top_k(probs, K)
            flat_e = top_e.reshape(-1)
            flat_p = top_p.reshape(-1)
            tok = jnp.repeat(jnp.arange(T), K)
            order = jnp.argsort(flat_e)
            se, sp, st = (flat_e[order], flat_p[order], tok[order])
            xd = x2[st]
            N = xd.shape[0]
            h = jnp.zeros((N, H), x.dtype)
            for e in range(E):
                m = (se == e)[:, None]
                h = h + jnp.where(m, jax.nn.gelu(xd @ w_in[e] + b_in[e]), 0.0)
            y = jnp.zeros((N, Dm), x.dtype)
            for e in range(E):
                m = (se == e)[:, None]
                y = y + jnp.where(m, h @ w_out[e] + b_out[e], 0.0)
            y = y * sp[:, None]
            out = jnp.zeros((T, Dm), x.dtype).at[st].add(y)
            return out.reshape(B, S, Dm)
        key = jax.random.key(seed)
        ks = jax.random.split(key, 5)
        s = lambda k, shape, scale: jax.random.normal(k, shape, dtype=jnp.float32) * scale
        return {'input_batch': s(ks[0], (2, 128, D), 1.0), 'router_w': s(ks[1], (D, E), D ** (-0.5)), 'w_in': s(ks[2], (E, D, H), D ** (-0.5)), 'b_in': jnp.zeros((E, H), jnp.float32), 'w_out': s(ks[3], (E, H, D), H ** (-0.5)), 'b_out': jnp.zeros((E, D), jnp.float32)}
    _L1_ffn_all = _L1_ffn_setup()
    _L1_ffn_in = {k: v for k, v in _L1_ffn_all.items() if k in ('router_w', 'w_in', 'b_in', 'w_out', 'b_out')}
    del _L1_ffn_all
    return {'x': x, 'ctx_1024': ctx_1024, 'mask_BxS2_ik0': mask_BxS2_ik0, 'g_xattn': g_xattn, 'g_ffn': g_ffn, 'L0_ffn_W': _L0_ffn_in['W'], 'L0_ffn_Wp': _L0_ffn_in['Wp'], 'L0_ffn_bp': _L0_ffn_in['bp'], 'L0_ffn_sim': _L0_ffn_in['sim'], 'L0_ffn_temp': _L0_ffn_in['temp'], 'L0_ffn_Wd0': _L0_ffn_in['Wd0'], 'L0_ffn_Wu0': _L0_ffn_in['Wu0'], 'L0_ffn_Wd1': _L0_ffn_in['Wd1'], 'L0_ffn_Wu1': _L0_ffn_in['Wu1'], 'L0_ffn_Wd2': _L0_ffn_in['Wd2'], 'L0_ffn_Wu2': _L0_ffn_in['Wu2'], 'L0_ffn_Wd3': _L0_ffn_in['Wd3'], 'L0_ffn_Wu3': _L0_ffn_in['Wu3'], 'L1_xattn_Wq': _L1_xattn_in['Wq'], 'L1_xattn_Wk': _L1_xattn_in['Wk'], 'L1_xattn_Wv': _L1_xattn_in['Wv'], 'L1_xattn_Wo': _L1_xattn_in['Wo'], 'L1_ffn_router_w': _L1_ffn_in['router_w'], 'L1_ffn_w_in': _L1_ffn_in['w_in'], 'L1_ffn_b_in': _L1_ffn_in['b_in'], 'L1_ffn_w_out': _L1_ffn_in['w_out'], 'L1_ffn_b_out': _L1_ffn_in['b_out']}

def reference(x, ctx_1024, mask_BxS2_ik0, g_xattn, g_ffn, L0_ffn_W, L0_ffn_Wp, L0_ffn_bp, L0_ffn_sim, L0_ffn_temp, L0_ffn_Wd0, L0_ffn_Wu0, L0_ffn_Wd1, L0_ffn_Wu1, L0_ffn_Wd2, L0_ffn_Wu2, L0_ffn_Wd3, L0_ffn_Wu3, L1_xattn_Wq, L1_xattn_Wk, L1_xattn_Wv, L1_xattn_Wo, L1_ffn_router_w, L1_ffn_w_in, L1_ffn_b_in, L1_ffn_w_out, L1_ffn_b_out):
    import jax
    import jax.numpy as jnp

    def _L0_xattn_ref(q, k, v):
        import jax, jax.numpy as jnp
        import numpy as np
        DECAY = 0.9
        kv = jnp.swapaxes(k * v, 0, 1)

        def step(r, kv_t):
            r = DECAY * r + kv_t
            return (r, r)
        r0 = jnp.zeros(q.shape[:1] + q.shape[2:], dtype=q.dtype)
        _, rs = jax.lax.scan(step, r0, kv)
        return q * jnp.swapaxes(rs, 0, 1)

    def _L0_ffn_ref(x, W, Wp, bp, sim, temp, Wd0, Wu0, Wd1, Wu1, Wd2, Wu2, Wd3, Wu3):
        import jax, jax.numpy as jnp
        import numpy as np
        B, C, D, O = (4, 1024, 256, 256)
        PROJ = 64
        RANKS = [1, 2, 4, 8]
        E = len(RANKS)
        CLAMP_MAX = float(np.log(1.0 / 0.01))

        def _l2norm(v, axis):
            return v / jnp.maximum(jnp.linalg.norm(v, axis=axis, keepdims=True), 1e-12)
        base = jnp.einsum('bcd,od->bco', x, W)
        xf = x.reshape(-1, x.shape[-1])
        proj = _l2norm(xf @ Wp.T + bp, axis=1)
        simn = _l2norm(sim, axis=0)
        scale = jnp.exp(jnp.minimum(temp, CLAMP_MAX))
        logits = proj @ simn * scale
        lw = jax.nn.softmax(logits, axis=1)
        top1 = jnp.argmax(lw, axis=1)
        ret = jnp.where(jnp.arange(E)[None, :] == top1[:, None], lw, 0.0)
        ret = ret.reshape(x.shape[0], x.shape[1], E)
        downs = (Wd0, Wd1, Wd2, Wd3)
        ups = (Wu0, Wu1, Wu2, Wu3)
        l = jnp.stack([jnp.einsum('bcr,or->bco', jnp.einsum('bcd,rd->bcr', x, d), u) for d, u in zip(downs, ups)], axis=2)
        res = jnp.sum(ret[..., None] * l, axis=2)
        return base + res

    def _L1_xattn_ref(query, key, value, attn_mask, Wq, Wk, Wv, Wo):
        import jax, jax.numpy as jnp
        import numpy as np
        BSZ, QLEN, KLEN = (2, 256, 512)
        QD = KD = VD = HID = 256
        NH = 16
        HD = HID // NH
        SCALE = 1.0 / HD ** 0.5
        NEG_INF = -1e+30
        bsz, qlen, _ = query.shape
        klen = key.shape[1]
        head_q = (query @ Wq).reshape(bsz, qlen, NH, HD)
        head_k = (key @ Wk).reshape(bsz, klen, NH, HD)
        head_v = (value @ Wv).reshape(bsz, klen, NH, HD)
        attn_score = jnp.einsum('bind,bjnd->bijn', head_q, head_k) * SCALE
        mask = (attn_mask == 0)[:, None, :, None]
        attn_score = jnp.where(mask, NEG_INF, attn_score)
        attn_prob = jax.nn.sigmoid(attn_score)
        attn_vec = jnp.einsum('bijn,bjnd->bind', attn_prob, head_v)
        attn_vec = attn_vec.reshape(bsz, qlen, HID)
        return attn_vec @ Wo

    def _L1_ffn_ref(input_batch, router_w, w_in, b_in, w_out, b_out):
        import jax, jax.numpy as jnp
        import numpy as np
        D, H, E, K = (256, 256, 8, 2)

        def _moe(x, router_w, w_in, b_in, w_out, b_out):
            B, S, Dm = x.shape
            T = B * S
            x2 = x.reshape(T, Dm)
            logits = x2 @ router_w
            probs = jax.nn.softmax(logits, axis=-1)
            top_p, top_e = jax.lax.top_k(probs, K)
            flat_e = top_e.reshape(-1)
            flat_p = top_p.reshape(-1)
            tok = jnp.repeat(jnp.arange(T), K)
            order = jnp.argsort(flat_e)
            se, sp, st = (flat_e[order], flat_p[order], tok[order])
            xd = x2[st]
            N = xd.shape[0]
            h = jnp.zeros((N, H), x.dtype)
            for e in range(E):
                m = (se == e)[:, None]
                h = h + jnp.where(m, jax.nn.gelu(xd @ w_in[e] + b_in[e]), 0.0)
            y = jnp.zeros((N, Dm), x.dtype)
            for e in range(E):
                m = (se == e)[:, None]
                y = y + jnp.where(m, h @ w_out[e] + b_out[e], 0.0)
            y = y * sp[:, None]
            out = jnp.zeros((T, Dm), x.dtype).at[st].add(y)
            return out.reshape(B, S, Dm)
        return _moe(input_batch, router_w, w_in, b_in, w_out, b_out)
    x = x + jnp.tanh(g_xattn[0]) * _L0_xattn_ref(_layernorm(x, axis=-1), ctx_1024, ctx_1024)
    x = x + jnp.tanh(g_ffn[0]) * _L0_ffn_ref(_layernorm(x, axis=-1), L0_ffn_W, L0_ffn_Wp, L0_ffn_bp, L0_ffn_sim, L0_ffn_temp, L0_ffn_Wd0, L0_ffn_Wu0, L0_ffn_Wd1, L0_ffn_Wu1, L0_ffn_Wd2, L0_ffn_Wu2, L0_ffn_Wd3, L0_ffn_Wu3)
    x = x + jnp.tanh(g_xattn[1]) * _L1_xattn_ref(_layernorm(x, axis=-1), ctx_1024, ctx_1024, mask_BxS2_ik0, L1_xattn_Wq, L1_xattn_Wk, L1_xattn_Wv, L1_xattn_Wo)
    x = x + jnp.tanh(g_ffn[1]) * _L1_ffn_ref(_layernorm(x, axis=-1), L1_ffn_router_w, L1_ffn_w_in, L1_ffn_b_in, L1_ffn_w_out, L1_ffn_b_out)
    return x

_drawn_inputs = setup_inputs


def setup_inputs(seed=0):
    import zlib

    import numpy as np

    out = dict(_drawn_inputs(seed))
    spreads = {'g_ffn': (-1.0, 0.6),
     'L0_ffn_bp': (0.0, 0.8),
     'L1_ffn_b_in': (0.0, 0.8),
     'L1_ffn_b_out': (0.0, 0.8)}
    factors = {'L0_ffn_Wp': 8.0,
     'L0_ffn_sim': 8.0,
     'L0_ffn_Wd0': 8.0,
     'L0_ffn_Wu0': 8.0,
     'L0_ffn_Wd1': 8.0,
     'L0_ffn_Wu1': 8.0,
     'L0_ffn_Wd2': 8.0,
     'L0_ffn_Wu2': 8.0,
     'L0_ffn_Wd3': 8.0,
     'L0_ffn_Wu3': 8.0,
     'L1_ffn_router_w': 2.701,
     'L1_ffn_w_in': 2.705}
    for name, (base, spread) in spreads.items():
        noise = np.random.default_rng([zlib.crc32(name.encode()), seed]).standard_normal(out[name].shape)
        drawn = base * np.exp(spread * noise) if base else spread * noise
        out[name] = jnp.asarray(drawn.astype(out[name].dtype))
    for name, factor in factors.items():
        out[name] = (out[name] * factor).astype(out[name].dtype)
    return out
```

```python
from contextlib import ExitStack

import concourse.bass as bass
from concourse import mybir

F32 = mybir.dt.float32
F16 = mybir.dt.float16
U32 = mybir.dt.uint32
I32 = mybir.dt.int32
ALU = mybir.AluOpType
ACT = mybir.ActivationFunctionType
AX = mybir.AxisListType.X

BATCH, S, D = 32, 128, 256
KT = D // 128
NP = BATCH // 2
HEADS, HD = 16, 16
PROJ = 64
RANKS = (1, 2, 4, 8)
NA = len(RANKS)
RSUM = sum(RANKS)
SMALL = PROJ + RSUM + NA
NE = 8
PROBS = 2
GROUP = 4
NG = BATCH // GROUP
LN_EPS = 1e-5
CLAMP_MAX = 4.605170185988092

C_BASE, C_K, C_V, C_Q, C_SMALL = 0, 256, 512, 768, 1024
C_ROUTER = C_SMALL + SMALL
WCOLS = C_ROUTER + NE

LAG = {"A": 0, "B": 1, "C": 2, "D": 3, "E": 4}
LAST_LAG = 4
BODIES = NP + LAST_LAG
LOOP_FROM, LOOP_TO = LAST_LAG, NP


class Step:

    def __init__(self, n, reg=None):
        self.n, self.reg = n, reg

    def __sub__(self, k):
        return Step(self.n - k, self.reg)

    @property
    def parity(self):
        return self.n % 2

    def times(self, k, plus=0):
        if self.reg is None:
            return self.n * k + plus
        return self.reg * (2 * k) + (self.n * k + plus)

    def done(self, per=1, back=0, short=0):
        return self.times(per, per * (1 - back) - short)

    def dma_done(self, per=16, back=0):
        half = self.n // 2 + 1 - back // 2
        return half * per if self.reg is None else self.reg * per + half * per


class Turns:

    def __init__(self, order):
        self.order = order

    def _before(self, t, name):
        n = 0
        for b in range(t + 1):
            for k, stage in self.order:
                if b == t and k == name:
                    return n
                n += 0 <= b - LAG[stage] < NP
        raise ValueError(name)

    def count(self, body, name, plus=0):
        if body.reg is None:
            return self._before(body.n, name) + plus
        k = len(self.order)
        at = self._before(LOOP_FROM, name)
        return body.times(k, at - k * LOOP_FROM + plus)


T_TURNS = Turns([("ctx", "C"), ("xb", "B"), ("xc", "C"), ("xe", "E")])
G_TURNS = Turns([("small", "B"), ("down", "B"), ("logits", "E")])


def need(eng, sem, count):
    if not isinstance(count, int) or count > 0:
        eng.wait_ge(sem, count)


def need_apart(eng, sem, count, passed):
    if isinstance(count, int):
        need(eng, sem, count)
    else:
        count = eng.to_reg(count)
        eng.wait_ge(passed, 1)
        eng.wait_ge(sem, count)


def run_bodies(eng, body):
    def active(t):
        return {s for s, lag in LAG.items() if 0 <= t - lag < NP}

    for t in range(LOOP_FROM):
        body(Step(t), active(t))
    with eng.Fori(LOOP_FROM // 2, LOOP_TO // 2) as u:
        for half in range(2):
            body(Step(half, u), set(LAG))
    for t in range(LOOP_TO, BODIES):
        body(Step(t), active(t))


def build(nc, x, ctx, mask, gates_in, temp, bp, sim, wall, wp, wu, wo, w_in, b_in, w_out, b_out, decay, eye, out):
    st = ExitStack()
    with st:
        def sb(name, shape, dt=F32):
            return st.enter_context(nc.sbuf_tensor(name, shape, dt))

        def bank(name, dt=F32):
            return st.enter_context(nc.psum_tensor(name, [128, 512], dt))

        def sem(name):
            return st.enter_context(nc.semaphore(name))

        ident = sb("ident", [128, 128])
        ident16 = sb("ident16", [128, 128], F16)
        decay_t = sb("decay_t", [128, 128])
        w_hi = sb("w_hi", [128, KT, WCOLS], F16)
        w_lo = sb("w_lo", [128, KT, WCOLS], F16)
        wo_t = sb("wo_t", [128, KT, D])
        wu_f32 = sb("wu_f32", [128, D])
        wu_parts = sb("wu_parts", [128, D], F16)
        small_bias = sb("small_bias", [128, SMALL])
        gates_raw = sb("gates_raw", [128, 4])
        tanh_g = sb("tanh_g", [128, 4])
        mask_i = sb("mask_i", [128, BATCH], I32)
        keep_all = sb("keep_all", [128, BATCH])
        minus_half = sb("minus_half", [128, 8])
        adapter_id = sb("adapter_id", [128, 2, RSUM])
        adapter_wt = sb("adapter_wt", [128, 2, NA])
        expert_id = sb("expert_id", [128, 2, NE])
        wp_t = sb("wp_t", [PROJ, D])
        sim_t = sb("sim_t", [PROJ, NA])
        sim_sq = sb("sim_sq", [PROJ, NA])
        sim_inv = sb("sim_inv", [PROJ, NA])
        sim_n = sb("sim_n", [PROJ, NA])
        temp_t = sb("temp_t", [PROJ, 1])
        temp_e = sb("temp_e", [PROJ, 1])
        bp_col = sb("bp_col", [PROJ, 1])
        bp_wide = sb("bp_wide", [PROJ, 128])
        ones = sb("ones", [PROJ, 128])

        xs = sb("xs", [128, BATCH, D])
        xe_hi = sb("xe_hi", [128, KT, BATCH * S], F16)
        xe_lo = sb("xe_lo", [128, KT, BATCH * S], F16)
        w_f32 = xe_hi[:, :, :].rearrange("p k s -> p (k s)").bitcast(F32)[:, 0:KT * WCOLS]\
            .rearrange("p (k c) -> p k c", k=KT)
        gate_all = sb("gate_all", [128, BATCH, NE])

        def two(name, shape, dt=F32):
            return [sb(f"{name}{i}", shape, dt) for i in range(2)]

        win_hi = sb("win_hi", [128, NE, KT, D], F16)
        win_lo = sb("win_lo", [128, NE, KT, D], F16)
        wout_hi = sb("wout_hi", [128, NE, KT, D], F16)
        wout_lo = sb("wout_lo", [128, NE, KT, D], F16)
        w_stage = two("w_stage", [128, KT, D])
        bin_t = sb("bin_t", [128, NE, KT])

        outer, pairs = sb, ExitStack()

        def sb(name, shape, dt=F32):
            return pairs.enter_context(nc.sbuf_tensor(name, shape, dt))

        def two(name, shape, dt=F32):
            return [pairs.enter_context(nc.sbuf_tensor(f"{name}{i}", shape, dt)) for i in range(2)]

        x_in = two("x_in", [128, 2, D])
        c_in = two("c_in", [128, 2, D])
        c_again = two("c_again", [128, 2, D])
        kv = two("kv", [128, 2, D])
        x1 = two("x1", [128, 2, D])
        moved = sb("moved", [128, 2, D])
        ln_gain = sb("ln_gain", [128, 2])
        LN = "ABCE"
        stats = {k: sb(f"stats_{k}", [128, 2, 6]) for k in LN}
        mv = {k: two(f"mv_{k}", [128, 2, 2]) for k in LN}
        var = {k: two(f"var_{k}", [128, 2]) for k in LN}
        rstd = {k: two(f"rstd_{k}", [128, 2]) for k in LN}
        shift = {k: two(f"shift_{k}", [128, 2]) for k in LN}
        xn = {k: sb(f"xn_{k}", [128, 2, D]) for k in "BCE"}
        xt_hi = {k: sb(f"xt_hi_{k}", [128, KT, 256], F16) for k in "BC"}
        xt_lo = {k: sb(f"xt_lo_{k}", [128, KT, 256], F16) for k in "BC"}
        ct_hi = sb("ct_hi", [128, KT, 256], F16)
        ct_lo = sb("ct_lo", [128, KT, 256], F16)
        small = sb("small", [128, 2, SMALL])
        square = sb("square", [128, 2, PROJ])
        norm2 = sb("norm2", [128, 2])
        norm2c = sb("norm2c", [128, 2])
        inv_norm = sb("inv_norm", [128, 2])
        lg = sb("lg", [128, 2, NA])
        lmax = sb("lmax", [128, 2])
        ldiff = sb("ldiff", [128, 2, NA])
        lsig = sb("lsig", [128, 2, NA])
        lsig_n = sb("lsig_n", [128, 2, NA])
        lrec = sb("lrec", [128, 2, NA])
        lexp = sb("lexp", [128, 2, NA])
        lsum = sb("lsum", [128, 2])
        ltop = sb("ltop", [128, 2])
        lcode = sb("lcode", [128, 2, NA])
        lwin = sb("lwin", [128, 2])
        picked = sb("picked", [128, 2, RSUM])
        down = sb("down", [128, 2, RSUM])
        down_g = sb("down_g", [128, 2, RSUM])
        down_parts = sb("down_parts", [128, 2, 128], F16)
        down_t = sb("down_t", [128, 2, 128], F16)
        keep = two("keep", [128, 2])
        parts = two("parts", [128, len(KINDS), KT, 256], F16)
        k_stack = two("k_stack", [128, 4, KT, 256], F16)
        q_stack = two("q_stack", [128, 2, 4, KT, 256], F16)
        v_wide = two("v_wide", [128, 2, 8, 4, HD])
        prob = [sb(f"prob{i}", [128, 4, 2, 128]) for i in range(PROBS)]
        av = sb("av", [128, KT, 2, 128])
        rl = sb("rl", [128, 2, NE])
        rmax = sb("rmax", [128, 2, 8])
        rindex = sb("rindex", [128, 2, 8], U32)
        rindex_f = sb("rindex_f", [128, 2, 8])
        rdiff = sb("rdiff", [128, 2, NE])
        rsig = sb("rsig", [128, 2, NE])
        rsig_n = sb("rsig_n", [128, 2, NE])
        rrec = sb("rrec", [128, 2, NE])
        rexp = sb("rexp", [128, 2, NE])
        rsum = sb("rsum", [128, 2])
        rinv = sb("rinv", [128, 2])
        first = sb("first", [128, 2, NE])
        second = sb("second", [128, 2, NE])
        both = sb("both", [128, 2, NE])
        both_e = sb("both_e", [128, 2, NE])

        pairs.close()

        def two(name, shape, dt=F32):
            return [outer(f"{name}{i}", shape, dt) for i in range(2)]

        bout_t = outer("bout_t", [128, NE, D])
        h_f32 = two("h_f32", [128, KT, 512])
        h_hi = two("h_hi", [128, KT, 512], F16)
        h_lo = two("h_lo", [128, KT, 512], F16)
        y_b = two("y_b", [128, GROUP, D])
        acc = two("acc", [128, GROUP, D])
        gate_g = two("gate_g", [128, GROUP, NE])

        names = ["R", "T", "J", "F", "G", "S0", "S1", "O"]
        P = {n: bank(f"ps_{n}") for n in names}
        bank_r = P["R"][:, :].rearrange("p (b d) -> p b d", b=2)
        bank_t = P["T"][:, :].rearrange("p (k b s) -> p k b s", k=KT, b=2)
        bank_j = P["J"][:, :].rearrange("p (k c) -> p k c", k=2)
        bank_f = P["F"][:, :].rearrange("p (b d) -> p b d", b=2)
        bank_g = P["G"]
        g_small = bank_g[:, 0:2 * SMALL].rearrange("p (b c) -> p b c", b=2)
        g_down = bank_g[:, 0:128].bitcast(F16).rearrange("p (b s) -> p b s", b=2)
        g_logits = bank_g[:, 0:2 * NE].rearrange("p (b e) -> p b e", b=2)
        bank_s = [P[f"S{i}"][:, :].rearrange("p (n h s) -> p n h s", n=2, h=2) for i in range(2)]
        bank_av = P["O"][:, :].rearrange("p (k b s) -> p k b s", k=KT, b=2)
        bank_o = P["O"][:, :].rearrange("p (b d) -> p b d", b=2)

        hid_banks = [[P["R"], P["T"]], [P["J"], P["F"]]]
        y_banks = [[P["G"], P["S0"]], [P["S1"], P["O"]]]

        s_const = sem("constants_loaded")
        s_wall = sem("weights_loaded")
        s_wup = sem("adapter_ups_loaded")
        s_zero = sem("zeroed")
        s_iota = sem("iotas_made")
        s_set = sem("setup_vector_steps")
        s_set_p = sem("setup_pool_steps")
        s_set_t = sem("setup_products")
        s_set_a = sem("setup_scalar_steps")
        s_whi = sem("weights_hi_made")
        s_wlo = sem("weights_lo_made")
        s_x = [sem(f"x_loaded{i}") for i in range(2)]
        s_c = [sem(f"ctx_loaded{i}") for i in range(2)]
        s_c2 = [sem(f"ctx_again_loaded{i}") for i in range(2)]
        s_stats = {k: sem(f"stats_{k}_made") for k in LN}
        s_aggr = {k: sem(f"mean_{k}_made") for k in LN}
        s_var = {k: sem(f"variance_{k}_made") for k in LN}
        s_rstd = {k: sem(f"rstd_{k}_made") for k in LN}
        s_shift = {k: sem(f"shift_{k}_made") for k in LN}
        s_xn = {k: sem(f"normed_{k}") for k in "BCE"}
        s_kv = sem("ctx_squared")
        s_scan = sem("running_sum_made")
        s_moved = sem("sum_weighted")
        s_x1 = sem("x1_made")
        s_t = sem("transposed")
        s_t_hi = sem("transposed_hi_copied")
        s_t_lo = sem("transposed_lo_copied")
        s_f = sem("base_product_made")
        s_g = sem("g_bank_written")
        s_g_free = sem("g_bank_read")
        s_square = sem("projection_squared")
        s_norm = sem("norm_clamped")
        s_inv = sem("inverse_norm_made")
        s_b = sem("adapter_gate_steps")
        s_lsig = sem("adapter_sigmoids_made")
        s_down = sem("gated_downs_split")
        s_up = sem("ups_added")
        s_x2 = sem("x2_made")
        s_keep = sem("keep_copied")
        s_k = sem("keys_made")
        s_k_hi = sem("keys_hi_copied")
        s_k_lo = sem("keys_lo_copied")
        s_v = sem("values_made")
        s_v_wide = sem("values_masked")
        s_q = sem("queries_made")
        s_q_hi = sem("queries_hi_copied")
        s_q_lo = sem("queries_lo_copied")
        s_scratch = [sem(f"parts_stored{i}") for i in range(2)]
        s_stacked = [sem(f"stacked{i}") for i in range(2)]
        s_score = sem("scores_made")
        s_prob = sem("probabilities_made")
        s_pv = sem("values_weighted")
        s_av = sem("attended_copied")
        s_o = sem("attention_projected")
        s_x3 = sem("x3_made")
        s_e = sem("router_steps")
        s_rsig = sem("router_sigmoids_made")
        s_gate = sem("gates_made")
        s_ew = [sem(f"expert_weights_loaded{i}") for i in range(2)]
        s_eb = sem("expert_biases_loaded")
        s_ew_hi = sem("expert_weights_hi_made")
        s_ew_lo = sem("expert_weights_lo_made")
        s_h = sem("hidden_product_made")
        s_gelu = sem("gelu_made")
        s_h_hi = sem("hidden_hi_made")
        s_h_lo = sem("hidden_lo_made")
        s_y = sem("expert_output_made")
        s_y_b = sem("expert_output_copied")
        s_acc = sem("expert_output_added")
        s_gate_g = sem("group_gates_copied")
        s_fin = sem("output_made")
        s_out = [sem(f"output_stored{i}") for i in range(2)]

        STACK_DMAS = 4 + 8
        N_CONST = 10

        scratch = [nc.dram_tensor(f"parts_scratch{i}", (len(KINDS), 128, KT * 256), F16, kind="Internal").ap()
                   for i in range(2)]

        block = st.enter_context(nc.Block())

        @block.sync
        def _(sp):
            def pair_rows(t, pair):
                at = pair.times(2)
                return t[at:at + 2] if isinstance(at, int) else t[bass.ds(at, 2)]

            def load_a(p):
                q = p.parity
                need_apart(sp, s_x1, p.done(2, back=2), s_zero)
                sp.dma_start(x_in[q][:, :, :], pair_rows(x, p).rearrange("b s d -> s b d")).then_inc(s_x[q], 16)
                need_apart(sp, s_kv, p.done(back=2), s_zero)
                sp.dma_start(c_in[q][:, :, :], pair_rows(ctx, p).rearrange("b s d -> s b d")).then_inc(s_c[q], 16)

            def load_c(p, body):
                q = p.parity
                need_apart(sp, s_k, p.done(back=2), s_zero)
                sp.dma_start(c_again[q][:, :, :],
                             pair_rows(ctx, p).rearrange("b s d -> s b d")).then_inc(s_c2[q], 16)

            def stack(p):
                q = p.parity
                need_apart(sp, s_stacked[q], p.dma_done(16 * STACK_DMAS, back=2), s_zero)
                sp.wait_ge(s_k_hi, p.done())
                sp.wait_ge(s_k_lo, p.done())
                sp.wait_ge(s_q_hi, p.done())
                sp.wait_ge(s_q_lo, p.done())
                sp.dma_start(scratch[q].rearrange("n p c -> p n c"),
                             parts[q][:, :, :, :].rearrange("p n k c -> p n (k c)")).then_inc(s_scratch[q], 16)
                need_apart(sp, s_score, p.done(4, back=2), s_zero)
                sp.wait_ge(s_scratch[q], p.dma_done())
                for c in range(4):
                    sp.dma_start(k_stack[q][32 * c:32 * c + 32, :, :, :].rearrange("r g k c -> r g (k c)"),
                                 scratch[q][c % 2].rearrange("(g r) c -> r g c", g=4)).then_inc(s_stacked[q], 16)
                    for h in range(2):
                        at = 32 * c + HD * h
                        sp.dma_start(q_stack[q][at:at + HD, h, :, :, :].rearrange("r g k c -> r g (k c)"),
                                     scratch[q][2 + c // 2].rearrange("(g h r) c -> h r g c", g=4, h=2)[h])\
                            .then_inc(s_stacked[q], 16)

            load_a(Step(0))
            for dst, src in ((ident, eye), (decay_t, decay), (wo_t, wo), (gates_raw, gates_in.partition_broadcast(128)),
                             (mask_i, mask), (wp_t, wp), (sim_t, sim), (temp_t, temp.partition_broadcast(PROJ)),
                             (bp_col, bp.rearrange("(p a) -> p a", a=1))):
                sp.dma_start(dst[tuple(slice(None) for _ in dst.shape)], src).then_inc(s_const, 16)
            sp.wait_ge(s_zero, 2)
            sp.dma_start(small_bias[:, 0:PROJ], bp.partition_broadcast(128)).then_inc(s_const, 16)
            for i in range(3):
                sp.dma_start(wu_f32[32 * i:32 * i + RSUM, :], wu).then_inc(s_wup, 16)
            sp.dma_start(w_f32[:, :, :], wall.rearrange("(k p) c -> p k c", p=128)).then_inc(s_wall, 16)

            def body(t, on):
                if "C" in on or t.n + 1 == LAG["C"]:
                    pass
                nxt = t - (-1)
                if nxt.reg is not None or nxt.n < NP:
                    load_a(nxt)
                c_next = nxt - LAG["C"]
                if c_next.reg is not None or 0 <= c_next.n < NP:
                    load_c(c_next, t)
                if "C" in on:
                    stack(t - LAG["C"])

            for t in range(LOOP_FROM):
                body(Step(t), {s for s, lag in LAG.items() if 0 <= t - lag < NP})
            with sp.Fori(LOOP_FROM // 2, LOOP_TO // 2 - 1) as u:
                for half in range(2):
                    body(Step(half, u), set(LAG))
            for t in range(LOOP_TO - 2, BODIES):
                body(Step(t), {s for s, lag in LAG.items() if 0 <= t - lag < NP})

            sp.dma_start(bin_t[:, :, :], b_in).then_inc(s_eb, 16)
            for n in range(2 * NE):
                src = (w_in, w_out)[n % 2]
                if n >= 2:
                    sp.wait_ge(s_ew_hi, n - 1)
                    sp.wait_ge(s_ew_lo, n - 1)
                sp.dma_start(w_stage[n % 2][:, :, :], src[n // 2].rearrange("(k p) c -> p k c", p=128))\
                    .then_inc(s_ew[n % 2], 16)
            sp.wait_ge(s_gate, NP)
            sp.dma_start(bout_t[:, :, :], b_out.partition_broadcast(128)).then_inc(s_eb, 16)
            with sp.Fori(0, NG // 2) as u:
                for half in range(2):
                    g = Step(half, u)
                    need_apart(sp, s_fin, g.done(), s_zero)
                    sp.dma_start(out[bass.ds(g.times(GROUP), GROUP)].rearrange("b s d -> s b d"),
                                 acc[half][:, :, :]).then_inc(s_out[half], 16)
            for i in range(2):
                sp.wait_ge(s_out[i], 16 * NG // 2)

        @block.gpsimd
        def _(pool):
            pool.memset(minus_half[:, :], -0.5).then_inc(s_set_p, 1)
            at = 0
            for a, r in enumerate(RANKS):
                pool.memset(adapter_id[:, :, at:at + r], float(NA - a)).then_inc(s_iota, 1)
                pool.memset(adapter_wt[:, :, a:a + 1], float(NA - a)).then_inc(s_iota, 1)
                at += r
            for e in range(NE):
                pool.memset(expert_id[:, :, e:e + 1], float(e)).then_inc(s_iota, 1)
            for q in range(2):
                pool.memset(q_stack[q][:, :, :, :, :], 0.0).then_inc(s_iota, 1)
                pool.memset(v_wide[q][:, :, :, :, :], 0.0).then_inc(s_iota, 1)
            pool.wait_ge(s_set_p, 1)
            pool.wait_ge(s_set, 2)
            pool.tensor_tensor(sim_inv[:, :], sim_sq[:, :], minus_half[0:PROJ, 0:NA], ALU.pow).then_inc(s_set_p, 1)

            def inverse_root(k, p):
                q = p.parity
                pool.wait_ge(s_var[k], p.done())
                pool.tensor_tensor(rstd[k][q][:, :], var[k][q][:, :], minus_half[:, 0:2], ALU.pow)\
                    .then_inc(s_rstd[k], 1)

            def body(t, on):
                if "B" in on:
                    inverse_root("B", t - LAG["B"])
                if "C" in on:
                    inverse_root("C", t - LAG["C"])
                if "A" in on:
                    p = t - LAG["A"]
                    q = p.parity
                    pool.wait_ge(s_c[q], p.dma_done())
                    need(pool, s_scan, p.done(back=2))
                    pool.tensor_tensor(kv[q][:, :, :], c_in[q][:, :, :], c_in[q][:, :, :], ALU.mult)\
                        .then_inc(s_kv, 1)
                if "E" in on:
                    inverse_root("E", t - LAG["E"])
                if "A" in on:
                    inverse_root("A", t - LAG["A"])
                if "B" in on:
                    p = t - LAG["B"]
                    pool.wait_ge(s_norm, p.done())
                    pool.tensor_tensor(inv_norm[:, :], norm2c[:, :], minus_half[:, 0:2], ALU.pow).then_inc(s_inv, 1)

            run_bodies(pool, body)

        @block.scalar
        def _(act):
            act.wait_ge(s_const, 16 * N_CONST)
            act.wait_ge(s_set, 3)
            act.activation(temp_e[:, :], temp_e[:, :], ACT.Exp).then_inc(s_set_a, 1)
            act.activation(tanh_g[:, :], gates_raw[:, :], ACT.Tanh).then_inc(s_set_a, 1)
            act.activation(ident16[:, :], ident[:, :], ACT.Copy).then_inc(s_set_a, 1)
            act.wait_ge(s_set, 6)
            act.activation(w_hi[:, :, :], w_f32[:, :, :], ACT.Copy).then_inc(s_whi, 1)
            act.wait_ge(s_wup, 48)
            act.wait_ge(s_zero, 2)
            act.activation(wu_parts[:, :], wu_f32[:, :], ACT.Copy).then_inc(s_whi, 1)

            def hi(t, name, dst):
                act.wait_ge(s_t, T_TURNS.count(t, name, 1))
                act.activation(dst, bank_t, ACT.Copy).then_inc(s_t_hi, 1)

            def normed(k, p, t, src):
                q = p.parity
                act.wait_ge(s_shift[k], p.done())
                name = {"B": "xb", "C": "xc", "E": "xe"}[k]
                need(act, s_t, T_TURNS.count(t - 1, name, 1) if t.reg is not None or t.n > LAG[k] else 0)
                for b in range(2):
                    act.activation(xn[k][:, b, :], src(b), ACT.Identity, bias=shift[k][q][:, b:b + 1],
                                   scale=rstd[k][q][:, b:b + 1]).then_inc(s_xn[k], 1)

            def stored(p):
                def at(b):
                    i = p.times(2, b)
                    return xs[:, i, :] if isinstance(i, int) else xs[:, bass.ds(i, 1), :]
                return at

            def sigmoids(p, m):
                act.wait_ge(s_score, p.times(4, m + 1))
                need(act, s_pv, p.times(4, m + 1 - PROBS))
                for n in range(2):
                    ins = act.activation(prob[m % PROBS][:, 2 * n:2 * n + 2, :, :], bank_s[n], ACT.Sigmoid,
                                         scale=float(HD) ** -0.5)
                ins.then_inc(s_prob, 1)

            def part_hi(dst, ready, p, made):
                q = p.parity
                act.wait_ge(ready, p.done())
                need(act, s_scratch[q], p.dma_done(back=2))
                act.activation(parts[q][:, dst, :, :], bank_j, ACT.Copy).then_inc(made, 1)

            def body(t, on):
                P_ = {s: t - lag for s, lag in LAG.items()}
                if "C" in on:
                    hi(t, "ctx", ct_hi[:, :, :].rearrange("p k (b s) -> p k b s", b=2))
                if "B" in on:
                    normed("B", P_["B"], t, lambda b: x1[P_["B"].parity][:, b, :])
                if "D" in on:
                    sigmoids(P_["D"], 0)
                if "C" in on:
                    part_hi(0, s_k, P_["C"], s_k_hi)
                    normed("C", P_["C"], t, stored(P_["C"]))
                if "D" in on:
                    sigmoids(P_["D"], 1)
                if "B" in on:
                    hi(t, "xb", xt_hi["B"][:, :, :].rearrange("p k (b s) -> p k b s", b=2))
                if "C" in on:
                    p = P_["C"]
                    q = p.parity
                    act.wait_ge(s_v, p.done())
                    act.wait_ge(s_keep, p.done())
                    need(act, s_pv, p.done(4, back=2))
                    if t.reg is None:
                        act.wait_ge(s_iota, 2 * NA + NE + 4)
                    for b in range(2):
                        act.activation(v_wide[q][:, b, :, 0:4:3, :],
                                       bank_j[:, b, :].rearrange("p (n h d) -> p n h d", n=8, h=2),
                                       ACT.Copy, scale=keep[q][:, b:b + 1]).then_inc(s_v_wide, 1)
                if "D" in on:
                    sigmoids(P_["D"], 2)
                if "E" in on:
                    normed("E", P_["E"], t, stored(P_["E"]))
                if "C" in on:
                    hi(t, "xc", xt_hi["C"][:, :, :].rearrange("p k (b s) -> p k b s", b=2))
                if "D" in on:
                    sigmoids(P_["D"], 3)
                if "C" in on:
                    part_hi(2, s_q, P_["C"], s_q_hi)
                if "E" in on:
                    at = P_["E"].times(256)
                    dst = xe_hi[:, :, at:at + 256] if isinstance(at, int) else xe_hi[:, :, bass.ds(at, 256)]
                    hi(t, "xe", dst.rearrange("p k (b s) -> p k b s", b=2))
                if "D" in on:
                    p = P_["D"]
                    act.wait_ge(s_pv, p.done(4))
                    need(act, s_o, p.done(back=1))
                    act.activation(av[:, :, :, :], bank_av, ACT.Copy).then_inc(s_av, 1)
                if "B" in on:
                    p = P_["B"]
                    act.wait_ge(s_b, p.times(B_STEPS, B_DIFF))
                    act.activation(lsig[:, :, :], ldiff[:, :, :], ACT.Sigmoid).then_inc(s_lsig, 1)
                    act.activation(lsig_n[:, :, :], ldiff[:, :, :], ACT.Sigmoid, scale=-1.0).then_inc(s_lsig, 1)
                    act.wait_ge(s_g, G_TURNS.count(t, "down", 1))
                    act.activation(down_t[:, :, :], g_down, ACT.Copy).then_inc(s_g_free, 1)
                if "E" in on:
                    p = P_["E"]
                    act.wait_ge(s_e, p.times(E_STEPS, E_DIFF))
                    act.activation(rsig[:, :, :], rdiff[:, :, :], ACT.Sigmoid).then_inc(s_rsig, 1)
                    act.activation(rsig_n[:, :, :], rdiff[:, :, :], ACT.Sigmoid, scale=-1.0).then_inc(s_rsig, 1)

            run_bodies(act, body)

            for n in range(2 * NE):
                act.wait_ge(s_ew[n % 2], 16 * (n // 2 + 1))
                act.activation((win_hi, wout_hi)[n % 2][:, n // 2, :, :], w_stage[n % 2][:, :, :], ACT.Copy)\
                    .then_inc(s_ew_hi, 1)
            act.wait_ge(s_eb, 32)

            def hidden(k, first_group):
                q = k.parity
                if not (first_group and k.n < 2):
                    act.wait_ge(s_h_lo, k.done(back=2))
                for m in range(KT):
                    act.wait_ge(s_h, k.times(KT, m + 1))
                    act.activation(h_f32[q][:, m, :], hid_banks[q][m][:, :], ACT.Gelu_apprx_tanh,
                                   bias=bin_t[:, k.n % NE, m:m + 1]).then_inc(s_gelu, 1)

            experts_loop(act, hidden)


        @block.tensor
        def _(pe):
            def split_mm(o, lhs, rhs, start=True, stop=True, skip=False):
                terms = [(l, r) for l, r in zip(lhs, rhs)]
                seq = []
                for (lh, ll), (rh, rl_) in terms:
                    seq += [(lh, rh), (lh, rl_), (ll, rh)]
                for i, (l, r) in enumerate(seq):
                    ins = pe.matmul(o, l, r, start=start and i == 0, stop=stop and i == len(seq) - 1,
                                    skip_group_check=skip)
                return ins

            pe.wait_ge(s_const, 16 * N_CONST)
            pe.wait_ge(s_set, 1)
            pe.matmul(P["O"][0:PROJ, 0:NA], ones[:, 0:PROJ], sim_sq[:, :], start=True, stop=True).then_inc(s_set_t, 1)
            pe.wait_ge(s_set, 5)
            for k in range(KT):
                pe.matmul(P["O"][:, 8 * k:8 * k + NA], wp_t[:, 128 * k:128 * k + 128], sim_n[:, :],
                          start=True, stop=True)
            pe.matmul(P["O"][:, 16:16 + NA], bp_wide[:, :], sim_n[:, :], start=True, stop=True).then_inc(s_set_t, 1)
            pe.wait_ge(s_set_a, 3)
            pe.wait_ge(s_whi, 2)
            pe.wait_ge(s_wlo, 2)

            def transposes(t, name, src):
                n = T_TURNS.count(t, name)
                need(pe, s_t_hi, n)
                need(pe, s_t_lo, n)
                for k in range(KT):
                    for b in range(2):
                        ins = pe.transpose(bank_t[:, k, b, :], src[:, b, 128 * k:128 * k + 128], ident[:, :])
                ins.then_inc(s_t, 1)

            def wcols(k, c, n):
                return w_hi[:, k, c:c + n], w_lo[:, k, c:c + n]

            def feature_major(t, name, c, xh, xl):
                for m in range(2):
                    ins = split_mm(bank_j[:, m, :], [wcols(k, c + 128 * m, 128) for k in range(KT)],
                                   [(xh[:, k, :], xl[:, k, :]) for k in range(KT)])
                return ins

            def scores(p, m):
                q, b, k = p.parity, m // 2, m % 2
                cut = slice(128 * b, 128 * b + 128)
                need(pe, s_prob, p.times(4, m))
                for g in range(4):
                    ins = pe.matmul(bank_s[g // 2][:, g % 2, :, :], k_stack[q][:, g, k, cut],
                                    q_stack[q][:, :, g, k, cut], start=True, stop=True)
                ins.then_inc(s_score, 1)

            def weigh(p, m):
                q, b, k = p.parity, m // 2, m % 2
                pe.wait_ge(s_prob, p.times(4, m + 1))
                for h in range(2):
                    for g in range(4):
                        ins = pe.matmul(bank_av[32 * g:32 * g + 32, k, b, :],
                                        v_wide[q][:, b, 4 * k + g, 2 * h:2 * h + 2, :].rearrange("p a d -> p (a d)"),
                                        prob[m % PROBS][:, g, h, :], start=(h == 0), stop=(h == 1))
                ins.then_inc(s_pv, 1)

            def body(t, on):
                P_ = {s: t - lag for s, lag in LAG.items()}
                c, d = P_["C"], P_["D"]
                if "C" in on:
                    pe.wait_ge(s_c2[c.parity], c.dma_done())
                    transposes(t, "ctx", c_again[c.parity])
                if "D" in on:
                    pe.wait_ge(s_stacked[d.parity], d.dma_done(16 * STACK_DMAS))
                    pe.wait_ge(s_v_wide, d.done(2))
                    scores(d, 0)
                if "C" in on:
                    pe.wait_ge(s_t_hi, T_TURNS.count(t, "ctx", 1))
                    pe.wait_ge(s_t_lo, T_TURNS.count(t, "ctx", 1))
                    need(pe, s_q_hi, c.done(back=1))
                    need(pe, s_q_lo, c.done(back=1))
                    feature_major(t, "k", C_K, ct_hi, ct_lo).then_inc(s_k, 1)
                if "D" in on:
                    need(pe, s_x3, d.done(back=1))
                    scores(d, 1)
                    weigh(d, 0)
                if "B" in on:
                    pe.wait_ge(s_xn["B"], P_["B"].done(2))
                    transposes(t, "xb", xn["B"])
                if "C" in on:
                    pe.wait_ge(s_k_hi, c.done())
                    pe.wait_ge(s_k_lo, c.done())
                    for b in range(2):
                        cut = slice(128 * b, 128 * b + 128)
                        ins = split_mm(bank_j[:, b, :], [(ct_hi[:, k, cut], ct_lo[:, k, cut]) for k in range(KT)],
                                       [wcols(k, C_V, D) for k in range(KT)])
                    ins.then_inc(s_v, 1)
                if "D" in on:
                    scores(d, 2)
                    weigh(d, 1)
                if "B" in on:
                    p = P_["B"]
                    pe.wait_ge(s_t_hi, T_TURNS.count(t, "xb", 1))
                    pe.wait_ge(s_t_lo, T_TURNS.count(t, "xb", 1))
                    need(pe, s_x2, p.done(back=1))
                    need(pe, s_g_free, G_TURNS.count(t, "small"))
                    for b in range(2):
                        cut = slice(128 * b, 128 * b + 128)
                        acts = [(xt_hi["B"][:, k, cut], xt_lo["B"][:, k, cut]) for k in range(KT)]
                        small_ins = split_mm(g_small[:, b, :], acts, [wcols(k, C_SMALL, SMALL) for k in range(KT)])
                        base_ins = split_mm(bank_f[:, b, :], acts, [wcols(k, C_BASE, D) for k in range(KT)],
                                            start=(b == 0), stop=False, skip=True)
                    small_ins.then_inc(s_g, 1)
                    base_ins.then_inc(s_f, 1)
                if "C" in on:
                    pe.wait_ge(s_xn["C"], c.done(2))
                    transposes(t, "xc", xn["C"])
                if "D" in on:
                    scores(d, 3)
                    weigh(d, 2)
                if "A" in on:
                    a = P_["A"]
                    pe.wait_ge(s_kv, a.done())
                    need(pe, s_moved, a.done(2, back=1))
                    pe.matmul(P["R"][:, :], decay_t[:, :], kv[a.parity][:, :, :].rearrange("p b d -> p (b d)"),
                              start=True, stop=True).then_inc(s_scan, 1)
                if "C" in on:
                    pe.wait_ge(s_t_hi, T_TURNS.count(t, "xc", 1))
                    pe.wait_ge(s_t_lo, T_TURNS.count(t, "xc", 1))
                    pe.wait_ge(s_v_wide, c.done(2))
                    feature_major(t, "q", C_Q, xt_hi["C"], xt_lo["C"]).then_inc(s_q, 1)
                if "D" in on:
                    weigh(d, 3)
                if "E" in on:
                    pe.wait_ge(s_xn["E"], P_["E"].done(2))
                    transposes(t, "xe", xn["E"])
                if "D" in on:
                    pe.wait_ge(s_av, d.done())
                    for b in range(2):
                        for k in range(KT):
                            ins = pe.matmul(bank_o[:, b, :], av[:, k, b, :], wo_t[:, k, :], start=(k == 0),
                                            stop=(k == KT - 1))
                    ins.then_inc(s_o, 1)
                if "B" in on:
                    p = P_["B"]
                    pe.wait_ge(s_down, p.done())
                    pe.wait_ge(s_g_free, G_TURNS.count(t, "down"))
                    for b in range(2):
                        ins = pe.transpose(g_down[:, b, :], down_parts[:, b, :], ident16[:, :])
                    ins.then_inc(s_g, 1)
                    pe.wait_ge(s_g_free, G_TURNS.count(t, "down", 1))
                    for b in range(2):
                        ins = pe.matmul(bank_f[:, b, :], down_t[:, b, :], wu_parts[:, :], start=False, stop=(b == 1),
                                        skip_group_check=True)
                    ins.then_inc(s_up, 1)
                if "E" in on:
                    e = P_["E"]
                    pe.wait_ge(s_t_hi, T_TURNS.count(t, "xe", 1))
                    pe.wait_ge(s_t_lo, T_TURNS.count(t, "xe", 1))
                    need(pe, s_g_free, G_TURNS.count(t, "logits"))
                    for b in range(2):
                        at = e.times(256, 128 * b)
                        cut = slice(at, at + 128) if isinstance(at, int) else bass.ds(at, 128)
                        acts = [(xe_hi[:, k, cut], xe_lo[:, k, cut]) for k in range(KT)]
                        ins = split_mm(g_logits[:, b, :], acts, [wcols(k, C_ROUTER, NE) for k in range(KT)])
                    ins.then_inc(s_g, 1)

            run_bodies(pe, body)

            pe.wait_ge(s_gate, NP)

            def expert(k, first_group):
                q, e = k.parity, k.n % NE
                if first_group:
                    pe.wait_ge(s_ew_hi, 2 * e + 2)
                    pe.wait_ge(s_ew_lo, 2 * e + 2)

                def layer1():
                    if not (first_group and k.n < 2):
                        pe.wait_ge(s_gelu, k.done(KT, back=2))
                    at = group_of(k).times(512)
                    cut = bass.ds(at, 512) if not isinstance(at, int) else slice(at, at + 512)
                    for m in range(KT):
                        split_mm(hid_banks[q][m][:, :],
                                 [(win_hi[:, e, i, 128 * m:128 * m + 128], win_lo[:, e, i, 128 * m:128 * m + 128])
                                  for i in range(KT)],
                                 [(xe_hi[:, i, cut], xe_lo[:, i, cut]) for i in range(KT)]).then_inc(s_h, 1)

                def layer2():
                    pe.wait_ge(s_h_hi, k.done())
                    pe.wait_ge(s_h_lo, k.done())
                    if not (first_group and k.n < 2):
                        pe.wait_ge(s_y_b, k.done(GROUP, back=2))
                    for b in range(GROUP):
                        cut = slice(128 * b, 128 * b + 128)
                        ins = split_mm(y_banks[q][b // 2][:, 256 * (b % 2):256 * (b % 2) + 256],
                                       [(h_hi[q][:, i, cut], h_lo[q][:, i, cut]) for i in range(KT)],
                                       [(wout_hi[:, e, i, :], wout_lo[:, e, i, :]) for i in range(KT)])
                    ins.then_inc(s_y, 1)
                return layer1, layer2

            def pe_experts():
                one, _ = expert(Count(0), True)
                one()

                def both_layers(k, first_group, last):
                    if not last:
                        expert(k.plus(1), first_group and k.n < NE - 1)[0]()
                    expert(k, first_group)[1]()

                for n in range(NE):
                    both_layers(Count(n), True, False)
                with pe.Fori(1, NG - 1) as g:
                    for n in range(NE):
                        both_layers(Count(n, g), False, False)
                for n in range(NE):
                    both_layers(Count(n + NE * (NG - 1)), False, n == NE - 1)

            pe_experts()

        @block.vector
        def _(dve):
            dve.memset(small_bias[:, :], 0.0).then_inc(s_zero, 1)
            dve.memset(wu_f32[:, :], 0.0).then_inc(s_zero, 1)
            dve.memset(ones[:, :], 1.0)
            dve.memset(down_parts[:, :, :], 0.0).then_inc(s_zero, 1)
            dve.wait_ge(s_const, 16 * N_CONST)
            dve.tensor_tensor(sim_sq[:, :], sim_t[:, :], sim_t[:, :], ALU.mult).then_inc(s_set, 1)
            dve.wait_ge(s_set_t, 1)
            dve.tensor_scalar(sim_sq[:, :], P["O"][0:PROJ, 0:NA], 1e-24, None, ALU.max).then_inc(s_set, 1)
            dve.tensor_scalar(temp_e[:, :], temp_t[:, :], CLAMP_MAX, None, ALU.min).then_inc(s_set, 1)
            dve.tensor_scalar(bp_wide[:, :], ones[:, :], bp_col[:, 0:1], None, ALU.mult).then_inc(s_set, 1)
            dve.wait_ge(s_set_p, 2)
            dve.wait_ge(s_set_a, 1)
            dve.scalar_tensor_tensor(out=sim_n[:, :], in0=sim_t[:, :], scalar=temp_e[:, 0:1], in1=sim_inv[:, :],
                                     op0=ALU.mult, op1=ALU.mult).then_inc(s_set, 1)
            dve.wait_ge(s_set_t, 2)
            dve.wait_ge(s_wall, 16)
            for k in range(KT):
                dve.tensor_copy(w_f32[:, k, C_SMALL + PROJ + RSUM:C_ROUTER], P["O"][:, 8 * k:8 * k + NA])
            dve.tensor_copy(small_bias[:, PROJ + RSUM:SMALL], P["O"][:, 16:16 + NA]).then_inc(s_set, 1)
            dve.tensor_scalar(keep_all[:, :], mask_i[:, :], 0, None, ALU.not_equal).then_inc(s_set, 1)
            dve.wait_ge(s_whi, 2)
            dve.wait_ge(s_set, 7)
            dve.tensor_tensor(w_lo[:, :, :], w_f32[:, :, :], w_hi[:, :, :], ALU.subtract).then_inc(s_wlo, 1)
            dve.tensor_tensor(wu_parts[64:96, :], wu_f32[64:96, :], wu_parts[64:96, :], ALU.subtract).then_inc(s_wlo, 1)
            dve.wait_ge(s_set_a, 2)

            def statistics(k, p, src):
                q = p.parity
                for b in range(2):
                    dve.bn_stats(stats[k][:, b, :], src(b)).then_inc(s_stats[k], 1)
                need_apart(dve, s_stats[k], p.done(2), s_zero)
                for b in range(2):
                    dve.bn_aggr(mv[k][q][:, b, :], stats[k][:, b, :]).then_inc(s_aggr[k], 1)
                dve.wait_ge(s_aggr[k], p.done(2))
                dve.tensor_scalar(var[k][q][:, :], mv[k][q][:, :, 1], LN_EPS, None, ALU.add).then_inc(s_var[k], 1)

            def shifts(k, p):
                q = p.parity
                dve.wait_ge(s_rstd[k], p.done())
                dve.scalar_tensor_tensor(out=shift[k][q][:, :], in0=mv[k][q][:, :, 0], scalar=-1.0,
                                         in1=rstd[k][q][:, :], op0=ALU.mult, op1=ALU.mult).then_inc(s_shift[k], 1)

            def stored(p):
                def at(b):
                    i = p.times(2, b)
                    return xs[:, i, :] if isinstance(i, int) else xs[:, bass.ds(i, 1), :]
                return at

            def pair_of(tile, p):
                at = p.times(2)
                return tile[:, at:at + 2] if isinstance(at, int) else tile[:, bass.ds(at, 2)]

            def lo(t, name, hi_part, dst):
                n = T_TURNS.count(t, name, 1)
                dve.wait_ge(s_t_hi, n)
                dve.tensor_tensor(dst, bank_t, hi_part, ALU.subtract).then_inc(s_t_lo, 1)

            def part_lo(n, made_hi, p, made):
                q = p.parity
                dve.wait_ge(made_hi, p.done())
                dve.tensor_tensor(parts[q][:, n + 1, :, :], bank_j, parts[q][:, n, :, :], ALU.subtract)\
                    .then_inc(made, 1)

            class Chain:
                def __init__(self, s, p, per):
                    self.s, self.p, self.per, self.n = s, p, per, 0

                def link(self, ins):
                    self.n += 1
                    ins.then_inc(self.s, 1)
                    return self.n

                def after(self, n):
                    dve.wait_ge(self.s, self.p.times(self.per, n))

            def adapter_gates_1(t, p):
                ch = Chain(s_b, p, B_STEPS)
                dve.wait_ge(s_g, G_TURNS.count(t, "small", 1))
                n = ch.link(dve.tensor_tensor(small[:, :, :], g_small, small_bias[:, :].unsqueeze(1)
                                              .broadcast_to([128, 2, SMALL]), ALU.add))
                ch.after(n)
                dve.sem_inc(s_g_free, 1)
                for b in range(2):
                    dve.tensor_tensor_reduce(square[:, b, :], small[:, b, 0:PROJ], small[:, b, 0:PROJ], 1.0, 0.0,
                                             ALU.mult, ALU.add, norm2[:, b:b + 1]).then_inc(s_square, 1)
                dve.wait_ge(s_square, p.done(2))
                dve.tensor_scalar(norm2c[:, :], norm2[:, :], 1e-24, None, ALU.max).then_inc(s_norm, 1)

            def adapter_gates_2(t, p):
                ch = Chain(s_b, p, B_STEPS)
                ch.n = 1
                dve.wait_ge(s_inv, p.done())
                n = ch.link(dve.tensor_tensor(lg[:, :, :], small[:, :, PROJ + RSUM:], inv_norm[:, :].unsqueeze(2)
                                              .broadcast_to([128, 2, NA]), ALU.mult))
                ch.after(n)
                n = ch.link(dve.tensor_reduce(lmax[:, :], lg[:, :, :], AX, ALU.max))
                ch.after(n)
                n = ch.link(dve.tensor_tensor(ldiff[:, :, :], lg[:, :, :], lmax[:, :].unsqueeze(2)
                                              .broadcast_to([128, 2, NA]), ALU.subtract))
                assert n == B_DIFF
                ch.after(n)
                n = ch.link(dve.scalar_tensor_tensor(out=lcode[:, :, :], in0=ldiff[:, :, :], scalar=0.0,
                                                     in1=adapter_wt[:, :, :], op0=ALU.is_ge, op1=ALU.mult))
                ch.after(n)
                n = ch.link(dve.tensor_reduce(lwin[:, :], lcode[:, :, :], AX, ALU.max))
                ch.after(n)
                n = ch.link(dve.tensor_tensor(picked[:, :, :], adapter_id[:, :, :], lwin[:, :].unsqueeze(2)
                                              .broadcast_to([128, 2, RSUM]), ALU.is_equal))
                ch.after(n)
                n = ch.link(dve.tensor_tensor(down[:, :, :], picked[:, :, :], small[:, :, PROJ:PROJ + RSUM],
                                              ALU.mult))
                assert n == B_DOWN

            def adapter_gates_3(t, p):
                ch = Chain(s_b, p, B_STEPS)
                ch.n = B_DOWN
                dve.wait_ge(s_lsig, p.done(2))
                n = ch.link(dve.reciprocal(lrec[:, :, :], lsig_n[:, :, :]))
                ch.after(n)
                n = ch.link(dve.tensor_tensor(lexp[:, :, :], lsig[:, :, :], lrec[:, :, :], ALU.mult))
                ch.after(n)
                n = ch.link(dve.tensor_reduce(lsum[:, :], lexp[:, :, :], AX, ALU.add))
                ch.after(n)
                n = ch.link(dve.reciprocal(ltop[:, :], lsum[:, :]))
                ch.after(n)
                n = ch.link(dve.tensor_tensor(down_g[:, :, :], down[:, :, :], ltop[:, :].unsqueeze(2)
                                              .broadcast_to([128, 2, RSUM]), ALU.mult))
                ch.after(n)
                n = ch.link(dve.tensor_copy(down_parts[:, :, 0:RSUM], down_g[:, :, :]))
                ch.after(n)
                n = ch.link(dve.tensor_copy(down_parts[:, :, 64:64 + RSUM], down_parts[:, :, 0:RSUM]))
                dve.tensor_tensor(down_parts[:, :, 32:32 + RSUM], down_g[:, :, :], down_parts[:, :, 0:RSUM],
                                  ALU.subtract).then_inc(s_down, 1)
                assert n == B_STEPS

            def router_1(t, p):
                ch = Chain(s_e, p, E_STEPS)
                dve.wait_ge(s_g, G_TURNS.count(t, "logits", 1))
                n = ch.link(dve.tensor_copy(rl[:, :, :], g_logits))
                ch.after(n)
                dve.sem_inc(s_g_free, 1)
                for b in range(2):
                    n = ch.link(dve.max(rmax[:, b, :], rl[:, b, :]))
                ch.after(n)
                n = ch.link(dve.tensor_tensor(rdiff[:, :, :], rl[:, :, :], rmax[:, :, 0:1]
                                              .broadcast_to([128, 2, NE]), ALU.subtract))
                assert n == E_DIFF
                for b in range(2):
                    n = ch.link(dve.max_index(rindex[:, b, :], rmax[:, b, :], rl[:, b, :]))
                ch.after(n)
                n = ch.link(dve.tensor_copy(rindex_f[:, :, :], rindex[:, :, :]))
                ch.after(n)
                n = ch.link(dve.tensor_tensor(first[:, :, :], expert_id[:, :, :], rindex_f[:, :, 0:1]
                                              .broadcast_to([128, 2, NE]), ALU.is_equal))
                n = ch.link(dve.tensor_tensor(second[:, :, :], expert_id[:, :, :], rindex_f[:, :, 1:2]
                                              .broadcast_to([128, 2, NE]), ALU.is_equal))
                ch.after(n)
                n = ch.link(dve.tensor_tensor(both[:, :, :], first[:, :, :], second[:, :, :], ALU.add))
                assert n == E_BOTH

            def router_2(t, p):
                ch = Chain(s_e, p, E_STEPS)
                ch.n = E_BOTH
                dve.wait_ge(s_rsig, p.done(2))
                n = ch.link(dve.reciprocal(rrec[:, :, :], rsig_n[:, :, :]))
                ch.after(n)
                n = ch.link(dve.tensor_tensor(rexp[:, :, :], rsig[:, :, :], rrec[:, :, :], ALU.mult))
                ch.after(n)
                n = ch.link(dve.tensor_reduce(rsum[:, :], rexp[:, :, :], AX, ALU.add))
                n = ch.link(dve.tensor_tensor(both_e[:, :, :], both[:, :, :], rexp[:, :, :], ALU.mult))
                ch.after(n)
                n = ch.link(dve.reciprocal(rinv[:, :], rsum[:, :]))
                ch.after(n)
                assert n == E_STEPS
                dve.tensor_tensor(pair_of(gate_all, p), both_e[:, :, :], rinv[:, :].unsqueeze(2)
                                  .broadcast_to([128, 2, NE]), ALU.mult).then_inc(s_gate, 1)

            def body(t, on):
                P_ = {s: t - lag for s, lag in LAG.items()}
                a, b_, c, d, e = (P_[k] for k in "ABCDE")
                if "B" in on:
                    need_apart(dve, s_x1, b_.done(2), s_zero)
                    statistics("B", b_, lambda b: x1[b_.parity][:, b, :])
                if "C" in on:
                    need_apart(dve, s_x2, c.done(), s_zero)
                    statistics("C", c, stored(c))
                    dve.tensor_copy(keep[c.parity][:, :], pair_of(keep_all, c)).then_inc(s_keep, 1)
                if "B" in on:
                    shifts("B", b_)
                if "C" in on:
                    lo(t, "ctx", ct_hi[:, :, :].rearrange("p k (b s) -> p k b s", b=2),
                       ct_lo[:, :, :].rearrange("p k (b s) -> p k b s", b=2))
                    shifts("C", c)
                if "A" in on:
                    need_apart(dve, s_x[a.parity], a.dma_done(), s_zero)
                    statistics("A", a, lambda b: x_in[a.parity][:, b, :])
                if "C" in on:
                    part_lo(0, s_k_hi, c, s_k_lo)
                if "E" in on:
                    need_apart(dve, s_x3, e.done(), s_zero)
                    statistics("E", e, stored(e))
                if "B" in on:
                    lo(t, "xb", xt_hi["B"][:, :, :].rearrange("p k (b s) -> p k b s", b=2),
                       xt_lo["B"][:, :, :].rearrange("p k (b s) -> p k b s", b=2))
                if "E" in on:
                    shifts("E", e)
                if "C" in on:
                    lo(t, "xc", xt_hi["C"][:, :, :].rearrange("p k (b s) -> p k b s", b=2),
                       xt_lo["C"][:, :, :].rearrange("p k (b s) -> p k b s", b=2))
                if "B" in on:
                    adapter_gates_1(t, b_)
                if "A" in on:
                    q = a.parity
                    dve.wait_ge(s_rstd["A"], a.done())
                    dve.tensor_scalar(ln_gain[:, :], rstd["A"][q][:, :], tanh_g[:, 0:1], None, ALU.mult)\
                        .then_inc(s_shift["A"], 1)
                    dve.wait_ge(s_scan, a.done())
                    for b in range(2):
                        dve.scalar_tensor_tensor(out=moved[:, b, :], in0=x_in[q][:, b, :],
                                                 scalar=mv["A"][q][:, b, 0:1], in1=bank_r[:, b, :],
                                                 op0=ALU.subtract, op1=ALU.mult).then_inc(s_moved, 1)
                    dve.wait_ge(s_moved, a.done(2))
                    dve.wait_ge(s_shift["A"], a.done())
                    for b in range(2):
                        dve.scalar_tensor_tensor(out=x1[q][:, b, :], in0=moved[:, b, :], scalar=ln_gain[:, b:b + 1],
                                                 in1=x_in[q][:, b, :], op0=ALU.mult, op1=ALU.add).then_inc(s_x1, 1)
                if "B" in on:
                    adapter_gates_2(t, b_)
                if "C" in on:
                    part_lo(2, s_q_hi, c, s_q_lo)
                if "E" in on:
                    at = e.times(256)
                    cut = slice(at, at + 256) if isinstance(at, int) else bass.ds(at, 256)
                    lo(t, "xe", xe_hi[:, :, cut].rearrange("p k (b s) -> p k b s", b=2),
                       xe_lo[:, :, cut].rearrange("p k (b s) -> p k b s", b=2))
                if "B" in on:
                    adapter_gates_3(t, b_)
                if "D" in on:
                    dve.wait_ge(s_o, d.done())
                    dve.scalar_tensor_tensor(out=pair_of(xs, d), in0=bank_o, scalar=tanh_g[:, 1:2],
                                             in1=pair_of(xs, d), op0=ALU.mult, op1=ALU.add).then_inc(s_x3, 1)
                if "B" in on:
                    dve.wait_ge(s_up, b_.done())
                    dve.scalar_tensor_tensor(out=pair_of(xs, b_), in0=bank_f, scalar=tanh_g[:, 2:3],
                                             in1=x1[b_.parity][:, :, :], op0=ALU.mult, op1=ALU.add)\
                        .then_inc(s_x2, 1)
                if "E" in on:
                    router_1(t, e)
                    router_2(t, e)

            run_bodies(dve, body)

            for n in range(2 * NE):
                dve.wait_ge(s_ew_hi, n + 1)
                dve.tensor_tensor((win_lo, wout_lo)[n % 2][:, n // 2, :, :], w_stage[n % 2][:, :, :],
                                  (win_hi, wout_hi)[n % 2][:, n // 2, :, :], ALU.subtract).then_inc(s_ew_lo, 1)
            dve.wait_ge(s_eb, 32)

            def expert(k, first_group):
                q, e = k.parity, k.n % NE
                g = group_of(k)
                gq = g.parity if g.reg is None else None
                dve.wait_ge(s_gelu, k.done(KT))
                if not (first_group and k.n < 2):
                    dve.wait_ge(s_y, k.done(back=2))
                dve.tensor_copy(h_hi[q][:, :, :], h_f32[q][:, :, :]).then_inc(s_h_hi, 1)
                dve.wait_ge(s_h_hi, k.done())
                dve.tensor_tensor(h_lo[q][:, :, :], h_f32[q][:, :, :], h_hi[q][:, :, :], ALU.subtract)\
                    .then_inc(s_h_lo, 1)

            def add_up(k, first_group, gq, g):
                q, e = k.parity, k.n % NE
                if e == 0:
                    if not (first_group or (g.reg is None and g.n < 2)):
                        dve.wait_ge(s_out[gq], g.dma_done(back=2))
                    at = g.times(GROUP)
                    cut = slice(at, at + GROUP) if isinstance(at, int) else bass.ds(at, GROUP)
                    dve.tensor_copy(gate_g[gq][:, :, :], gate_all[:, cut, :]).then_inc(s_gate_g, 1)
                    dve.wait_ge(s_gate_g, g.done())
                dve.wait_ge(s_y, k.done())
                for b in range(GROUP):
                    dve.tensor_tensor(y_b[q][:, b, :], y_banks[q][b // 2][:, 256 * (b % 2):256 * (b % 2) + 256],
                                      bout_t[:, e, :], ALU.add).then_inc(s_y_b, 1)
                dve.wait_ge(s_y_b, k.done(GROUP))
                if e > 0:
                    dve.wait_ge(s_acc, k.done(GROUP, back=1))
                for b in range(GROUP):
                    if e == 0:
                        dve.tensor_scalar(acc[gq][:, b, :], y_b[q][:, b, :], gate_g[gq][:, b, e:e + 1], None,
                                          ALU.mult).then_inc(s_acc, 1)
                    else:
                        dve.scalar_tensor_tensor(out=acc[gq][:, b, :], in0=y_b[q][:, b, :],
                                                 scalar=gate_g[gq][:, b, e:e + 1], in1=acc[gq][:, b, :],
                                                 op0=ALU.mult, op1=ALU.add).then_inc(s_acc, 1)
                if e == NE - 1:
                    at = g.times(GROUP)
                    cut = slice(at, at + GROUP) if isinstance(at, int) else bass.ds(at, GROUP)
                    dve.wait_ge(s_acc, k.done(GROUP))
                    dve.scalar_tensor_tensor(out=acc[gq][:, :, :], in0=acc[gq][:, :, :], scalar=tanh_g[:, 3:4],
                                             in1=xs[:, cut, :], op0=ALU.mult, op1=ALU.add).then_inc(s_fin, 1)

            def turn(n, base_group, g, last=False):
                pass

            expert(Count(0), True)
            for n in range(2 * NE):
                k = Count(n)
                expert(k.plus(1), k.n < NE - 1)
                add_up(k, k.n < NE, n // NE, Step(n // NE))
            with dve.Fori(1, NG // 2 - 1) as u:
                for n in range(2 * NE):
                    k = Count(n, u, 2)
                    expert(k.plus(1), False)
                    add_up(k, False, n // NE, Step(n // NE, u))
            for n in range(2 * NE):
                k = Count(n + NE * (NG - 2))
                if k.n < NE * NG - 1:
                    expert(k.plus(1), False)
                add_up(k, False, n // NE, Step(NG - 2 + n // NE))


KINDS = ("k_hi", "k_lo", "q_hi", "q_lo")
B_DIFF, B_DOWN, B_STEPS = 4, 8, 15
E_DIFF, E_BOTH, E_STEPS = 4, 10, 15


class Count(Step):

    def __init__(self, n, reg=None, groups=1):
        super().__init__(n, reg)
        self.groups = groups

    def plus(self, k):
        return Count(self.n + k, self.reg, self.groups)

    def times(self, k, plus=0):
        if self.reg is None:
            return self.n * k + plus
        return self.reg * (NE * self.groups * k) + (self.n * k + plus)


def group_of(k):
    if k.reg is None:
        return Step(k.n // NE)

    class Group(Step):
        def times(self, m, plus=0):
            return self.reg * (k.groups * m) + (self.n * m + plus)
    return Group(k.n // NE, k.reg)


def experts_loop(eng, one):
    for n in range(NE):
        one(Count(n), True)
    with eng.Fori(1, NG) as g:
        for n in range(NE):
            one(Count(n, g), False)


def kernel(**inputs):
    import numpy as np
    import concourse.bacc as bacc
    from concourse.bass_utils import run_bass_kernel_spmd as run

    a = {k: np.asarray(v) for k, v in inputs.items()}
    f = np.float32
    gap = np.zeros((D, NA), f)
    wall = np.concatenate([a["L0_ffn_W"].T, a["L1_xattn_Wk"], a["L1_xattn_Wv"], a["L1_xattn_Wq"],
                           a["L0_ffn_Wp"].T] + [a[f"L0_ffn_Wd{i}"].T for i in range(NA)] + [gap, a["L1_ffn_router_w"]],
                          axis=1)
    wu = np.concatenate([a[f"L0_ffn_Wu{i}"].T for i in range(NA)], axis=0)
    steps = np.arange(S)
    decay = np.where(steps[None, :] >= steps[:, None], 0.9 ** np.maximum(steps[None, :] - steps[:, None], 0), 0.0)
    arrays = {
        "x": a["x"], "ctx": a["ctx_1024"], "mask": a["mask_BxS2_ik0"].T,
        "gates": np.stack([a["g_xattn"][0], a["g_xattn"][1], a["g_ffn"][0], a["g_ffn"][1]]),
        "temp": a["L0_ffn_temp"], "bp": a["L0_ffn_bp"], "sim": a["L0_ffn_sim"], "wall": wall, "wp": a["L0_ffn_Wp"],
        "wu": wu, "wo": a["L1_xattn_Wo"].reshape(KT, 128, D).transpose(1, 0, 2),
        "w_in": a["L1_ffn_w_in"], "b_in": a["L1_ffn_b_in"].reshape(NE, KT, 128).transpose(2, 0, 1),
        "w_out": a["L1_ffn_w_out"], "b_out": a["L1_ffn_b_out"],
        "decay": decay.astype(f), "eye": np.eye(128, dtype=f),
    }
    nc = bacc.Bacc("TRN2", target_bir_lowering=False, num_devices=1)
    feed, aps = {}, []
    for name, v in arrays.items():
        v = np.ascontiguousarray(v)
        feed[f"in_{name}"] = v
        aps.append(nc.dram_tensor(f"in_{name}", v.shape, mybir.dt.from_np(v.dtype), kind="ExternalInput").ap())
    o = nc.dram_tensor("out_0", (BATCH, S, D), F32, kind="ExternalOutput").ap()
    build(nc, *aps, o)
    r = run(nc, [feed], core_ids=[0])
    return r.results[0]["out_0"]
```

```python
from contextlib import ExitStack

import concourse.bass as bass
from concourse import mybir

F32 = mybir.dt.float32
F16 = mybir.dt.float16
U32 = mybir.dt.uint32
I32 = mybir.dt.int32
ALU = mybir.AluOpType
ACT = mybir.ActivationFunctionType
AX = mybir.AxisListType.X

BATCH, S, D = 32, 128, 256
KT = D // 128
NP = BATCH // 2
HEADS, HD = 16, 16
PROJ = 64
RANKS = (1, 2, 4, 8)
NA = len(RANKS)
RSUM = sum(RANKS)
SMALL = PROJ + RSUM + NA
NE = 8
PROBS = 2
TOP = 2
TOKENS = BATCH * S
CAP = TOKENS + 128
SPARE = NE * CAP
BLOCKS = -(-(TOP * TOKENS + NE * 127) // 128 // 4) * 4
FAR = 4
LEFT = BLOCKS * 128
WIDE = D + 1
LN_EPS = 1e-5
CLAMP_MAX = 4.605170185988092

C_BASE, C_K, C_V, C_Q, C_SMALL = 0, 256, 512, 768, 1024
C_ROUTER = C_SMALL + SMALL
WCOLS = C_ROUTER + NE

LAG = {"A": 0, "B": 1, "C": 2, "D": 3, "E": 4, "F": 5}
BODIES = NP + LAG["F"]
LOOP_FROM, LOOP_TO = 6, NP
SPLITS = {t: (2 * i, 2 * i + 1) for i, t in enumerate([1, 2, 3, 4, 5, LOOP_TO, LOOP_TO + 1, LOOP_TO + 2])}

K_CAP, K_PAD, K_ID = 0, 8, 17
K_TRI = K_ID + NE
K_THR = K_TRI + NE * NE
K_BLK = K_THR + NE * (TOKENS // 128)
K_ROW = K_BLK + BLOCKS + FAR
KCOLS = K_ROW + BLOCKS + FAR
PLANNED = BLOCKS + FAR


class Step:

    def __init__(self, n, reg=None):
        self.n, self.reg = n, reg

    def __sub__(self, k):
        return Step(self.n - k, self.reg)

    @property
    def parity(self):
        return self.n % 2

    def times(self, k, plus=0):
        if self.reg is None:
            return self.n * k + plus
        return self.reg * (2 * k) + (self.n * k + plus)

    def done(self, per=1, back=0, short=0):
        return self.times(per, per * (1 - back) - short)

    def dma_done(self, per=16, back=0):
        half = self.n // 2 + 1 - back // 2
        return half * per if self.reg is None else self.reg * per + half * per


class Turns:

    def __init__(self, order):
        self.order = order

    def _before(self, t, name):
        n = 0
        for b in range(t + 1):
            for k, stage in self.order:
                if b == t and k == name:
                    return n
                n += 0 <= b - LAG[stage] < NP
        raise ValueError(name)

    def count(self, body, name, plus=0):
        if body.reg is None:
            return self._before(body.n, name) + plus
        k = len(self.order)
        at = self._before(LOOP_FROM, name)
        return body.times(k, at - k * LOOP_FROM + plus)


T_TURNS = Turns([("xb", "B"), ("ctx", "C"), ("xc", "C"), ("xe", "E")])
G_TURNS = Turns([("small", "B"), ("rank", "F"), ("down", "B"), ("logits", "E")])


def need(eng, sem, count):
    if not isinstance(count, int) or count > 0:
        eng.wait_ge(sem, count)


def need_apart(eng, sem, count, passed):
    if isinstance(count, int):
        need(eng, sem, count)
    else:
        count = eng.to_reg(count)
        eng.wait_ge(passed, 1)
        eng.wait_ge(sem, count)


def run_bodies(eng, body, after_first=None, loop_to=LOOP_TO, beside=None):
    def active(t):
        return {s for s, lag in LAG.items() if 0 <= t - lag < NP}

    for t in range(LOOP_FROM):
        body(Step(t), active(t))
        if t == 0 and after_first:
            after_first()
        if beside:
            beside(t)
    with eng.Fori(LOOP_FROM // 2, loop_to // 2) as u:
        for half in range(2):
            body(Step(half, u), set(LAG))
    for t in range(loop_to, BODIES):
        body(Step(t), active(t))
        if beside:
            beside(t)


class Block(Step):

    def __add__(self, k):
        return Block(self.n + k, self.reg)

    def __sub__(self, k):
        return Block(self.n - k, self.reg)

    def times(self, k, plus=0):
        if self.reg is None:
            return self.n * k + plus
        return self.reg * (FAR * k) + (self.n * k + plus)

    def dma_done(self, per=16, back=0):
        turns = self.n // FAR + 1 - back // FAR
        return turns * per if self.reg is None else self.reg * per + turns * per


def run_blocks(eng, step, last, entries, ahead=0):
    known = entries(Block(0), True)
    for n in range(-ahead, 0):
        step(Block(n), known)
    known = entries(Block(0), False, known)
    for n in range(FAR):
        step(Block(n), known)
    with eng.Fori(1, BLOCKS // FAR - 1) as u:
        known = entries(Block(0, u), False)
        for n in range(FAR):
            step(Block(n, u), known)
    known = entries(Block(BLOCKS - FAR), False)
    for n in range(BLOCKS - FAR, last):
        step(Block(n), known)


def build(nc, x, ctx, mask, gates_in, temp, bp, sim, wall, wp, wu, wo, w_in, b_in, w_out, b_out, decay, eye, before,
          routing, y_rows_in, left_rows_in, out):
    st = ExitStack()
    with st:
        def sb(name, shape, dt=F32):
            return st.enter_context(nc.sbuf_tensor(name, shape, dt))

        def bank(name, dt=F32):
            return st.enter_context(nc.psum_tensor(name, [128, 512], dt))

        def sem(name):
            return st.enter_context(nc.semaphore(name))

        ident = sb("ident", [128, 128])
        ident16 = sb("ident16", [128, 128], F16)
        decay_t = sb("decay_t", [128, 128])
        w_hi = sb("w_hi", [128, KT, WCOLS], F16)
        w_lo = sb("w_lo", [128, KT, WCOLS], F16)
        wo_t = sb("wo_t", [128, KT, D])
        wu_f32 = sb("wu_f32", [128, D])
        wu_parts = sb("wu_parts", [128, D], F16)
        small_bias = sb("small_bias", [128, SMALL])
        gates_raw = sb("gates_raw", [128, 4])
        tanh_g = sb("tanh_g", [128, 4])
        mask_i = sb("mask_i", [128, BATCH], I32)
        keep_all = sb("keep_all", [128, BATCH])
        minus_half = sb("minus_half", [128, 8])
        adapter_id = sb("adapter_id", [128, 2, RSUM])
        adapter_wt = sb("adapter_wt", [128, 2, NA])
        wp_t = sb("wp_t", [PROJ, D])
        sim_t = sb("sim_t", [PROJ, NA])
        sim_sq = sb("sim_sq", [PROJ, NA])
        sim_inv = sb("sim_inv", [PROJ, NA])
        sim_n = sb("sim_n", [PROJ, NA])
        temp_t = sb("temp_t", [PROJ, 1])
        temp_e = sb("temp_e", [PROJ, 1])
        bp_col = sb("bp_col", [PROJ, 1])
        bp_wide = sb("bp_wide", [PROJ, 128])
        ones = sb("ones", [PROJ, 128])

        xs = sb("xs", [128, BATCH, D])
        w_f32 = sb("w_f32", [128, KT, WCOLS])
        route = sb("route", [128, KCOLS])
        before_t = sb("before_t", [128, 128], F16)
        ones16 = sb("ones16", [128, 128], F16)
        gate_all = sb("gate_all", [128, BATCH, TOP])
        y_rows = sb("y_rows", [128, NP, 2 * TOP])
        left_rows = sb("left_rows", [128, BLOCKS])
        running = sb("running", [128, NE])
        zeros = sb("zeros", [128, WIDE])
        count = sb("count", [128, NE])
        n_blocks = sb("n_blocks", [128, NE])
        end = sb("end", [128, NE])
        start = sb("start", [128, NE])
        y_base = sb("y_base", [128, NE])
        pad = sb("pad", [128, NE + 1])
        pad_u = sb("pad_u", [128, NE + 1], U32)
        used = sb("used", [1, PLANNED])
        row_sum = sb("row_sum", [1, PLANNED])
        owner = sb("owner", [1, PLANNED])
        row_f = sb("row_f", [1, PLANNED])
        table = sb("table", [1, len(LINES), PLANNED], I32)
        bout_t = sb("bout_t", [128, NE, D])

        def two(name, shape, dt=F32):
            return [sb(f"{name}{i}", shape, dt) for i in range(2)]

        win_hi = sb("win_hi", [128, NE, KT, D], F16)
        win_lo = sb("win_lo", [128, NE, KT, D], F16)
        wout_hi = sb("wout_hi", [128, NE, KT, D], F16)
        wout_lo = sb("wout_lo", [128, NE, KT, D], F16)
        w_stage = two("w_stage", [128, KT, D])
        bin_t = sb("bin_t", [128, NE, KT])

        outer, pairs = sb, ExitStack()

        def sb(name, shape, dt=F32):
            return pairs.enter_context(nc.sbuf_tensor(name, shape, dt))

        def two(name, shape, dt=F32):
            return [pairs.enter_context(nc.sbuf_tensor(f"{name}{i}", shape, dt)) for i in range(2)]

        x_in = two("x_in", [128, 2, D])
        c_in = two("c_in", [128, 2, D])
        c_again = two("c_again", [128, 2, D])
        kv = two("kv", [128, 2, D])
        x1 = two("x1", [128, 2, D])
        moved = sb("moved", [128, 2, D])
        ln_gain = sb("ln_gain", [128, 2])
        LN = "ABCE"
        stats = {k: sb(f"stats_{k}", [128, 2, 6]) for k in LN}
        mv = {k: two(f"mv_{k}", [128, 2, 2]) for k in LN}
        var = {k: two(f"var_{k}", [128, 2]) for k in LN}
        rstd = {k: two(f"rstd_{k}", [128, 2]) for k in LN}
        shift = {k: two(f"shift_{k}", [128, 2]) for k in LN}
        xn = {k: sb(f"xn_{k}", [128, 2, D]) for k in "BC"}
        xn_e = two("xn_E", [128, 2 * TOP, WIDE])
        xt_hi = {k: sb(f"xt_hi_{k}", [128, KT, 256], F16) for k in "BCE"}
        xt_lo = {k: sb(f"xt_lo_{k}", [128, KT, 256], F16) for k in "BCE"}
        ct_hi = sb("ct_hi", [128, KT, 256], F16)
        ct_lo = sb("ct_lo", [128, KT, 256], F16)
        small = sb("small", [128, 2, SMALL])
        square = sb("square", [128, 2, PROJ])
        norm2 = sb("norm2", [128, 2])
        norm2c = sb("norm2c", [128, 2])
        inv_norm = sb("inv_norm", [128, 2])
        lg = sb("lg", [128, 2, NA])
        lmax = sb("lmax", [128, 2])
        ldiff = sb("ldiff", [128, 2, NA])
        lsig = sb("lsig", [128, 2, NA])
        lsig_n = sb("lsig_n", [128, 2, NA])
        lrec = sb("lrec", [128, 2, NA])
        lexp = sb("lexp", [128, 2, NA])
        lsum = sb("lsum", [128, 2])
        ltop = sb("ltop", [128, 2])
        lcode = sb("lcode", [128, 2, NA])
        lwin = sb("lwin", [128, 2])
        picked = sb("picked", [128, 2, RSUM])
        down = sb("down", [128, 2, RSUM])
        down_g = sb("down_g", [128, 2, RSUM])
        down_parts = sb("down_parts", [128, 2, 128], F16)
        down_t = sb("down_t", [128, 2, 128], F16)
        keep = two("keep", [128, 2])
        parts = two("parts", [128, len(KINDS), KT, 256], F16)
        k_stack = two("k_stack", [128, 4, KT, 256], F16)
        q_stack = two("q_stack", [128, 2, 4, KT, 256], F16)
        v_wide = two("v_wide", [128, 2, 8, 4, HD])
        prob = [sb(f"prob{i}", [128, 4, 2, 128]) for i in range(PROBS)]
        av = sb("av", [128, KT, 2, 128])
        rl = sb("rl", [128, 2, NE])
        rmax = sb("rmax", [128, 2, 8])
        rindex = sb("rindex", [128, 2, 8], U32)
        rdiff = sb("rdiff", [128, 2, NE])
        rsig = sb("rsig", [128, 2, NE])
        rsig_n = sb("rsig_n", [128, 2, NE])
        rrec = sb("rrec", [128, 2, NE])
        rexp = sb("rexp", [128, 2, NE])
        rsum = sb("rsum", [128, 2])
        rinv = sb("rinv", [128, 2])
        picks = sb("picks", [128, 2 * TOP, NE])
        both = sb("both", [128, 2, NE], F16)
        chosen = sb("chosen", [128, 2, TOP])
        slot = sb("slot", [128, 2, TOP])
        pick_exp = sb("pick_exp", [128, 2, TOP, NE])
        top_exp = sb("top_exp", [128, 2, TOP])
        rank = sb("rank", [128, 2, NE])
        pick_row = sb("pick_row", [128, 2, TOP, NE])
        slot_u = two("slot_u", [128, 2 * TOP], U32)

        pairs.close()

        def several(name, n, shape, dt=F32):
            return [outer(f"{name}{i}", shape, dt) for i in range(n)]

        over = outer("over", [128, NE, TOKENS // 128])
        in_block = outer("in_block", [1, PLANNED, NE])
        below = outer("below", [1, PLANNED, NE])
        row_part = outer("row_part", [1, PLANNED, NE])
        ends = outer("ends", [128, NE, NE])
        xb = several("xb", FAR, [128, WIDE])
        xb_hi = several("xb_hi", 2, [128, KT, 128], F16)
        xb_lo = several("xb_lo", 2, [128, KT, 128], F16)
        h_f32 = several("h_f32", 2, [128, KT, 128])
        h_hi = several("h_hi", 2, [128, KT, 128], F16)
        h_lo = several("h_lo", 2, [128, KT, 128], F16)
        y_out = several("y_out", FAR, [128, D])
        y_row = several("y_row", FAR, [128, 1], U32)
        y_got = several("y_got", PICK_BUFS, [128, 2, TOP * D])
        half_sum = several("half_sum", 2, [128, D])
        result = several("result", PICK_BUFS, [128, 2, D])

        names = ["R", "T", "J", "F", "G", "S0", "S1", "O"]
        P = {n: bank(f"ps_{n}") for n in names}
        bank_r = P["R"][:, :].rearrange("p (b d) -> p b d", b=2)
        bank_t = P["T"][:, :].rearrange("p (k b s) -> p k b s", k=KT, b=2)
        bank_j = P["J"][:, :].rearrange("p (k c) -> p k c", k=2)
        bank_f = P["F"][:, :].rearrange("p (b d) -> p b d", b=2)
        bank_g = P["G"]
        g_small = bank_g[:, 0:2 * SMALL].rearrange("p (b c) -> p b c", b=2)
        g_down = bank_g[:, 0:128].bitcast(F16).rearrange("p (b s) -> p b s", b=2)
        g_logits = bank_g[:, 0:2 * NE].rearrange("p (b e) -> p b e", b=2)
        bank_s = [P[f"S{i}"][:, :].rearrange("p (n h s) -> p n h s", n=2, h=2) for i in range(2)]
        bank_av = P["O"][:, :].rearrange("p (k b s) -> p k b s", k=KT, b=2)
        bank_o = P["O"][:, :].rearrange("p (b d) -> p b d", b=2)

        g_rank = bank_g[:, 0:3 * NE].rearrange("p (b e) -> p b e", b=3)

        xb_banks = [P["R"][:, 0:D].rearrange("p (k s) -> p k s", k=KT), P["T"][:, 0:D].rearrange("p (k s) -> p k s", k=KT)]
        hid_banks = [P["J"][:, 0:D].rearrange("p (k s) -> p k s", k=KT), P["F"][:, 0:D].rearrange("p (k s) -> p k s", k=KT)]
        y_banks = [P["G"][:, 0:D], P["S0"][:, 0:D]]

        s_const = sem("constants_loaded")
        s_first = sem("first_constants_loaded")
        s_wo = sem("output_weights_loaded")
        s_wall = sem("weights_loaded")
        s_wup = sem("adapter_ups_loaded")
        s_tanh = sem("gates_tanh_made")
        s_zero = sem("zeroed")
        s_iota = sem("iotas_made")
        s_set = sem("setup_vector_steps")
        s_set_p = sem("setup_pool_steps")
        s_set_t = sem("setup_products")
        s_set_a = sem("setup_scalar_steps")
        s_whi = sem("weights_hi_made")
        s_wlo = sem("weights_lo_made")
        s_x = [sem(f"x_loaded{i}") for i in range(2)]
        s_c = [sem(f"ctx_loaded{i}") for i in range(2)]
        s_c2 = [sem(f"ctx_again_loaded{i}") for i in range(2)]
        s_stats = {k: sem(f"stats_{k}_made") for k in LN}
        s_aggr = {k: sem(f"mean_{k}_made") for k in LN}
        s_var = {k: sem(f"variance_{k}_made") for k in LN}
        s_rstd = {k: sem(f"rstd_{k}_made") for k in LN}
        s_shift = {k: sem(f"shift_{k}_made") for k in LN}
        s_xn = {k: sem(f"normed_{k}") for k in "BCE"}
        s_kv = sem("ctx_squared")
        s_scan = sem("running_sum_made")
        s_moved = sem("sum_weighted")
        s_x1 = sem("x1_made")
        s_t = sem("transposed")
        s_t_hi = sem("transposed_hi_copied")
        s_t_lo = sem("transposed_lo_copied")
        s_f = sem("base_product_made")
        s_g = sem("g_bank_written")
        s_g_free = sem("g_bank_read")
        s_small = sem("small_products_copied")
        s_rl = sem("logits_copied")
        s_square = sem("projection_squared")
        s_norm = sem("norm_clamped")
        s_inv = sem("inverse_norm_made")
        s_b = sem("adapter_gate_steps")
        s_lsig = sem("adapter_sigmoids_made")
        s_down = sem("gated_downs_split")
        s_up = sem("ups_added")
        s_x2 = sem("x2_made")
        s_keep = sem("keep_copied")
        s_k = sem("keys_made")
        s_k_hi = sem("keys_hi_copied")
        s_k_lo = sem("keys_lo_copied")
        s_v = sem("values_made")
        s_v_wide = sem("values_masked")
        s_q = sem("queries_made")
        s_q_hi = sem("queries_hi_copied")
        s_q_lo = sem("queries_lo_copied")
        s_scratch = [sem(f"parts_stored{i}") for i in range(2)]
        s_stacked = [sem(f"stacked{i}") for i in range(2)]
        s_score = sem("scores_made")
        s_prob = sem("probabilities_made")
        s_pv = sem("values_weighted")
        s_av = sem("attended_copied")
        s_o = sem("attention_projected")
        s_x3 = sem("x3_made")
        s_e = sem("router_steps")
        s_rsig = sem("router_sigmoids_made")
        s_gate = sem("gates_made")
        s_ew = [sem(f"expert_weights_loaded{i}") for i in range(2)]
        s_eb = sem("expert_biases_loaded")
        s_ew_hi = sem("expert_weights_hi_made")
        s_ew_lo = sem("expert_weights_lo_made")
        s_run = sem("first_rows_set")
        s_both = sem("choices_made")
        s_r = sem("rank_steps")
        s_slot = sem("slots_made")
        s_scat = [sem(f"rows_scattered{i}") for i in range(2)]
        s_plan = sem("plan_steps")
        s_pad = [sem(f"padding_zeroed{i}") for i in range(NE + 1)]
        s_xb = [sem(f"block_loaded{i}") for i in range(FAR)]
        s_xb_t = sem("block_transposed")
        s_xb_hi = sem("block_hi_copied")
        s_xb_lo = sem("block_lo_copied")
        s_h = sem("hidden_product_made")
        s_gelu = sem("gelu_made")
        s_h_hi = sem("hidden_hi_made")
        s_h_lo = sem("hidden_lo_made")
        s_y = sem("expert_product_made")
        s_y_row = sem("output_rows_taken")
        s_y_out = sem("expert_output_made")
        s_y_kept = [sem(f"expert_output_scattered{i}") for i in range(FAR)]
        s_got = [sem(f"outputs_loaded{i}") for i in range(PICK_BUFS)]
        s_half = sem("first_choice_added")
        s_fin = sem("output_made")
        s_out = [sem(f"output_stored{i}") for i in range(PICK_BUFS)]

        STACK_DMAS = 4 + 8
        N_CONST = 11
        N_IOTA = 2 * NA + 2 + 4

        scratch = [nc.dram_tensor(f"parts_scratch{i}", (len(KINDS), 128, KT * 256), F16, kind="Internal").ap()
                   for i in range(2)]

        store_x = nc.dram_tensor("store_x", (SPARE + 128, WIDE), F32, kind="Internal").ap()
        store_y = nc.dram_tensor("store_y", (LEFT + TOP * TOKENS, D), F32, kind="Internal").ap()

        block = st.enter_context(nc.Block())

        def plan_reader(eng, line, shift, n, top):
            row_at, calls = LINES.index(line), []

            def entries(i, before, known=None):
                if known is not None and shift == 0:
                    return known
                at = i.times(1, 0 if before else shift)
                regs = [eng.alloc_register(f"{line}{len(calls)}_{k}") for k in range(n)]
                calls.append(regs)
                eng.reg_load(regs, table[0:1, row_at, at:at + n] if isinstance(at, int)
                             else table[0:1, row_at, bass.ds(at, n)])
                return [bass.RuntimeValue.of_register_unchecked(x).with_bounds(min_val=0, max_val=top) for x in regs]
            return entries

        @block.sync
        def _(sp):
            def pair_rows(t, pair):
                at = pair.times(2)
                return t[at:at + 2] if isinstance(at, int) else t[bass.ds(at, 2)]

            def load_a(p):
                q = p.parity
                need_apart(sp, s_x1, p.done(2, back=2), s_zero)
                sp.dma_start(x_in[q][:, :, :], pair_rows(x, p).rearrange("b s d -> s b d")).then_inc(s_x[q], 16)
                need_apart(sp, s_kv, p.done(back=2), s_zero)
                sp.dma_start(c_in[q][:, :, :], pair_rows(ctx, p).rearrange("b s d -> s b d")).then_inc(s_c[q], 16)

            def load_c(p, body):
                q = p.parity
                need_apart(sp, s_k, p.done(back=2), s_zero)
                sp.dma_start(c_again[q][:, :, :],
                             pair_rows(ctx, p).rearrange("b s d -> s b d")).then_inc(s_c2[q], 16)

            def stack_keys(p):
                q = p.parity
                need_apart(sp, s_stacked[q], p.dma_done(16 * STACK_DMAS, back=2), s_zero)
                sp.wait_ge(s_k_hi, p.done())
                sp.wait_ge(s_k_lo, p.done())
                sp.dma_start(scratch[q][0:2].rearrange("n p c -> p n c"),
                             parts[q][:, 0:2, :, :].rearrange("p n k c -> p n (k c)")).then_inc(s_scratch[q], 16)
                need_apart(sp, s_score, p.done(4, back=2), s_zero)
                sp.wait_ge(s_scratch[q], p.dma_done(32) - 16)
                for c in range(4):
                    sp.dma_start(k_stack[q][32 * c:32 * c + 32, :, :, :].rearrange("r g k c -> r g (k c)"),
                                 scratch[q][c % 2].rearrange("(g r) c -> r g c", g=4)).then_inc(s_stacked[q], 16)

            def stack_queries(p, meanwhile):
                q = p.parity
                sp.wait_ge(s_q_hi, p.done())
                sp.wait_ge(s_q_lo, p.done())
                sp.dma_start(scratch[q][2:4].rearrange("n p c -> p n c"),
                             parts[q][:, 2:4, :, :].rearrange("p n k c -> p n (k c)")).then_inc(s_scratch[q], 16)
                meanwhile()
                sp.wait_ge(s_scratch[q], p.dma_done(32))
                for c in range(4):
                    for h in range(2):
                        at = 32 * c + HD * h
                        sp.dma_start(q_stack[q][at:at + HD, h, :, :, :].rearrange("r g k c -> r g (k c)"),
                                     scratch[q][2 + c // 2].rearrange("(g h r) c -> h r g c", g=4, h=2)[h])\
                            .then_inc(s_stacked[q], 16)

            load_a(Step(0))
            def load(sem_, dst, src):
                sp.dma_start(dst[tuple(slice(None) for _ in dst.shape)], src).then_inc(sem_, 16)

            load(s_first, decay_t, decay)
            load(s_first, gates_raw, gates_in.partition_broadcast(128))
            load(s_const, sim_t, sim)
            load(s_const, temp_t, temp.partition_broadcast(PROJ))
            load(s_const, bp_col, bp.rearrange("(p a) -> p a", a=1))
            load(s_const, wp_t, wp)
            sp.dma_start(w_f32[:, :, :], wall.rearrange("(k p) c -> p k c", p=128)).then_inc(s_wall, 16)
            load(s_const, ident, eye)
            load(s_const, mask_i, mask)
            load(s_const, route, routing)
            load(s_const, before_t, before)
            load(s_const, y_rows, y_rows_in)
            load(s_const, left_rows, left_rows_in)
            sp.wait_ge(s_zero, 2)
            sp.dma_start(small_bias[:, 0:PROJ], bp.partition_broadcast(128)).then_inc(s_const, 16)
            for i in range(3):
                sp.dma_start(wu_f32[32 * i:32 * i + RSUM, :], wu).then_inc(s_wup, 16)
            load(s_wo, wo_t, wo)

            def body(t, on):
                nxt = t - (-1)

                def loads():
                    if nxt.reg is not None or nxt.n < NP:
                        load_a(nxt)
                    c_next = nxt - LAG["C"]
                    if c_next.reg is not None or 0 <= c_next.n < NP:
                        load_c(c_next, t)

                if "C" in on:
                    stack_keys(t - LAG["C"])
                    stack_queries(t - LAG["C"], loads)
                else:
                    loads()

            def matrices(t):
                for n in SPLITS.get(t, ()):
                    src = (w_in, w_out)[n % 2]
                    if n >= 2:
                        sp.wait_ge(s_ew_hi, n - 1)
                        sp.wait_ge(s_ew_lo, n - 1)
                    sp.dma_start(w_stage[n % 2][:, :, :], src[n // 2].rearrange("(k p) c -> p k c", p=128))\
                        .then_inc(s_ew[n % 2], 16)

            for t in range(LOOP_FROM):
                matrices(t)
                body(Step(t), {s for s, lag in LAG.items() if 0 <= t - lag < NP})
            sp.dma_start(bin_t[:, :, :], b_in).then_inc(s_eb, 16)
            sp.dma_start(bout_t[:, :, :], b_out.partition_broadcast(128)).then_inc(s_eb, 16)
            with sp.Fori(LOOP_FROM // 2, LOOP_TO // 2 - 1) as u:
                for half in range(2):
                    body(Step(half, u), set(LAG))
            for t in range(LOOP_TO - 2, BODIES):
                matrices(t)
                body(Step(t), {s for s, lag in LAG.items() if 0 <= t - lag < NP})

            sp.wait_ge(s_plan, PLAN_STEPS)
            for i in range(2):
                sp.wait_ge(s_scat[i], 16 * 2 * TOP * NP // 2)
            for i in range(NE + 1):
                sp.wait_ge(s_pad[i], 16)

            def load_block(i, at):
                if i.reg is not None or i.n >= FAR:
                    need_apart(sp, s_xb_t, i.done(back=FAR), s_zero)
                    need_apart(sp, s_y_row, i.done(back=FAR), s_zero)
                sp.dma_start(xb[i.n % FAR][:, :], store_x[bass.ds(at, 128), :]).then_inc(s_xb[i.n % FAR], 16)

            def sp_step(i, rows):
                if i.reg is not None or i.n + FAR - 1 < BLOCKS:
                    load_block(i + (FAR - 1), rows[(i.n + FAR - 1 if i.n < 0 else i.n) % FAR])
            run_blocks(sp, sp_step, BLOCKS, plan_reader(sp, "row", FAR - 1, FAR, SPARE), ahead=FAR - 1)

            for i in range(FAR):
                sp.wait_ge(s_y_kept[i], 16 * BLOCKS // FAR)
            for n in range(NP + PICK_BUFS - 1):
                if n < NP:
                    if n >= PICK_BUFS:
                        sp.wait_ge(s_fin, 2 * (n - PICK_BUFS + 1))
                    at = LEFT + 2 * n * TOP * 128
                    sp.dma_start(y_got[n % PICK_BUFS][:, :, :], store_y[at:at + 2 * TOP * 128]
                                 .rearrange("(b s k) d -> s b (k d)", b=2, k=TOP)).then_inc(s_got[n % PICK_BUFS], 16)
                m = n - (PICK_BUFS - 1)
                if m >= 0:
                    sp.wait_ge(s_fin, 2 * m + 2)
                    sp.dma_start(out[2 * m:2 * m + 2].rearrange("b s d -> s b d"), result[m % PICK_BUFS][:, :, :])\
                        .then_inc(s_out[m % PICK_BUFS], 16)
            for i in range(PICK_BUFS):
                sp.wait_ge(s_out[i], 16 * NP // PICK_BUFS)

        @block.gpsimd
        def _(pool):
            pool.memset(minus_half[:, :], -0.5).then_inc(s_set_p, 1)
            at = 0
            for a, r in enumerate(RANKS):
                pool.memset(adapter_id[:, :, at:at + r], float(NA - a)).then_inc(s_iota, 1)
                pool.memset(adapter_wt[:, :, a:a + 1], float(NA - a)).then_inc(s_iota, 1)
                at += r
            pool.memset(zeros[:, :], 0.0).then_inc(s_iota, 1)
            pool.memset(ones16[:, :], 1.0).then_inc(s_iota, 1)
            for q in range(2):
                pool.memset(q_stack[q][:, :, :, :, :], 0.0).then_inc(s_iota, 1)
                pool.memset(v_wide[q][:, :, :, :, :], 0.0).then_inc(s_iota, 1)
            pool.wait_ge(s_set_p, 1)

            def setup():
                pool.wait_ge(s_set, 2)
                pool.tensor_tensor(sim_inv[:, :], sim_sq[:, :], minus_half[0:PROJ, 0:NA], ALU.pow)\
                    .then_inc(s_set_p, 1)

            def inverse_root(k, p):
                q = p.parity
                pool.wait_ge(s_var[k], p.done())
                pool.tensor_tensor(rstd[k][q][:, :], var[k][q][:, :], minus_half[:, 0:2], ALU.pow)\
                    .then_inc(s_rstd[k], 1)

            def squared(p):
                q = p.parity
                pool.wait_ge(s_c[q], p.dma_done())
                need(pool, s_scan, p.done(back=2))
                pool.tensor_tensor(kv[q][:, :, :], c_in[q][:, :, :], c_in[q][:, :, :], ALU.mult).then_inc(s_kv, 1)

            def scatter(p):
                q = p.parity
                need_apart(pool, s_slot, p.done(), s_zero)
                for b in range(2):
                    for k in range(TOP):
                        at = b * TOP + k
                        pool.indirect_dma_start(store_x, bass.IndirectOffsetOnAxis(slot_u[q][:, at:at + 1], 0),
                                                xn_e[q][:, at, :], None).then_inc(s_scat[q], 16)

            squared(Step(0))

            def body(t, on):
                if "A" in on:
                    inverse_root("A", t - LAG["A"])
                if "C" in on:
                    inverse_root("C", t - LAG["C"])
                if "E" in on:
                    inverse_root("E", t - LAG["E"])
                if "B" in on:
                    p = t - LAG["B"]
                    pool.wait_ge(s_norm, p.done())
                    pool.tensor_tensor(inv_norm[:, :], norm2c[:, :], minus_half[:, 0:2], ALU.pow).then_inc(s_inv, 1)
                if "A" in on:
                    inverse_root("B", t - LAG["A"])
                nxt = t - (-1)
                if nxt.reg is not None or nxt.n < NP:
                    squared(nxt)
                if "F" in on:
                    scatter(t - LAG["F"])

            run_bodies(pool, body, after_first=setup, loop_to=LOOP_TO - 2)

            pool.wait_ge(s_plan, PAD_STEPS)
            for e in range(NE + 1):
                pool.indirect_dma_start(store_x, bass.IndirectOffsetOnAxis(pad_u[:, e:e + 1], 0), zeros[:, :], None)\
                    .then_inc(s_pad[e], 16)

            def scatter_block(i, _):
                need_apart(pool, s_y_out, i.done(), s_plan)
                pool.indirect_dma_start(store_y, bass.IndirectOffsetOnAxis(y_row[i.n % FAR][:, :], 0),
                                        y_out[i.n % FAR][:, :], None).then_inc(s_y_kept[i.n % FAR], 16)

            run_blocks(pool, scatter_block, BLOCKS, lambda i, before, known=None: None)

        @block.scalar
        def _(act):
            act.wait_ge(s_first, 32)
            act.activation(tanh_g[:, :], gates_raw[:, :], ACT.Tanh).then_inc(s_tanh, 1)

            def setup():
                act.wait_ge(s_set, 3)
                act.activation(temp_e[:, :], temp_e[:, :], ACT.Exp).then_inc(s_set_a, 1)
                act.wait_ge(s_const, 16 * N_CONST)
                act.activation(ident16[:, :], ident[:, :], ACT.Copy).then_inc(s_set_a, 1)
                act.wait_ge(s_wup, 48)
                act.wait_ge(s_zero, 2)
                act.activation(wu_parts[:, :], wu_f32[:, :], ACT.Copy).then_inc(s_whi, 1)
                act.wait_ge(s_set, 5 + 1)
                act.activation(w_hi[:, :, :], w_f32[:, :, :], ACT.Copy).then_inc(s_whi, 1)

            def hi(t, name, dst):
                act.wait_ge(s_t, T_TURNS.count(t, name, 1))
                act.activation(dst, bank_t, ACT.Copy).then_inc(s_t_hi, 1)

            def normed(k, p, src, read, dst=None):
                q = p.parity
                dst = dst or (lambda b: xn[k][:, b, :])
                need(act, s_t, read)
                act.wait_ge(s_shift[k], p.done())
                for b in range(2):
                    act.activation(dst(b), src(b), ACT.Identity, bias=shift[k][q][:, b:b + 1],
                                   scale=rstd[k][q][:, b:b + 1]).then_inc(s_xn[k], 1)

            def stored(p):
                def at(b):
                    i = p.times(2, b)
                    return xs[:, i, :] if isinstance(i, int) else xs[:, bass.ds(i, 1), :]
                return at

            def sigmoids(p, m):
                act.wait_ge(s_score, p.times(4, m + 1))
                need(act, s_pv, p.times(4, m + 1 - PROBS))
                for n in range(2):
                    ins = act.activation(prob[m % PROBS][:, 2 * n:2 * n + 2, :, :], bank_s[n], ACT.Sigmoid,
                                         scale=float(HD) ** -0.5)
                ins.then_inc(s_prob, 1)

            def part_hi(dst, ready, p, made):
                q = p.parity
                act.wait_ge(ready, p.done())
                need(act, s_scratch[q], p.dma_done(32, back=2))
                act.activation(parts[q][:, dst, :, :], bank_j, ACT.Copy).then_inc(made, 1)

            def body(t, on):
                a, b_, c, d, e, f = (t - lag for lag in LAG.values())
                if "B" in on:
                    hi(t, "xb", xt_hi["B"][:, :, :].rearrange("p k (b s) -> p k b s", b=2))
                if "D" in on:
                    sigmoids(d, 0)
                if "C" in on:
                    normed("C", c, stored(c), T_TURNS.count(t - 1, "xc", 1)
                           if t.reg is not None or t.n > LAG["C"] else 0)
                if "C" in on:
                    hi(t, "ctx", ct_hi[:, :, :].rearrange("p k (b s) -> p k b s", b=2))
                if "D" in on:
                    sigmoids(d, 1)
                if "C" in on:
                    part_hi(0, s_k, c, s_k_hi)
                    hi(t, "xc", xt_hi["C"][:, :, :].rearrange("p k (b s) -> p k b s", b=2))
                if "D" in on:
                    sigmoids(d, 2)
                if "E" in on:
                    need(act, s_scat[e.parity], e.dma_done(16 * 2 * TOP, back=2))
                    normed("E", e, lambda b: stored(e)(b).rearrange("p a d -> p (a d)").unsqueeze(1)
                           .broadcast_to([128, TOP, D]) if e.reg is not None else
                           stored(e)(b).unsqueeze(1).broadcast_to([128, TOP, D]), T_TURNS.count(t - 1, "xe", 1)
                           if t.reg is not None or t.n > LAG["E"] else 0,
                           lambda b: xn_e[e.parity][:, TOP * b:TOP * b + TOP, 0:D])
                if "C" in on:
                    part_hi(2, s_q, c, s_q_hi)
                if "B" in on:
                    act.wait_ge(s_b, b_.times(B_STEPS, B_DIFF))
                    act.activation(lsig[:, :, :], ldiff[:, :, :], ACT.Sigmoid).then_inc(s_lsig, 1)
                    act.activation(lsig_n[:, :, :], ldiff[:, :, :], ACT.Sigmoid, scale=-1.0).then_inc(s_lsig, 1)
                if "F" in on:
                    act.wait_ge(s_e, f.times(E_STEPS, E_DIFF))
                    act.activation(rsig[:, :, :], rdiff[:, :, :], ACT.Sigmoid).then_inc(s_rsig, 1)
                    act.activation(rsig_n[:, :, :], rdiff[:, :, :], ACT.Sigmoid, scale=-1.0).then_inc(s_rsig, 1)
                if "E" in on:
                    hi(t, "xe", xt_hi["E"][:, :, :].rearrange("p k (b s) -> p k b s", b=2))
                if "D" in on:
                    sigmoids(d, 3)
                if "A" in on:
                    normed("B", a, lambda b: x1[a.parity][:, b, :], T_TURNS.count(t, "xb", 1) if "B" in on else 0)
                if "D" in on:
                    act.wait_ge(s_pv, d.done(4))
                    need(act, s_o, d.done(back=1))
                    act.activation(av[:, :, :, :], bank_av, ACT.Copy).then_inc(s_av, 1)
                if "B" in on:
                    act.wait_ge(s_g, G_TURNS.count(t, "down", 1))
                    act.activation(down_t[:, :, :], g_down, ACT.Copy).then_inc(s_g_free, 1)
                if "C" in on:
                    q = c.parity
                    act.wait_ge(s_v, c.done())
                    act.wait_ge(s_keep, c.done())
                    need(act, s_pv, c.done(4, back=2))
                    if t.reg is None:
                        act.wait_ge(s_iota, N_IOTA)
                    for b in range(2):
                        act.activation(v_wide[q][:, b, :, 0:4:3, :],
                                       bank_j[:, b, :].rearrange("p (n h d) -> p n h d", n=8, h=2),
                                       ACT.Copy, scale=keep[q][:, b:b + 1]).then_inc(s_v_wide, 1)
            def matrices(t):
                for n in SPLITS.get(t, ()):
                    act.wait_ge(s_ew[n % 2], 16 * (n // 2 + 1))
                    act.activation((win_hi, wout_hi)[n % 2][:, n // 2, :, :], w_stage[n % 2][:, :, :], ACT.Copy)\
                        .then_inc(s_ew_hi, 1)

            run_bodies(act, body, after_first=setup, beside=matrices)

            act.wait_ge(s_eb, 32)
            act.wait_ge(s_plan, PLAN_STEPS)

            def copy_hi(i):
                q = i.n % 2
                act.wait_ge(s_xb_t, i.done())
                if i.reg is not None or i.n >= 2:
                    act.wait_ge(s_h, i.done(back=2))
                act.activation(xb_hi[q][:, :, :], xb_banks[q], ACT.Copy).then_inc(s_xb_hi, 1)

            biases = bin_t[:, :, :].rearrange("p e m -> p (e m)")

            def gelu(i, at):
                q = i.n % 2
                if i.reg is not None or i.n >= 2:
                    need_apart(act, s_h_lo, i.done(back=2), s_tanh)
                need_apart(act, s_h, i.done(), s_tanh)
                for m in range(KT):
                    act.activation(h_f32[q][:, m, :], hid_banks[q][:, m, :], ACT.Gelu_apprx_tanh,
                                   bias=biases[:, bass.ds(at + m, 1)]).then_inc(s_gelu, 1)
                act.wait_ge(s_gelu, i.done(KT))
                if i.reg is not None or i.n >= 2:
                    act.wait_ge(s_y, i.done(back=2))
                act.activation(h_hi[q][:, :, :], h_f32[q][:, :, :], ACT.Copy).then_inc(s_h_hi, 1)

            def act_step(i, bias_at):
                if i.reg is not None or i.n + 2 < BLOCKS:
                    copy_hi(i + 2)
                if i.reg is not None or 0 <= i.n + 1 < BLOCKS:
                    gelu(i + 1, bias_at[(i.n % FAR if i.n >= 0 else i.n) + 1])

            run_blocks(act, act_step, BLOCKS - 1,
                       plan_reader(act, "bias_at", 0, FAR + 1, KT * (NE - 1)), ahead=2)

        @block.tensor
        def _(pe):
            def split_mm(o, lhs, rhs, start=True, stop=True, skip=False):
                terms = [(l, r) for l, r in zip(lhs, rhs)]
                seq = []
                for (lh, ll), (rh, rl_) in terms:
                    seq += [(lh, rh), (lh, rl_), (ll, rh)]
                for i, (l, r) in enumerate(seq):
                    ins = pe.matmul(o, l, r, start=start and i == 0, stop=stop and i == len(seq) - 1,
                                    skip_group_check=skip)
                return ins

            def setup():
                pe.wait_ge(s_const, 16 * N_CONST)
                pe.wait_ge(s_set, 1)
                pe.matmul(P["O"][0:PROJ, 0:NA], ones[:, 0:PROJ], sim_sq[:, :], start=True, stop=True)\
                    .then_inc(s_set_t, 1)
                pe.wait_ge(s_set, 5)
                for k in range(KT):
                    pe.matmul(P["O"][:, 8 * k:8 * k + NA], wp_t[:, 128 * k:128 * k + 128], sim_n[:, :],
                              start=True, stop=True)
                pe.matmul(P["O"][:, 16:16 + NA], bp_wide[:, :], sim_n[:, :], start=True, stop=True)\
                    .then_inc(s_set_t, 1)
                pe.wait_ge(s_set_a, 2)
                pe.wait_ge(s_whi, 2)
                pe.wait_ge(s_wlo, 2)
                pe.wait_ge(s_wo, 16)

            def transposes(t, name, src):
                n = T_TURNS.count(t, name)
                need(pe, s_t_hi, n)
                need(pe, s_t_lo, n)
                for k in range(KT):
                    for b in range(2):
                        ins = pe.transpose(bank_t[:, k, b, :], src[:, b, 128 * k:128 * k + 128], ident[:, :])
                ins.then_inc(s_t, 1)

            def wcols(k, c, n):
                return w_hi[:, k, c:c + n], w_lo[:, k, c:c + n]

            def feature_major(t, name, c, xh, xl):
                for m in range(2):
                    ins = split_mm(bank_j[:, m, :], [wcols(k, c + 128 * m, 128) for k in range(KT)],
                                   [(xh[:, k, :], xl[:, k, :]) for k in range(KT)])
                return ins

            def scores(p, m):
                q, b, k = p.parity, m // 2, m % 2
                cut = slice(128 * b, 128 * b + 128)
                need(pe, s_prob, p.times(4, m))
                for g in range(4):
                    ins = pe.matmul(bank_s[g // 2][:, g % 2, :, :], k_stack[q][:, g, k, cut],
                                    q_stack[q][:, :, g, k, cut], start=True, stop=True)
                ins.then_inc(s_score, 1)

            def weigh(p, m):
                q, b, k = p.parity, m // 2, m % 2
                pe.wait_ge(s_prob, p.times(4, m + 1))
                for h in range(2):
                    for g in range(4):
                        ins = pe.matmul(bank_av[32 * g:32 * g + 32, k, b, :],
                                        v_wide[q][:, b, 4 * k + g, 2 * h:2 * h + 2, :].rearrange("p a d -> p (a d)"),
                                        prob[m % PROBS][:, g, h, :], start=(h == 0), stop=(h == 1))
                ins.then_inc(s_pv, 1)

            def body(t, on):
                a, b_, c, d, e, f = (t - lag for lag in LAG.values())
                if "B" in on:
                    pe.wait_ge(s_xn["B"], b_.done(2))
                    transposes(t, "xb", xn["B"])
                if "A" in on:
                    if t.reg is None:
                        pe.wait_ge(s_first, 32)
                    pe.wait_ge(s_kv, a.done())
                    need(pe, s_moved, a.done(2, back=1))
                    pe.matmul(P["R"][:, :], decay_t[:, :], kv[a.parity][:, :, :].rearrange("p b d -> p (b d)"),
                              start=True, stop=True).then_inc(s_scan, 1)
                if "B" in on:
                    pe.wait_ge(s_t_hi, T_TURNS.count(t, "xb", 1))
                    pe.wait_ge(s_t_lo, T_TURNS.count(t, "xb", 1))
                    need(pe, s_g_free, G_TURNS.count(t, "small"))
                    for b in range(2):
                        cut = slice(128 * b, 128 * b + 128)
                        acts = [(xt_hi["B"][:, k, cut], xt_lo["B"][:, k, cut]) for k in range(KT)]
                        ins = split_mm(g_small[:, b, :], acts, [wcols(k, C_SMALL, SMALL) for k in range(KT)])
                    ins.then_inc(s_g, 1)
                if "D" in on:
                    pe.wait_ge(s_stacked[d.parity], d.dma_done(16 * STACK_DMAS))
                    pe.wait_ge(s_v_wide, d.done(2))
                    scores(d, 0)
                if "B" in on:
                    need(pe, s_x2, b_.done(back=1))
                    for b in range(2):
                        cut = slice(128 * b, 128 * b + 128)
                        acts = [(xt_hi["B"][:, k, cut], xt_lo["B"][:, k, cut]) for k in range(KT)]
                        split_mm(bank_f[:, b, :], acts, [wcols(k, C_BASE, D) for k in range(KT)],
                                 start=(b == 0), stop=False, skip=True)
                if "C" in on:
                    pe.wait_ge(s_c2[c.parity], c.dma_done())
                    transposes(t, "ctx", c_again[c.parity])
                if "D" in on:
                    scores(d, 1)
                    need(pe, s_x3, d.done(back=1))
                    weigh(d, 0)
                if "C" in on:
                    pe.wait_ge(s_t_hi, T_TURNS.count(t, "ctx", 1))
                    pe.wait_ge(s_t_lo, T_TURNS.count(t, "ctx", 1))
                    need(pe, s_v_wide, c.done(2, back=1))
                    feature_major(t, "k", C_K, ct_hi, ct_lo).then_inc(s_k, 1)
                    pe.wait_ge(s_xn["C"], c.done(2))
                    transposes(t, "xc", xn["C"])
                if "D" in on:
                    scores(d, 2)
                    weigh(d, 1)
                if "C" in on:
                    pe.wait_ge(s_t_hi, T_TURNS.count(t, "xc", 1))
                    pe.wait_ge(s_t_lo, T_TURNS.count(t, "xc", 1))
                    pe.wait_ge(s_k_hi, c.done())
                    pe.wait_ge(s_k_lo, c.done())
                    feature_major(t, "q", C_Q, xt_hi["C"], xt_lo["C"]).then_inc(s_q, 1)
                if "E" in on:
                    pe.wait_ge(s_xn["E"], e.done(2))
                    transposes(t, "xe", xn_e[e.parity][:, 0:2 * TOP:TOP, 0:D])
                if "D" in on:
                    scores(d, 3)
                    weigh(d, 2)
                if "F" in on:
                    pe.wait_ge(s_both, f.done())
                    need(pe, s_g_free, G_TURNS.count(t, "rank"))
                    pe.matmul(g_rank[:, 0, :], before_t[:, :], both[:, 0, :], start=True, stop=True)
                    pe.matmul(g_rank[:, 1, :], ones16[:, :], both[:, 0, :], start=True, stop=False)
                    pe.matmul(g_rank[:, 1, :], before_t[:, :], both[:, 1, :], start=False, stop=True)
                    pe.matmul(g_rank[:, 2, :], ones16[:, :], both[:, 0, :], start=True, stop=False)
                    pe.matmul(g_rank[:, 2, :], ones16[:, :], both[:, 1, :], start=False, stop=True).then_inc(s_g, 1)
                if "C" in on:
                    pe.wait_ge(s_q_hi, c.done())
                    pe.wait_ge(s_q_lo, c.done())
                    for b in range(2):
                        cut = slice(128 * b, 128 * b + 128)
                        ins = split_mm(bank_j[:, b, :], [(ct_hi[:, k, cut], ct_lo[:, k, cut]) for k in range(KT)],
                                       [wcols(k, C_V, D) for k in range(KT)])
                    ins.then_inc(s_v, 1)
                if "D" in on:
                    weigh(d, 3)
                if "B" in on:
                    pe.wait_ge(s_down, b_.done())
                    pe.wait_ge(s_g_free, G_TURNS.count(t, "down"))
                    for b in range(2):
                        ins = pe.transpose(g_down[:, b, :], down_parts[:, b, :], ident16[:, :])
                    ins.then_inc(s_g, 1)
                if "D" in on:
                    pe.wait_ge(s_av, d.done())
                    for b in range(2):
                        for k in range(KT):
                            ins = pe.matmul(bank_o[:, b, :], av[:, k, b, :], wo_t[:, k, :], start=(k == 0),
                                            stop=(k == KT - 1))
                    ins.then_inc(s_o, 1)
                if "B" in on:
                    pe.wait_ge(s_g_free, G_TURNS.count(t, "down", 1))
                    for b in range(2):
                        ins = pe.matmul(bank_f[:, b, :], down_t[:, b, :], wu_parts[:, :], start=False, stop=(b == 1),
                                        skip_group_check=True)
                    ins.then_inc(s_up, 1)
                if "E" in on:
                    pe.wait_ge(s_t_hi, T_TURNS.count(t, "xe", 1))
                    pe.wait_ge(s_t_lo, T_TURNS.count(t, "xe", 1))
                    need(pe, s_g_free, G_TURNS.count(t, "logits"))
                    for b in range(2):
                        cut = slice(128 * b, 128 * b + 128)
                        acts = [(xt_hi["E"][:, k, cut], xt_lo["E"][:, k, cut]) for k in range(KT)]
                        ins = split_mm(g_logits[:, b, :], acts, [wcols(k, C_ROUTER, NE) for k in range(KT)])
                    ins.then_inc(s_g, 1)

            run_bodies(pe, body, after_first=setup)

            pe.wait_ge(s_plan, PLAN_STEPS)
            pe.wait_ge(s_ew_hi, 2 * NE)
            pe.wait_ge(s_ew_lo, 2 * NE)

            def transpose_block(i):
                q = i.n % 2
                pe.wait_ge(s_xb[i.n % FAR], i.dma_done())
                if i.reg is not None or i.n >= 2:
                    pe.wait_ge(s_xb_hi, i.done(back=2))
                    pe.wait_ge(s_xb_lo, i.done(back=2))
                for k in range(KT):
                    ins = pe.transpose(xb_banks[q][:, k, :], xb[i.n % FAR][:, 128 * k:128 * k + 128], ident[:, :])
                ins.then_inc(s_xb_t, 1)

            first_hi, first_lo, second_hi, second_lo = (
                w[:, :, :, :].rearrange("p e k d -> p (e k d)") for w in (win_hi, win_lo, wout_hi, wout_lo))

            copies = []

            def copied(at):
                reg = pe.alloc_register(f"entry_copy{len(copies)}")
                copies.append(reg)
                pe.reg_mov(reg, at)
                return bass.RuntimeValue.of_register_unchecked(reg).with_bounds(min_val=at.min_val, max_val=at.max_val)

            def layer1(i, at):
                q, at = i.n % 2, copied(at)
                pe.wait_ge(s_xb_hi, i.done())
                pe.wait_ge(s_xb_lo, i.done())
                if i.reg is not None or i.n >= 2:
                    pe.wait_ge(s_gelu, i.done(KT, back=2))
                for m in range(KT):
                    ins = split_mm(hid_banks[q][:, m, :],
                                   [(first_hi[:, bass.ds(at + (D * k + 128 * m), 128)],
                                     first_lo[:, bass.ds(at + (D * k + 128 * m), 128)]) for k in range(KT)],
                                   [(xb_hi[q][:, k, :], xb_lo[q][:, k, :]) for k in range(KT)])
                ins.then_inc(s_h, 1)

            def layer2(i, at):
                q, at = i.n % 2, copied(at)
                pe.wait_ge(s_h_hi, i.done())
                pe.wait_ge(s_h_lo, i.done())
                if i.reg is not None or i.n >= 2:
                    pe.wait_ge(s_y_out, i.done(back=2))
                split_mm(y_banks[q], [(h_hi[q][:, k, :], h_lo[q][:, k, :]) for k in range(KT)],
                         [(second_hi[:, bass.ds(at + D * k, D)], second_lo[:, bass.ds(at + D * k, D)])
                          for k in range(KT)])\
                    .then_inc(s_y, 1)

            def pe_step(i, weights_at):
                if i.reg is not None or i.n + 2 < BLOCKS:
                    transpose_block(i + 2)
                if i.reg is not None or 0 <= i.n + 1 < BLOCKS:
                    layer1(i + 1, weights_at[(i.n % FAR if i.n >= 0 else i.n) + 1])
                if i.n >= 0:
                    layer2(i, weights_at[i.n % FAR])

            run_blocks(pe, pe_step, BLOCKS, plan_reader(pe, "weights_at", 0, FAR + 1, KT * D * (NE - 1)), ahead=2)

        @block.vector
        def _(dve):
            dve.memset(small_bias[:, :], 0.0).then_inc(s_zero, 1)
            dve.memset(wu_f32[:, :], 0.0).then_inc(s_zero, 1)
            dve.memset(ones[:, :], 1.0)
            dve.memset(down_parts[:, :, :], 0.0).then_inc(s_zero, 1)

            def setup():
                dve.wait_ge(s_const, 16 * N_CONST)
                dve.tensor_tensor(sim_sq[:, :], sim_t[:, :], sim_t[:, :], ALU.mult).then_inc(s_set, 1)
                dve.wait_ge(s_set_t, 1)
                dve.tensor_scalar(sim_sq[:, :], P["O"][0:PROJ, 0:NA], 1e-24, None, ALU.max).then_inc(s_set, 1)
                dve.tensor_scalar(temp_e[:, :], temp_t[:, :], CLAMP_MAX, None, ALU.min).then_inc(s_set, 1)
                dve.tensor_scalar(bp_wide[:, :], ones[:, :], bp_col[:, 0:1], None, ALU.mult).then_inc(s_set, 1)
                dve.wait_ge(s_set_p, 2)
                dve.wait_ge(s_set_a, 1)
                dve.scalar_tensor_tensor(out=sim_n[:, :], in0=sim_t[:, :], scalar=temp_e[:, 0:1],
                                         in1=sim_inv[:, :], op0=ALU.mult, op1=ALU.mult).then_inc(s_set, 1)
                dve.tensor_scalar(keep_all[:, :], mask_i[:, :], 0, None, ALU.not_equal)
                dve.tensor_copy(running[:, :], route[:, K_CAP:K_CAP + NE]).then_inc(s_run, 1)
                dve.wait_ge(s_set_t, 2)
                dve.wait_ge(s_wall, 16)
                for k in range(KT):
                    dve.tensor_copy(w_f32[:, k, C_SMALL + PROJ + RSUM:C_ROUTER], P["O"][:, 8 * k:8 * k + NA])
                dve.tensor_copy(small_bias[:, PROJ + RSUM:SMALL], P["O"][:, 16:16 + NA]).then_inc(s_set, 1)
                dve.wait_ge(s_whi, 1)
                dve.tensor_tensor(wu_parts[64:96, :], wu_f32[64:96, :], wu_parts[64:96, :], ALU.subtract)\
                    .then_inc(s_wlo, 1)
                dve.wait_ge(s_set, 6)
                dve.wait_ge(s_whi, 2)
                dve.tensor_tensor(w_lo[:, :, :], w_f32[:, :, :], w_hi[:, :, :], ALU.subtract).then_inc(s_wlo, 1)

            dve.wait_ge(s_tanh, 1)

            def statistics(k, p, src):
                q = p.parity
                for b in range(2):
                    dve.bn_stats(stats[k][:, b, :], src(b)).then_inc(s_stats[k], 1)
                need_apart(dve, s_stats[k], p.done(2), s_zero)
                for b in range(2):
                    dve.bn_aggr(mv[k][q][:, b, :], stats[k][:, b, :]).then_inc(s_aggr[k], 1)
                dve.wait_ge(s_aggr[k], p.done(2))
                dve.tensor_scalar(var[k][q][:, :], mv[k][q][:, :, 1], LN_EPS, None, ALU.add).then_inc(s_var[k], 1)

            def shifts(k, p):
                q = p.parity
                dve.wait_ge(s_rstd[k], p.done())
                dve.scalar_tensor_tensor(out=shift[k][q][:, :], in0=mv[k][q][:, :, 0], scalar=-1.0,
                                         in1=rstd[k][q][:, :], op0=ALU.mult, op1=ALU.mult).then_inc(s_shift[k], 1)

            def stored(p):
                def at(b):
                    i = p.times(2, b)
                    return xs[:, i, :] if isinstance(i, int) else xs[:, bass.ds(i, 1), :]
                return at

            def pair_of(tile, p):
                at = p.times(2)
                return tile[:, at:at + 2] if isinstance(at, int) else tile[:, bass.ds(at, 2)]

            def lo(t, name, hi_part, dst):
                n = T_TURNS.count(t, name, 1)
                dve.wait_ge(s_t_hi, n)
                dve.tensor_tensor(dst, bank_t, hi_part, ALU.subtract).then_inc(s_t_lo, 1)

            def part_lo(n, made_hi, p, made):
                q = p.parity
                dve.wait_ge(made_hi, p.done())
                dve.tensor_tensor(parts[q][:, n + 1, :, :], bank_j, parts[q][:, n, :, :], ALU.subtract)\
                    .then_inc(made, 1)

            class Chain:
                def __init__(self, s, p, per):
                    self.s, self.p, self.per, self.n = s, p, per, 0

                def link(self, ins):
                    self.n += 1
                    ins.then_inc(self.s, 1)

                def after(self):
                    dve.wait_ge(self.s, self.p.times(self.per, self.n))

                def after_apart(self):
                    need_apart(dve, self.s, self.p.times(self.per, self.n), s_zero)

            def adapter_norms(t, p):
                dve.wait_ge(s_g, G_TURNS.count(t, "small", 1))
                dve.tensor_tensor(small[:, :, :], g_small, small_bias[:, :].unsqueeze(1)
                                  .broadcast_to([128, 2, SMALL]), ALU.add).then_inc(s_small, 1)
                dve.wait_ge(s_small, p.done())
                dve.sem_inc(s_g_free, 1)
                for b in range(2):
                    dve.tensor_tensor_reduce(square[:, b, :], small[:, b, 0:PROJ], small[:, b, 0:PROJ], 1.0, 0.0,
                                             ALU.mult, ALU.add, norm2[:, b:b + 1]).then_inc(s_square, 1)
                dve.wait_ge(s_square, p.done(2))
                dve.tensor_scalar(norm2c[:, :], norm2[:, :], 1e-24, None, ALU.max).then_inc(s_norm, 1)

            def wide(tile, n):
                return tile[:, :].unsqueeze(2).broadcast_to([128, 2, n])

            def adapter_gates(p):
                ch = Chain(s_b, p, B_STEPS)
                dve.wait_ge(s_inv, p.done())
                ch.link(dve.tensor_tensor(lg[:, :, :], small[:, :, PROJ + RSUM:], wide(inv_norm, NA), ALU.mult))
                yield
                ch.after()
                ch.link(dve.tensor_reduce(lmax[:, :], lg[:, :, :], AX, ALU.max))
                yield
                ch.after()
                ch.link(dve.tensor_tensor(ldiff[:, :, :], lg[:, :, :], wide(lmax, NA), ALU.subtract))
                assert ch.n == B_DIFF
                yield
                ch.after()
                ch.link(dve.scalar_tensor_tensor(out=lcode[:, :, :], in0=ldiff[:, :, :], scalar=0.0,
                                                 in1=adapter_wt[:, :, :], op0=ALU.is_ge, op1=ALU.mult))
                yield
                ch.after()
                ch.link(dve.tensor_reduce(lwin[:, :], lcode[:, :, :], AX, ALU.max))
                yield
                ch.after()
                ch.link(dve.tensor_tensor(picked[:, :, :], adapter_id[:, :, :], wide(lwin, RSUM), ALU.is_equal))
                yield
                ch.after()
                ch.link(dve.tensor_tensor(down[:, :, :], picked[:, :, :], small[:, :, PROJ:PROJ + RSUM], ALU.mult))
                yield
                dve.wait_ge(s_lsig, p.done(2))
                ch.link(dve.reciprocal(lrec[:, :, :], lsig_n[:, :, :]))
                yield
                ch.after()
                ch.link(dve.tensor_tensor(lexp[:, :, :], lsig[:, :, :], lrec[:, :, :], ALU.mult))
                yield
                ch.after()
                ch.link(dve.tensor_reduce(lsum[:, :], lexp[:, :, :], AX, ALU.add))
                yield
                ch.after()
                ch.link(dve.reciprocal(ltop[:, :], lsum[:, :]))
                yield
                ch.after()
                ch.link(dve.tensor_tensor(down_g[:, :, :], down[:, :, :], wide(ltop, RSUM), ALU.mult))
                yield
                ch.after()
                ch.link(dve.tensor_copy(down_parts[:, :, 0:RSUM], down_g[:, :, :]))
                yield
                ch.after()
                ch.link(dve.tensor_copy(down_parts[:, :, 64:64 + RSUM], down_parts[:, :, 0:RSUM]))
                assert ch.n == B_STEPS
                yield
                ch.after()
                dve.tensor_tensor(down_parts[:, :, 32:32 + RSUM], down_g[:, :, :], down_parts[:, :, 0:RSUM],
                                  ALU.subtract).then_inc(s_down, 1)

            def ids(n):
                return route[:, K_ID:K_ID + NE].unsqueeze(1).broadcast_to([128, n, NE])

            picks4 = picks[:, :, :].rearrange("p (b k) e -> p b k e", b=2)

            def router_gates(p):
                ch = Chain(s_e, p, E_STEPS)
                need_apart(dve, s_rl, p.done(), s_zero)
                for b in range(2):
                    ch.link(dve.max(rmax[:, b, :], rl[:, b, :]))
                yield
                ch.after()
                ch.link(dve.tensor_tensor(rdiff[:, :, :], rl[:, :, :], rmax[:, :, 0:1]
                                          .broadcast_to([128, 2, NE]), ALU.subtract))
                assert ch.n == E_DIFF
                yield
                for b in range(2):
                    ch.link(dve.max_index(rindex[:, b, :], rmax[:, b, :], rl[:, b, :]))
                yield
                ch.after()
                ch.link(dve.tensor_copy(chosen[:, :, :], rindex[:, :, 0:TOP]))
                yield
                ch.after()
                ch.link(dve.tensor_tensor(picks[:, :, :], ids(2 * TOP), chosen[:, :, :]
                                          .rearrange("p b k -> p (b k)").unsqueeze(2)
                                          .broadcast_to([128, 2 * TOP, NE]), ALU.is_equal))
                yield
                ch.after()
                dve.tensor_tensor(both[:, :, :], picks4[:, :, 0, :], picks4[:, :, 1, :], ALU.add).then_inc(s_both, 1)
                yield
                dve.wait_ge(s_rsig, p.done(2))
                ch.link(dve.reciprocal(rrec[:, :, :], rsig_n[:, :, :]))
                yield
                ch.after()
                ch.link(dve.tensor_tensor(rexp[:, :, :], rsig[:, :, :], rrec[:, :, :], ALU.mult))
                yield
                ch.after()
                ch.link(dve.tensor_reduce(rsum[:, :], rexp[:, :, :], AX, ALU.add))
                yield
                ch.link(dve.tensor_tensor(pick_exp[:, :, :, :], picks4, rexp[:, :, :].unsqueeze(2)
                                          .broadcast_to([128, 2, TOP, NE]), ALU.mult))
                yield
                ch.after()
                ch.link(dve.reciprocal(rinv[:, :], rsum[:, :]))
                yield
                ch.link(dve.tensor_reduce(top_exp[:, :, :], pick_exp[:, :, :, :], AX, ALU.add))
                assert ch.n == E_STEPS
                yield
                ch.after()
                dve.tensor_tensor(pair_of(gate_all, p), top_exp[:, :, :], wide(rinv, TOP), ALU.mult)\
                    .then_inc(s_gate, 1)

            def ranks(t, p):
                ch = Chain(s_r, p, RANK_STEPS)
                if p.reg is None and p.n == 0:
                    dve.wait_ge(s_run, 1)
                need(dve, s_r, p.done(RANK_STEPS, back=1) if p.reg is not None or p.n > 0 else 0)
                dve.wait_ge(s_g, G_TURNS.count(t, "rank", 1))
                ch.link(dve.tensor_tensor(rank[:, :, :], g_rank[:, 0:2, :], running[:, :].unsqueeze(1)
                                          .broadcast_to([128, 2, NE]), ALU.add))
                yield
                ch.after()
                ch.link(dve.tensor_tensor(running[:, :], running[:, :], g_rank[:, 2, :], ALU.add))
                yield
                ch.after()
                dve.sem_inc(s_g_free, 1)
                ch.link(dve.tensor_tensor(pick_row[:, :, :, :], picks4, rank[:, :, :].unsqueeze(2)
                                          .broadcast_to([128, 2, TOP, NE]), ALU.mult))
                yield
                ch.after()
                ch.link(dve.tensor_reduce(slot[:, :, :], pick_row[:, :, :, :], AX, ALU.add))
                assert ch.n == RANK_STEPS
                yield
                need_apart(dve, s_scat[p.parity], p.dma_done(16 * 2 * TOP, back=2), s_zero)
                at = p.times(1)
                rows = y_rows[:, at:at + 1, :] if isinstance(at, int) else y_rows[:, bass.ds(at, 1), :]
                dve.tensor_copy(xn_e[p.parity][:, :, D:WIDE], rows.rearrange("p a c -> p (a c)").unsqueeze(2))
                ch.after()
                dve.tensor_copy(slot_u[p.parity][:, :], slot[:, :, :].rearrange("p b k -> p (b k)"))\
                    .then_inc(s_slot, 1)

            def in_turn(*chains):
                chains = list(chains)
                while chains:
                    chains = [c for c in chains if next(c, chains) is not chains]

            def body(t, on):
                a, b_, c, d, e, f = (t - lag for lag in LAG.values())
                if "A" in on:
                    need_apart(dve, s_x[a.parity], a.dma_done(), s_zero)
                    statistics("A", a, lambda b: x_in[a.parity][:, b, :])
                if "B" in on:
                    lo(t, "xb", xt_hi["B"][:, :, :].rearrange("p k (b s) -> p k b s", b=2),
                       xt_lo["B"][:, :, :].rearrange("p k (b s) -> p k b s", b=2))
                if "C" in on:
                    need_apart(dve, s_x2, c.done(), s_zero)
                    statistics("C", c, stored(c))
                if "E" in on:
                    need_apart(dve, s_x3, e.done(), s_zero)
                    statistics("E", e, stored(e))
                if "A" in on:
                    q = a.parity
                    dve.wait_ge(s_rstd["A"], a.done())
                    dve.tensor_scalar(ln_gain[:, :], rstd["A"][q][:, :], tanh_g[:, 0:1], None, ALU.mult)\
                        .then_inc(s_shift["A"], 1)
                    dve.wait_ge(s_scan, a.done())
                    for b in range(2):
                        dve.scalar_tensor_tensor(out=moved[:, b, :], in0=x_in[q][:, b, :],
                                                 scalar=mv["A"][q][:, b, 0:1], in1=bank_r[:, b, :],
                                                 op0=ALU.subtract, op1=ALU.mult).then_inc(s_moved, 1)
                if "C" in on:
                    shifts("C", c)
                if "E" in on:
                    shifts("E", e)
                if "A" in on:
                    dve.wait_ge(s_moved, a.done(2))
                    dve.wait_ge(s_shift["A"], a.done())
                    for b in range(2):
                        dve.scalar_tensor_tensor(out=x1[q][:, b, :], in0=moved[:, b, :], scalar=ln_gain[:, b:b + 1],
                                                 in1=x_in[q][:, b, :], op0=ALU.mult, op1=ALU.add).then_inc(s_x1, 1)
                if "B" in on:
                    adapter_norms(t, b_)
                if "C" in on:
                    lo(t, "ctx", ct_hi[:, :, :].rearrange("p k (b s) -> p k b s", b=2),
                       ct_lo[:, :, :].rearrange("p k (b s) -> p k b s", b=2))
                if "A" in on:
                    need_apart(dve, s_x1, a.done(2), s_zero)
                    statistics("B", a, lambda b: x1[a.parity][:, b, :])
                if "C" in on:
                    part_lo(0, s_k_hi, c, s_k_lo)
                    lo(t, "xc", xt_hi["C"][:, :, :].rearrange("p k (b s) -> p k b s", b=2),
                       xt_lo["C"][:, :, :].rearrange("p k (b s) -> p k b s", b=2))
                    dve.tensor_copy(keep[c.parity][:, :], pair_of(keep_all, c)).then_inc(s_keep, 1)

                def copies():
                    yield
                    yield
                    if "A" in on:
                        shifts("B", a)
                    yield
                    if "C" in on:
                        part_lo(2, s_q_hi, c, s_q_lo)
                    for _ in range(7):
                        yield
                    if "E" in on:
                        lo(t, "xe", xt_hi["E"][:, :, :].rearrange("p k (b s) -> p k b s", b=2),
                           xt_lo["E"][:, :, :].rearrange("p k (b s) -> p k b s", b=2))

                in_turn(*([adapter_gates(b_)] if "B" in on else []), *([router_gates(f)] if "F" in on else []),
                        copies())
                if "F" in on:
                    for _ in ranks(t, f):
                        pass
                if "D" in on:
                    dve.wait_ge(s_o, d.done())
                    dve.scalar_tensor_tensor(out=pair_of(xs, d), in0=bank_o, scalar=tanh_g[:, 1:2],
                                             in1=pair_of(xs, d), op0=ALU.mult, op1=ALU.add).then_inc(s_x3, 1)
                if "B" in on:
                    dve.wait_ge(s_up, b_.done())
                    dve.scalar_tensor_tensor(out=pair_of(xs, b_), in0=bank_f, scalar=tanh_g[:, 2:3],
                                             in1=x1[b_.parity][:, :, :], op0=ALU.mult, op1=ALU.add)\
                        .then_inc(s_x2, 1)
                if "E" in on:
                    dve.wait_ge(s_g, G_TURNS.count(t, "logits", 1))
                    dve.tensor_copy(rl[:, :, :], g_logits).then_inc(s_rl, 1)
                    dve.wait_ge(s_rl, e.done())
                    dve.sem_inc(s_g_free, 1)

            def matrices(t):
                for n in SPLITS.get(t, ()):
                    dve.wait_ge(s_ew_hi, n + 1)
                    dve.tensor_tensor((win_lo, wout_lo)[n % 2][:, n // 2, :, :], w_stage[n % 2][:, :, :],
                                      (win_hi, wout_hi)[n % 2][:, n // 2, :, :], ALU.subtract).then_inc(s_ew_lo, 1)

            run_bodies(dve, body, after_first=setup, beside=matrices)

            steps = 0

            def planned(ins):
                nonlocal steps
                steps += 1
                ins.then_inc(s_plan, 1)
                dve.wait_ge(s_plan, steps)

            def const(c, n):
                return route[:, c:c + n]

            def over_rows(ap, n):
                return ap.unsqueeze(1).broadcast_to([ap.shape[0], n, NE])

            dve.wait_ge(s_r, RANK_STEPS * NP)
            dve.wait_ge(s_slot, NP)
            dve.wait_ge(s_gate, NP)
            planned(dve.tensor_tensor(count[:, :], running[:, :], const(K_CAP, NE), ALU.subtract))
            planned(dve.tensor_copy(pad[:, :], const(K_PAD, NE + 1)))
            planned(dve.tensor_tensor(pad[:, 0:NE], pad[:, 0:NE], count[:, :], ALU.add))
            planned(dve.tensor_copy(pad_u[:, :], pad[:, :]))
            assert steps == PAD_STEPS
            planned(dve.tensor_tensor(over[:, :, :], const(K_THR, NE * (TOKENS // 128))
                                      .rearrange("p (e j) -> p e j", e=NE), count[:, :].unsqueeze(2)
                                      .broadcast_to([128, NE, TOKENS // 128]), ALU.is_lt))
            planned(dve.tensor_reduce(n_blocks[:, :], over[:, :, :], AX, ALU.add))
            planned(dve.tensor_tensor(ends[:, :, :], const(K_TRI, NE * NE).rearrange("p (a b) -> p a b", a=NE),
                                      over_rows(n_blocks[:, :], NE), ALU.mult))
            planned(dve.tensor_reduce(end[:, :], ends[:, :, :], AX, ALU.add))
            planned(dve.tensor_tensor(start[:, :], end[:, :], n_blocks[:, :], ALU.subtract))
            planned(dve.scalar_tensor_tensor(out=y_base[:, :], in0=start[:, :], scalar=128.0, in1=const(K_CAP, NE),
                                             op0=ALU.mult, op1=ALU.subtract))
            blocks = route[0:1, K_BLK:K_BLK + PLANNED].unsqueeze(2).broadcast_to([1, PLANNED, NE])
            planned(dve.tensor_tensor(below[:, :, :], over_rows(start[0:1, :], PLANNED), blocks, ALU.is_le))
            planned(dve.tensor_tensor(in_block[:, :, :], over_rows(end[0:1, :], PLANNED), blocks, ALU.is_gt))
            planned(dve.tensor_tensor(in_block[:, :, :], in_block[:, :, :], below[:, :, :], ALU.mult))
            planned(dve.tensor_tensor(row_part[:, :, :], in_block[:, :, :], over_rows(y_base[0:1, :], PLANNED),
                                      ALU.mult))
            planned(dve.tensor_tensor(below[:, :, :], in_block[:, :, :], over_rows(route[0:1, K_ID:K_ID + NE], PLANNED),
                                      ALU.mult))
            planned(dve.tensor_reduce(used[:, :], in_block[:, :, :], AX, ALU.add))
            planned(dve.tensor_reduce(row_sum[:, :], row_part[:, :, :], AX, ALU.add))
            planned(dve.tensor_reduce(owner[:, :], below[:, :, :], AX, ALU.add))
            planned(dve.tensor_tensor(row_f[:, :], used[:, :], route[0:1, K_ROW:K_ROW + PLANNED], ALU.mult))
            planned(dve.tensor_tensor(row_f[:, :], row_f[:, :], row_sum[:, :], ALU.subtract))
            planned(dve.tensor_scalar(row_f[:, :], row_f[:, :], float(SPARE), None, ALU.add))
            planned(dve.tensor_copy(table[:, 0, :], row_f[:, :]))
            for line, scale in (("weights_at", KT * D), ("bias_at", KT), ("out_bias_at", D)):
                planned(dve.tensor_scalar(table[:, LINES.index(line), :], owner[:, :], float(scale), None, ALU.mult))
            planned(dve.tensor_scalar(gate_all[:, :, :], gate_all[:, :, :], tanh_g[:, 3:4], None, ALU.mult))
            assert steps == PLAN_STEPS
            dve.wait_ge(s_eb, 32)

            def copy_lo(i):
                q = i.n % 2
                dve.wait_ge(s_xb_hi, i.done())
                if i.reg is not None or i.n >= 2:
                    dve.wait_ge(s_h, i.done(back=2))
                dve.tensor_tensor(xb_lo[q][:, :, :], xb_banks[q], xb_hi[q][:, :, :], ALU.subtract)\
                    .then_inc(s_xb_lo, 1)

            def hidden_lo(i):
                q = i.n % 2
                dve.wait_ge(s_h_hi, i.done())
                if i.reg is not None or i.n >= 2:
                    dve.wait_ge(s_y, i.done(back=2))
                dve.tensor_tensor(h_lo[q][:, :, :], h_f32[q][:, :, :], h_hi[q][:, :, :], ALU.subtract)\
                    .then_inc(s_h_lo, 1)

            out_biases = bout_t[:, :, :].rearrange("p e d -> p (e d)")

            def add_bias(i, at):
                n = i.n % FAR
                need_apart(dve, s_xb[n], i.dma_done(), s_plan)
                if i.reg is not None or i.n >= FAR:
                    need_apart(dve, s_y_kept[n], i.dma_done(back=FAR), s_plan)
                col = i.times(1)
                dve.tensor_tensor(y_row[n][:, :], xb[n][:, D:WIDE], left_rows[:, col:col + 1] if isinstance(col, int)
                                  else left_rows[:, bass.ds(col, 1)], ALU.max).then_inc(s_y_row, 1)
                dve.wait_ge(s_y, i.done())
                dve.tensor_tensor(y_out[i.n % FAR][:, :], y_banks[i.n % 2], out_biases[:, bass.ds(at, D)],
                                  ALU.add).then_inc(s_y_out, 1)

            def dve_step(i, out_bias_at):
                if i.reg is not None or i.n + 2 < BLOCKS:
                    copy_lo(i + 2)
                if i.reg is not None or 0 <= i.n + 1 < BLOCKS:
                    hidden_lo(i + 1)
                if i.n >= 0:
                    add_bias(i, out_bias_at[i.n % FAR])

            run_blocks(dve, dve_step, BLOCKS, plan_reader(dve, "out_bias_at", 0, FAR, D * (NE - 1)), ahead=2)

            for n in range(BATCH):
                pair, b = n // 2, n % 2
                got = y_got[pair % PICK_BUFS]
                dve.wait_ge(s_got[pair % PICK_BUFS], 16 * (pair // PICK_BUFS + 1))
                dve.scalar_tensor_tensor(out=half_sum[b][:, :], in0=got[:, b, 0:D], scalar=gate_all[:, n, 0:1],
                                         in1=xs[:, n, :], op0=ALU.mult, op1=ALU.add).then_inc(s_half, 1)
                dve.wait_ge(s_half, n + 1)
                if pair >= PICK_BUFS:
                    dve.wait_ge(s_out[pair % PICK_BUFS], 16 * (pair // PICK_BUFS))
                dve.scalar_tensor_tensor(out=result[pair % PICK_BUFS][:, b, :], in0=got[:, b, D:TOP * D],
                                         scalar=gate_all[:, n, 1:2], in1=half_sum[b][:, :], op0=ALU.mult,
                                         op1=ALU.add).then_inc(s_fin, 1)


KINDS = ("k_hi", "k_lo", "q_hi", "q_lo")
B_DIFF, B_STEPS = 3, 14
E_DIFF, E_STEPS = 3, 13
RANK_STEPS = 4
PAD_STEPS, PLAN_STEPS = 4, 26
LINES = ("row", "weights_at", "bias_at", "out_bias_at")
PICK_BUFS = 4


def kernel(**inputs):
    import numpy as np
    import concourse.bacc as bacc
    from concourse.bass_utils import run_bass_kernel_spmd as run

    a = {k: np.asarray(v) for k, v in inputs.items()}
    f = np.float32
    gap = np.zeros((D, NA), f)
    wall = np.concatenate([a["L0_ffn_W"].T, a["L1_xattn_Wk"], a["L1_xattn_Wv"], a["L1_xattn_Wq"],
                           a["L0_ffn_Wp"].T] + [a[f"L0_ffn_Wd{i}"].T for i in range(NA)] + [gap, a["L1_ffn_router_w"]],
                          axis=1)
    wu = np.concatenate([a[f"L0_ffn_Wu{i}"].T for i in range(NA)], axis=0)
    steps = np.arange(S)
    decay = np.where(steps[None, :] >= steps[:, None], 0.9 ** np.maximum(steps[None, :] - steps[:, None], 0), 0.0)
    ex = np.arange(NE)
    lanes = np.arange(128)[:, None]
    rows = [ex * CAP, (np.arange(NE + 1) * CAP)[None, :] + lanes, ex, (ex[None, :] <= ex[:, None]).ravel(),
            np.tile(128 * np.arange(TOKENS // 128), NE), np.arange(PLANNED), 128 * np.arange(PLANNED) - SPARE]
    routing = np.concatenate([np.broadcast_to(v, (128, v.shape[-1])) for v in rows], axis=1).astype(f)
    arrays = {
        "x": a["x"], "ctx": a["ctx_1024"], "mask": a["mask_BxS2_ik0"].T,
        "gates": np.stack([a["g_xattn"][0], a["g_xattn"][1], a["g_ffn"][0], a["g_ffn"][1]]),
        "temp": a["L0_ffn_temp"], "bp": a["L0_ffn_bp"], "sim": a["L0_ffn_sim"], "wall": wall, "wp": a["L0_ffn_Wp"],
        "wu": wu, "wo": a["L1_xattn_Wo"].reshape(KT, 128, D).transpose(1, 0, 2),
        "w_in": a["L1_ffn_w_in"], "b_in": a["L1_ffn_b_in"].reshape(NE, KT, 128).transpose(2, 0, 1),
        "w_out": a["L1_ffn_w_out"], "b_out": a["L1_ffn_b_out"],
        "decay": decay.astype(f), "eye": np.eye(128, dtype=f),
        "before": (steps[:, None] < steps[None, :]).astype(np.float16), "routing": routing,
        "y_rows": (LEFT + TOP * (128 * np.arange(BATCH)[None, :, None] + lanes[:, :, None]) + np.arange(TOP))
        .reshape(128, NP, 2 * TOP).astype(f),
        "left_rows": (128 * np.arange(BLOCKS)[None, :] + lanes).astype(f),
    }
    nc = bacc.Bacc("TRN2", target_bir_lowering=False, num_devices=1)
    feed, aps = {}, []
    for name, v in arrays.items():
        v = np.ascontiguousarray(v)
        feed[f"in_{name}"] = v
        aps.append(nc.dram_tensor(f"in_{name}", v.shape, mybir.dt.from_np(v.dtype), kind="ExternalInput").ap())
    o = nc.dram_tensor("out_0", (BATCH, S, D), F32, kind="ExternalOutput").ap()
    build(nc, *aps, o)
    r = run(nc, [feed], core_ids=[0])
    return r.results[0]["out_0"]
```

```python
from contextlib import ExitStack

import concourse.bass as bass
from concourse import mybir

F32 = mybir.dt.float32
F16 = mybir.dt.float16
U32 = mybir.dt.uint32
I32 = mybir.dt.int32
ALU = mybir.AluOpType
ACT = mybir.ActivationFunctionType
AX = mybir.AxisListType.X

BATCH, S, D = 32, 128, 256
KT = D // 128
NP = BATCH // 2
HEADS, HD = 16, 16
PROJ = 64
RANKS = (1, 2, 4, 8)
NA = len(RANKS)
RSUM = sum(RANKS)
SMALL = PROJ + RSUM + NA
NE = 8
PROBS = 2
TOP = 2
TOKENS = BATCH * S
CAP = TOKENS + 128
FAR = 18
BLOCKS = -(-((TOP * TOKENS + NE * 127) // 128) // FAR) * FAR
SPARES = BLOCKS - TOP * TOKENS // 128
LEFT = BLOCKS * 128
WIDE = D + 1
LN_EPS = 1e-5
CLAMP_MAX = 4.605170185988092

C_BASE, C_K, C_V, C_Q, C_SMALL = 0, 256, 512, 768, 1024
C_ROUTER = C_SMALL + SMALL
WCOLS = C_ROUTER + NE

LAG = {"A": 0, "B": 1, "C": 2, "D": 3, "E": 4, "F": 5}
BODIES = NP + LAG["F"]
LOOP_FROM, LOOP_TO = 6, NP
SPLITS = {t: (2 * i, 2 * i + 1) for i, t in enumerate([1, 2, 3, 4, 5, LOOP_TO, LOOP_TO + 1, LOOP_TO + 2])}

K_CAP, K_ID = 0, NE
K_TRI = K_ID + NE
K_THR = K_TRI + NE * NE
K_BLK = K_THR + NE * (TOKENS // 128)
KCOLS = K_BLK + BLOCKS + FAR
PLANNED = BLOCKS + FAR


class Step:

    def __init__(self, n, reg=None):
        self.n, self.reg = n, reg

    def __sub__(self, k):
        return Step(self.n - k, self.reg)

    @property
    def parity(self):
        return self.n % 2

    def times(self, k, plus=0):
        if self.reg is None:
            return self.n * k + plus
        return self.reg * (2 * k) + (self.n * k + plus)

    def done(self, per=1, back=0, short=0):
        return self.times(per, per * (1 - back) - short)

    def dma_done(self, per=16, back=0):
        half = self.n // 2 + 1 - back // 2
        return half * per if self.reg is None else self.reg * per + half * per


class Turns:

    def __init__(self, order):
        self.order = order

    def _before(self, t, name):
        n = 0
        for b in range(t + 1):
            for k, stage in self.order:
                if b == t and k == name:
                    return n
                n += 0 <= b - LAG[stage] < NP
        raise ValueError(name)

    def count(self, body, name, plus=0):
        if body.reg is None:
            return self._before(body.n, name) + plus
        k = len(self.order)
        at = self._before(LOOP_FROM, name)
        return body.times(k, at - k * LOOP_FROM + plus)


T_TURNS = Turns([("ctx", "C"), ("xc", "C"), ("xe", "E"), ("xb", "A")])
G_TURNS = Turns([("small", "B"), ("rank", "F"), ("logits", "E"), ("down", "B")])


def need(eng, sem, count):
    if not isinstance(count, int) or count > 0:
        eng.wait_ge(sem, count)


def need_apart(eng, sem, count, passed):
    if isinstance(count, int):
        need(eng, sem, count)
    else:
        count = eng.to_reg(count)
        eng.wait_ge(passed, 1)
        eng.wait_ge(sem, count)


def run_bodies(eng, body, after_first=None, loop_to=LOOP_TO, beside=None):
    def active(t):
        return {s for s, lag in LAG.items() if 0 <= t - lag < NP}

    for t in range(LOOP_FROM):
        body(Step(t), active(t))
        if t == 0 and after_first:
            after_first()
        if beside:
            beside(t)
    with eng.Fori(LOOP_FROM // 2, loop_to // 2) as u:
        for half in range(2):
            body(Step(half, u), set(LAG))
    for t in range(loop_to, BODIES):
        body(Step(t), active(t))
        if beside:
            beside(t)


class Block(Step):

    def __add__(self, k):
        return Block(self.n + k, self.reg)

    def __sub__(self, k):
        return Block(self.n - k, self.reg)

    def times(self, k, plus=0):
        if self.reg is None:
            return self.n * k + plus
        return self.reg * (FAR * k) + (self.n * k + plus)

    def dma_done(self, per=16, back=0):
        turns = self.n // FAR + 1 - back // FAR
        return turns * per if self.reg is None else self.reg * per + turns * per


def run_blocks(eng, step, last, entries, ahead=0):
    known = entries(Block(0), True)
    for n in range(-ahead, 0):
        step(Block(n), known)
    known = entries(Block(0), False, known)
    for n in range(FAR):
        step(Block(n), known)
    with eng.Fori(1, BLOCKS // FAR - 1) as u:
        known = entries(Block(0, u), False)
        for n in range(FAR):
            step(Block(n, u), known)
    known = entries(Block(BLOCKS - FAR), False)
    for n in range(BLOCKS - FAR, last):
        step(Block(n), known)


def build(nc, x, ctx, mask, gates_in, temp, bp, sim, wall, wp, wu, wo, w_in, b_in, w_out, b_out, decay, eye, before,
          routing, y_rows_in, left_rows_in, out):
    st = ExitStack()
    with st:
        def sb(name, shape, dt=F32):
            return st.enter_context(nc.sbuf_tensor(name, shape, dt))

        def bank(name, dt=F32):
            return st.enter_context(nc.psum_tensor(name, [128, 512], dt))

        def sem(name):
            return st.enter_context(nc.semaphore(name))

        ident = sb("ident", [128, 128])
        ident16 = sb("ident16", [128, 128], F16)
        decay_t = sb("decay_t", [128, 128])
        w_hi = sb("w_hi", [128, KT, WCOLS], F16)
        w_lo = sb("w_lo", [128, KT, WCOLS], F16)
        wo_t = sb("wo_t", [128, KT, D])
        wu_f32 = sb("wu_f32", [128, D])
        wu_parts = sb("wu_parts", [128, D], F16)
        small_bias = sb("small_bias", [128, SMALL])
        gates_raw = sb("gates_raw", [128, 4])
        tanh_g = sb("tanh_g", [128, 4])
        mask_i = sb("mask_i", [128, BATCH], I32)
        keep_all = sb("keep_all", [128, BATCH])
        minus_half = sb("minus_half", [128, 8])
        adapter_id = sb("adapter_id", [128, 2, RSUM])
        adapter_wt = sb("adapter_wt", [128, 2, NA])
        wp_t = sb("wp_t", [PROJ, D])
        sim_t = sb("sim_t", [PROJ, NA])
        sim_sq = sb("sim_sq", [PROJ, NA])
        sim_inv = sb("sim_inv", [PROJ, NA])
        sim_n = sb("sim_n", [PROJ, NA])
        temp_t = sb("temp_t", [PROJ, 1])
        temp_e = sb("temp_e", [PROJ, 1])
        bp_col = sb("bp_col", [PROJ, 1])
        bp_wide = sb("bp_wide", [PROJ, 128])
        ones = sb("ones", [PROJ, 128])

        xs = sb("xs", [128, BATCH, D])
        w_f32 = sb("w_f32", [128, KT, WCOLS])
        route = sb("route", [128, KCOLS])
        before_t = sb("before_t", [128, 128], F16)
        ones16 = sb("ones16", [128, 128], F16)
        gate_all = sb("gate_all", [128, BATCH, TOP])
        rdiff = sb("rdiff", [128, BATCH, NE])
        picks = sb("picks", [128, BATCH * TOP, NE])
        y_rows = sb("y_rows", [128, NP, 2 * TOP])
        left_rows = sb("left_rows", [128, BLOCKS])
        running = sb("running", [128, NE])
        zeros = sb("zeros", [128, WIDE])
        count = sb("count", [128, NE])
        n_blocks = sb("n_blocks", [128, NE])
        end = sb("end", [128, NE])
        skip = sb("skip", [128, NE])
        row_sum = sb("row_sum", [1, PLANNED])
        owner = sb("owner", [1, PLANNED])
        pad_rows = sb("pad_rows", [1, NE], I32)
        table = sb("table", [1, len(LINES), PLANNED], I32)
        bout_t = sb("bout_t", [128, NE, D])

        def two(name, shape, dt=F32):
            return [sb(f"{name}{i}", shape, dt) for i in range(2)]

        win_hi = sb("win_hi", [128, NE, KT, D], F16)
        win_lo = sb("win_lo", [128, NE, KT, D], F16)
        wout_hi = sb("wout_hi", [128, NE, KT, D], F16)
        wout_lo = sb("wout_lo", [128, NE, KT, D], F16)
        w_stage = two("w_stage", [128, KT, D])
        bin_t = sb("bin_t", [128, NE, KT])

        outer, pairs = sb, ExitStack()

        def sb(name, shape, dt=F32):
            return pairs.enter_context(nc.sbuf_tensor(name, shape, dt))

        def two(name, shape, dt=F32):
            return [pairs.enter_context(nc.sbuf_tensor(f"{name}{i}", shape, dt)) for i in range(2)]

        x_in = two("x_in", [128, 2, D])
        c_in = two("c_in", [128, 2, D])
        c_again = two("c_again", [128, 2, D])
        kv = two("kv", [128, 2, D])
        x1 = two("x1", [128, 2, D])
        moved = sb("moved", [128, 2, D])
        ln_gain = sb("ln_gain", [128, 2])
        LN = "ABCE"
        stats = {k: sb(f"stats_{k}", [128, 2, 6]) for k in LN}
        mv = {k: two(f"mv_{k}", [128, 2, 2]) for k in LN}
        var = {k: two(f"var_{k}", [128, 2]) for k in LN}
        rstd = {k: two(f"rstd_{k}", [128, 2]) for k in LN}
        shift = {k: two(f"shift_{k}", [128, 2]) for k in LN}
        xn = {k: sb(f"xn_{k}", [128, 2, D]) for k in "BC"}
        xn_e = two("xn_E", [128, 2 * TOP, WIDE])
        xt_hi = {k: sb(f"xt_hi_{k}", [128, KT, 256], F16) for k in "BCE"}
        xt_lo = {k: sb(f"xt_lo_{k}", [128, KT, 256], F16) for k in "BCE"}
        ct_hi = sb("ct_hi", [128, KT, 256], F16)
        ct_lo = sb("ct_lo", [128, KT, 256], F16)
        small = sb("small", [128, 2, SMALL])
        square = sb("square", [128, 2, PROJ])
        norm2 = sb("norm2", [128, 2])
        norm2c = sb("norm2c", [128, 2])
        inv_norm = sb("inv_norm", [128, 2])
        lg = sb("lg", [128, 2, NA])
        lmax = sb("lmax", [128, 2])
        ldiff = sb("ldiff", [128, 2, NA])
        lsig = sb("lsig", [128, 2, NA])
        lsig_n = sb("lsig_n", [128, 2, NA])
        lrec = sb("lrec", [128, 2, NA])
        lexp = sb("lexp", [128, 2, NA])
        lsum = sb("lsum", [128, 2])
        ltop = sb("ltop", [128, 2])
        lcode = sb("lcode", [128, 2, NA])
        lwin = sb("lwin", [128, 2])
        picked = sb("picked", [128, 2, RSUM])
        down = sb("down", [128, 2, RSUM])
        down_g = sb("down_g", [128, 2, RSUM])
        down_parts = sb("down_parts", [128, 2, 128], F16)
        down_t = sb("down_t", [128, 2, 128], F16)
        keep = two("keep", [128, 2])
        parts = two("parts", [128, len(KINDS), KT, 256], F16)
        k_stack = two("k_stack", [128, 4, KT, 256], F16)
        q_stack = two("q_stack", [128, 2, 4, KT, 256], F16)
        v_wide = two("v_wide", [128, 2, 8, 4, HD])
        prob = [sb(f"prob{i}", [128, 4, 2, 128]) for i in range(PROBS)]
        av = sb("av", [128, KT, 2, 128])
        rl = sb("rl", [128, 2, NE])
        rmax = sb("rmax", [128, 2, 8])
        rindex = sb("rindex", [128, 2, 8], U32)
        both = sb("both", [128, 2, NE], F16)
        chosen = sb("chosen", [128, 2, TOP])
        slot = sb("slot", [128, 2, TOP])
        rank = sb("rank", [128, 2, NE])
        pick_row = sb("pick_row", [128, 2, TOP, NE])
        slot_u = two("slot_u", [128, 2 * TOP], U32)

        pairs.close()

        def several(name, n, shape, dt=F32):
            return [outer(f"{name}{i}", shape, dt) for i in range(n)]

        over = outer("over", [128, NE, TOKENS // 128])
        passed = outer("passed", [1, PLANNED, NE])
        skipped = outer("skipped", [1, PLANNED, NE])
        rsig = outer("rsig", [128, BATCH, NE])
        rsig_n = outer("rsig_n", [128, BATCH, NE])
        rrec = outer("rrec", [128, BATCH, NE])
        rexp = outer("rexp", [128, BATCH, NE])
        rsum = outer("rsum", [128, BATCH])
        rinv = outer("rinv", [128, BATCH])
        pick_exp = outer("pick_exp", [128, BATCH, TOP, NE])
        top_exp = outer("top_exp", [128, BATCH, TOP])
        ends = outer("ends", [128, NE, NE])
        xb = several("xb", FAR, [128, WIDE])
        xb_hi = several("xb_hi", 2, [128, KT, 128], F16)
        xb_lo = several("xb_lo", 2, [128, KT, 128], F16)
        h_f32 = several("h_f32", 2, [128, KT, 128])
        h_hi = several("h_hi", 2, [128, KT, 128], F16)
        h_lo = several("h_lo", 2, [128, KT, 128], F16)
        y_out = several("y_out", FAR, [128, D])
        y_row = several("y_row", FAR, [128, 1], U32)
        y_got = several("y_got", PICK_BUFS, [128, 2, TOP * D])
        half_sum = several("half_sum", 2, [128, D])
        result = several("result", PICK_BUFS, [128, 2, D])

        names = ["R", "T", "J", "F", "G", "S0", "S1", "O"]
        P = {n: bank(f"ps_{n}") for n in names}
        bank_r = P["R"][:, :].rearrange("p (b d) -> p b d", b=2)
        bank_t = P["T"][:, :].rearrange("p (k b s) -> p k b s", k=KT, b=2)
        bank_j = P["J"][:, :].rearrange("p (k c) -> p k c", k=2)
        bank_f = P["F"][:, :].rearrange("p (b d) -> p b d", b=2)
        bank_g = P["G"]
        g_small = bank_g[:, 0:2 * SMALL].rearrange("p (b c) -> p b c", b=2)
        g_down = bank_g[:, 0:128].bitcast(F16).rearrange("p (b s) -> p b s", b=2)
        g_logits = bank_g[:, 0:2 * NE].rearrange("p (b e) -> p b e", b=2)
        bank_s = [P[f"S{i}"][:, :].rearrange("p (n h s) -> p n h s", n=2, h=2) for i in range(2)]
        bank_av = P["O"][:, :].rearrange("p (k b s) -> p k b s", k=KT, b=2)
        bank_o = P["O"][:, :].rearrange("p (b d) -> p b d", b=2)

        g_rank = bank_g[:, 0:3 * NE].rearrange("p (b e) -> p b e", b=3)

        xb_banks = [P["R"][:, 0:D].rearrange("p (k s) -> p k s", k=KT), P["T"][:, 0:D].rearrange("p (k s) -> p k s", k=KT)]
        hid_banks = [P["J"][:, 0:D].rearrange("p (k s) -> p k s", k=KT), P["F"][:, 0:D].rearrange("p (k s) -> p k s", k=KT)]
        y_banks = [P["G"][:, 0:D], P["S0"][:, 0:D]]

        s_const = sem("constants_loaded")
        s_first = sem("first_constants_loaded")
        s_wo = sem("output_weights_loaded")
        s_wall = sem("weights_loaded")
        s_wup = sem("adapter_ups_loaded")
        s_tanh = sem("gates_tanh_made")
        s_zero = sem("zeroed")
        s_iota = sem("iotas_made")
        s_set = sem("setup_vector_steps")
        s_set_p = sem("setup_pool_steps")
        s_set_t = sem("setup_products")
        s_set_a = sem("setup_scalar_steps")
        s_whi = sem("weights_hi_made")
        s_wlo = sem("weights_lo_made")
        s_x = [sem(f"x_loaded{i}") for i in range(2)]
        s_c = [sem(f"ctx_loaded{i}") for i in range(2)]
        s_c2 = [sem(f"ctx_again_loaded{i}") for i in range(2)]
        s_stats = {k: sem(f"stats_{k}_made") for k in LN}
        s_aggr = {k: sem(f"mean_{k}_made") for k in LN}
        s_var = {k: sem(f"variance_{k}_made") for k in LN}
        s_rstd = {k: sem(f"rstd_{k}_made") for k in LN}
        s_shift = {k: sem(f"shift_{k}_made") for k in LN}
        s_xn = {k: sem(f"normed_{k}") for k in "ABCE"}
        s_kv = sem("ctx_squared")
        s_scan = sem("running_sum_made")
        s_moved = sem("sum_weighted")
        s_x1 = sem("x1_made")
        s_t = sem("transposed")
        s_t_hi = sem("transposed_hi_copied")
        s_t_lo = sem("transposed_lo_copied")
        s_f = sem("base_product_made")
        s_g = sem("g_bank_written")
        s_g_free = sem("g_bank_read")
        s_small = sem("small_products_copied")
        s_rl = sem("logits_copied")
        s_square = sem("projection_squared")
        s_norm = sem("norm_clamped")
        s_inv = sem("inverse_norm_made")
        s_b = sem("adapter_gate_steps")
        s_lsig = sem("adapter_sigmoids_made")
        s_down = sem("gated_downs_split")
        s_up = sem("ups_added")
        s_x2 = sem("x2_made")
        s_keep = sem("keep_copied")
        s_k = sem("keys_made")
        s_k_hi = sem("keys_hi_copied")
        s_k_lo = sem("keys_lo_copied")
        s_v = sem("values_made")
        s_v_wide = sem("values_masked")
        s_q = sem("queries_made")
        s_q_hi = sem("queries_hi_copied")
        s_q_lo = sem("queries_lo_copied")
        s_scratch = [sem(f"parts_stored{i}") for i in range(2)]
        s_stacked = [sem(f"stacked{i}") for i in range(2)]
        s_score = sem("scores_made")
        s_prob = sem("probabilities_made")
        s_pv = sem("values_weighted")
        s_av = sem("attended_copied")
        s_o = sem("attention_projected")
        s_x3 = sem("x3_made")
        s_e = sem("router_steps")
        s_rsig = sem("router_sigmoids_made")
        s_gate = sem("gate_steps")
        s_gain = sem("gain_A_made")
        s_ew = [sem(f"expert_weights_loaded{i}") for i in range(2)]
        s_eb = sem("expert_biases_loaded")
        s_ew_hi = sem("expert_weights_hi_made")
        s_ew_lo = sem("expert_weights_lo_made")
        s_run = sem("first_rows_set")
        s_both = sem("choices_made")
        s_r = sem("rank_steps")
        s_slot = sem("slots_made")
        s_scat = [sem(f"rows_scattered{i}") for i in range(2)]
        s_plan = sem("plan_steps")
        s_pad = sem("padding_zeroed")
        s_spare = sem("spare_rows_zeroed")
        s_xb = [sem(f"block_loaded{i}") for i in range(FAR)]
        s_xb_t = sem("block_transposed")
        s_xb_hi = sem("block_hi_copied")
        s_xb_lo = sem("block_lo_copied")
        s_h = sem("hidden_product_made")
        s_gelu = sem("gelu_made")
        s_h_hi = sem("hidden_hi_made")
        s_h_lo = sem("hidden_lo_made")
        s_y = sem("expert_product_made")
        s_y_row = sem("output_rows_taken")
        s_y_out = sem("expert_output_made")
        s_y_kept = [sem(f"expert_output_scattered{i}") for i in range(FAR)]
        s_got = [sem(f"outputs_loaded{i}") for i in range(PICK_BUFS)]
        s_half = sem("first_choice_added")
        s_fin = sem("output_made")
        s_out = [sem(f"output_stored{i}") for i in range(PICK_BUFS)]

        STACK_DMAS = 4 + 8
        N_CONST = 10
        N_IOTA = 2 * NA + 1 + 4

        scratch = [nc.dram_tensor(f"parts_scratch{i}", (len(KINDS), 128, KT * 256), F16, kind="Internal").ap()
                   for i in range(2)]

        store_x = nc.dram_tensor("store_x", (NE * CAP + SPARES * 128, WIDE), F32, kind="Internal").ap()
        store_y = nc.dram_tensor("store_y", (LEFT + TOP * TOKENS, D), F32, kind="Internal").ap()

        block = st.enter_context(nc.Block())

        def plan_reader(eng, line, shift, n, top):
            row_at, calls = LINES.index(line), []

            def entries(i, before, known=None):
                if known is not None and shift == 0:
                    return known
                at = i.times(1, 0 if before else shift)
                regs = [eng.alloc_register(f"{line}{len(calls)}_{k}") for k in range(n)]
                calls.append(regs)
                eng.reg_load(regs, table[0:1, row_at, at:at + n] if isinstance(at, int)
                             else table[0:1, row_at, bass.ds(at, n)])
                return [bass.RuntimeValue.of_register_unchecked(x).with_bounds(min_val=0, max_val=top) for x in regs]
            return entries

        @block.sync
        def _(sp):
            def pair_rows(t, pair):
                at = pair.times(2)
                return t[at:at + 2] if isinstance(at, int) else t[bass.ds(at, 2)]

            def load_a(p):
                q = p.parity
                need_apart(sp, s_x1, p.done(2, back=2), s_zero)
                sp.dma_start(x_in[q][:, :, :], pair_rows(x, p).rearrange("b s d -> s b d")).then_inc(s_x[q], 16)
                need_apart(sp, s_kv, p.done(back=2), s_zero)
                sp.dma_start(c_in[q][:, :, :], pair_rows(ctx, p).rearrange("b s d -> s b d")).then_inc(s_c[q], 16)

            def load_c(p):
                q = p.parity
                need_apart(sp, s_k, p.done(back=2), s_zero)
                sp.dma_start(c_again[q][:, :, :],
                             pair_rows(ctx, p).rearrange("b s d -> s b d")).then_inc(s_c2[q], 16)

            def stack_keys(p):
                q = p.parity
                need_apart(sp, s_stacked[q], p.dma_done(16 * STACK_DMAS, back=2), s_zero)
                sp.wait_ge(s_k_hi, p.done())
                sp.wait_ge(s_k_lo, p.done())
                sp.dma_start(scratch[q][0:2].rearrange("n p c -> p n c"),
                             parts[q][:, 0:2, :, :].rearrange("p n k c -> p n (k c)")).then_inc(s_scratch[q], 16)
                need_apart(sp, s_score, p.done(4, back=2), s_zero)
                sp.wait_ge(s_scratch[q], p.dma_done(32) - 16)
                for c in range(4):
                    sp.dma_start(k_stack[q][32 * c:32 * c + 32, :, :, :].rearrange("r g k c -> r g (k c)"),
                                 scratch[q][c % 2].rearrange("(g r) c -> r g c", g=4)).then_inc(s_stacked[q], 16)

            def stack_queries(p, meanwhile):
                q = p.parity
                sp.wait_ge(s_q_hi, p.done())
                sp.wait_ge(s_q_lo, p.done())
                sp.dma_start(scratch[q][2:4].rearrange("n p c -> p n c"),
                             parts[q][:, 2:4, :, :].rearrange("p n k c -> p n (k c)")).then_inc(s_scratch[q], 16)
                meanwhile()
                sp.wait_ge(s_scratch[q], p.dma_done(32))
                for c in range(4):
                    for h in range(2):
                        at = 32 * c + HD * h
                        sp.dma_start(q_stack[q][at:at + HD, h, :, :, :].rearrange("r g k c -> r g (k c)"),
                                     scratch[q][2 + c // 2].rearrange("(g h r) c -> h r g c", g=4, h=2)[h])\
                            .then_inc(s_stacked[q], 16)

            load_a(Step(0))

            def load(sem_, dst, src):
                sp.dma_start(dst[tuple(slice(None) for _ in dst.shape)], src).then_inc(sem_, 16)

            load(s_first, decay_t, decay)
            load(s_first, ident, eye)
            load(s_first, gates_raw, gates_in.partition_broadcast(128))
            load(s_const, sim_t, sim)
            load(s_const, temp_t, temp.partition_broadcast(PROJ))
            load(s_const, bp_col, bp.rearrange("(p a) -> p a", a=1))
            load(s_const, wp_t, wp)
            sp.dma_start(w_f32[:, :, :], wall.rearrange("(k p) c -> p k c", p=128)).then_inc(s_wall, 16)
            load(s_const, mask_i, mask)
            load(s_const, route, routing)
            load(s_const, before_t, before)
            load(s_const, y_rows, y_rows_in)
            load(s_const, left_rows, left_rows_in)
            sp.wait_ge(s_zero, 4)
            sp.dma_start(small_bias[:, 0:PROJ], bp.partition_broadcast(128)).then_inc(s_const, 16)
            for i in range(3):
                sp.dma_start(wu_f32[32 * i:32 * i + RSUM, :], wu).then_inc(s_wup, 16)
            load(s_wo, wo_t, wo)

            def body(t, on):
                nxt = t - (-1)

                def loads():
                    if nxt.reg is not None or nxt.n < NP:
                        load_a(nxt)
                    c_next = nxt - LAG["C"]
                    if c_next.reg is not None or 0 <= c_next.n < NP:
                        load_c(c_next)

                if "C" in on:
                    stack_keys(t - LAG["C"])
                    stack_queries(t - LAG["C"], loads)
                else:
                    loads()

            def matrices(t):
                for n in SPLITS.get(t, ()):
                    src = (w_in, w_out)[n % 2]
                    if n >= 2:
                        sp.wait_ge(s_ew_hi, n - 1)
                        sp.wait_ge(s_ew_lo, n - 1)
                    sp.dma_start(w_stage[n % 2][:, :, :], src[n // 2].rearrange("(k p) c -> p k c", p=128))\
                        .then_inc(s_ew[n % 2], 16)

            for i in range(SPARES):
                sp.dma_start(store_x[NE * CAP + 128 * i:NE * CAP + 128 * i + 128, :], zeros[:, :])\
                    .then_inc(s_spare, 16)
            for t in range(LOOP_FROM):
                matrices(t)
                body(Step(t), {s for s, lag in LAG.items() if 0 <= t - lag < NP})
            sp.dma_start(bin_t[:, :, :], b_in).then_inc(s_eb, 16)
            sp.dma_start(bout_t[:, :, :], b_out.partition_broadcast(128)).then_inc(s_eb, 16)
            with sp.Fori(LOOP_FROM // 2, LOOP_TO // 2 - 1) as u:
                for half in range(2):
                    body(Step(half, u), set(LAG))
            for t in range(LOOP_TO - 2, BODIES):
                matrices(t)
                body(Step(t), {s for s, lag in LAG.items() if 0 <= t - lag < NP})

            sp.wait_ge(s_plan, PAD_STEPS)
            ends_at = [sp.alloc_register(f"end_of_expert{e}") for e in range(NE)]
            sp.reg_load(ends_at, pad_rows[0:1, 0:NE])
            for e in range(NE):
                at = bass.RuntimeValue.of_register_unchecked(ends_at[e])\
                    .with_bounds(min_val=e * CAP, max_val=e * CAP + TOKENS)
                sp.dma_start(store_x[bass.ds(at, 128), :], zeros[:, :]).then_inc(s_pad, 16)
            for i in range(2):
                sp.wait_ge(s_scat[i], 16 * 2 * TOP * NP // 2)
            sp.wait_ge(s_pad, 16 * NE)
            sp.wait_ge(s_spare, 16 * SPARES)
            sp.wait_ge(s_plan, PLAN_STEPS)

            def load_block(i, at):
                if i.reg is not None or i.n >= FAR:
                    need_apart(sp, s_xb_t, i.done(back=FAR), s_zero)
                    need_apart(sp, s_y_row, i.done(back=FAR), s_zero)
                sp.dma_start(xb[i.n % FAR][:, :], store_x[bass.ds(at, 128), :]).then_inc(s_xb[i.n % FAR], 16)

            def sp_step(i, rows):
                if i.reg is not None or i.n + FAR - 1 < BLOCKS:
                    load_block(i + (FAR - 1), rows[(i.n + FAR - 1 if i.n < 0 else i.n) % FAR])
            run_blocks(sp, sp_step, BLOCKS, plan_reader(sp, "row", FAR - 1, FAR, NE * CAP + (SPARES - 1) * 128), ahead=FAR - 1)

            for i in range(FAR):
                sp.wait_ge(s_y_kept[i], 16 * BLOCKS // FAR)
            for n in range(NP + PICK_BUFS - 1):
                if n < NP:
                    if n >= PICK_BUFS:
                        sp.wait_ge(s_fin, 2 * (n - PICK_BUFS + 1))
                    at = LEFT + 2 * n * TOP * 128
                    sp.dma_start(y_got[n % PICK_BUFS][:, :, :], store_y[at:at + 2 * TOP * 128]
                                 .rearrange("(b s k) d -> s b (k d)", b=2, k=TOP)).then_inc(s_got[n % PICK_BUFS], 16)
                m = n - (PICK_BUFS - 1)
                if m >= 0:
                    sp.wait_ge(s_fin, 2 * m + 2)
                    sp.dma_start(out[2 * m:2 * m + 2].rearrange("b s d -> s b d"), result[m % PICK_BUFS][:, :, :])\
                        .then_inc(s_out[m % PICK_BUFS], 16)
            for i in range(PICK_BUFS):
                sp.wait_ge(s_out[i], 16 * NP // PICK_BUFS)

        @block.gpsimd
        def _(pool):
            pool.memset(minus_half[:, :], -0.5).then_inc(s_set_p, 1)
            at = 0
            for a, r in enumerate(RANKS):
                pool.memset(adapter_id[:, :, at:at + r], float(NA - a)).then_inc(s_iota, 1)
                pool.memset(adapter_wt[:, :, a:a + 1], float(NA - a)).then_inc(s_iota, 1)
                at += r
            pool.memset(ones16[:, :], 1.0).then_inc(s_iota, 1)
            for q in range(2):
                pool.memset(q_stack[q][:, :, :, :, :], 0.0).then_inc(s_iota, 1)
                pool.memset(v_wide[q][:, :, :, :, :], 0.0).then_inc(s_iota, 1)
            pool.wait_ge(s_set_p, 1)

            def setup():
                pool.wait_ge(s_set, 2)
                pool.tensor_tensor(sim_inv[:, :], sim_sq[:, :], minus_half[0:PROJ, 0:NA], ALU.pow)\
                    .then_inc(s_set_p, 1)

            def inverse_root(k, p):
                q = p.parity
                pool.wait_ge(s_var[k], p.done())
                pool.tensor_tensor(rstd[k][q][:, :], var[k][q][:, :], minus_half[:, 0:2], ALU.pow)\
                    .then_inc(s_rstd[k], 1)

            def squared(p):
                q = p.parity
                pool.wait_ge(s_c[q], p.dma_done())
                need(pool, s_scan, p.done(back=2))
                pool.tensor_tensor(kv[q][:, :, :], c_in[q][:, :, :], c_in[q][:, :, :], ALU.mult).then_inc(s_kv, 1)

            def scatter(p):
                q = p.parity
                need_apart(pool, s_slot, p.done(), s_zero)
                for b in range(2):
                    for k in range(TOP):
                        at = b * TOP + k
                        pool.indirect_dma_start(store_x, bass.IndirectOffsetOnAxis(slot_u[q][:, at:at + 1], 0),
                                                xn_e[q][:, at, :], None).then_inc(s_scat[q], 16)

            squared(Step(0))

            def body(t, on):
                if "C" in on:
                    inverse_root("C", t - LAG["C"])
                if "B" in on:
                    p = t - LAG["B"]
                    pool.wait_ge(s_norm, p.done())
                    pool.tensor_tensor(inv_norm[:, :], norm2c[:, :], minus_half[:, 0:2], ALU.pow).then_inc(s_inv, 1)
                if "A" in on:
                    inverse_root("A", t - LAG["A"])
                if "E" in on:
                    inverse_root("E", t - LAG["E"])
                if "A" in on:
                    p = t - LAG["A"]
                    q = p.parity
                    pool.wait_ge(s_moved, p.done(2))
                    for b in range(2):
                        pool.tensor_tensor(x1[q][:, b, :], moved[:, b, :], x_in[q][:, b, :], ALU.add).then_inc(s_x1, 1)
                if "A" in on:
                    inverse_root("B", t - LAG["A"])
                nxt = t - (-1)
                if nxt.reg is not None or nxt.n < NP:
                    squared(nxt)
                if "F" in on:
                    scatter(t - LAG["F"])

            run_bodies(pool, body, after_first=setup, loop_to=LOOP_TO - 2)

            def scatter_block(i, _):
                need_apart(pool, s_y_out, i.done(), s_plan)
                pool.indirect_dma_start(store_y, bass.IndirectOffsetOnAxis(y_row[i.n % FAR][:, :], 0),
                                        y_out[i.n % FAR][:, :], None).then_inc(s_y_kept[i.n % FAR], 16)

            run_blocks(pool, scatter_block, BLOCKS, lambda i, before, known=None: None)

        @block.scalar
        def _(act):
            act.wait_ge(s_first, 48)
            act.activation(tanh_g[:, :], gates_raw[:, :], ACT.Tanh).then_inc(s_tanh, 1)

            def setup():
                act.wait_ge(s_set, 3)
                act.activation(temp_e[:, :], temp_e[:, :], ACT.Exp).then_inc(s_set_a, 1)
                act.wait_ge(s_const, 16 * N_CONST)
                act.activation(ident16[:, :], ident[:, :], ACT.Copy).then_inc(s_set_a, 1)
                act.wait_ge(s_wup, 48)
                act.wait_ge(s_zero, 2)
                act.activation(wu_parts[:, :], wu_f32[:, :], ACT.Copy).then_inc(s_whi, 1)
                act.wait_ge(s_set, 5 + 1)
                act.activation(w_hi[:, :, :], w_f32[:, :, :], ACT.Copy).then_inc(s_whi, 1)

            def hi(t, name, dst):
                act.wait_ge(s_t, T_TURNS.count(t, name, 1))
                act.activation(dst, bank_t, ACT.Copy).then_inc(s_t_hi, 1)

            def normed(k, p, src, read, dst=None):
                q = p.parity
                dst = dst or (lambda b: xn[k][:, b, :])
                need(act, s_t, read)
                act.wait_ge(s_shift[k], p.done())
                for b in range(2):
                    act.activation(dst(b), src(b), ACT.Identity, bias=shift[k][q][:, b:b + 1],
                                   scale=rstd[k][q][:, b:b + 1]).then_inc(s_xn[k], 1)

            def stored(p):
                def at(b):
                    i = p.times(2, b)
                    return xs[:, i, :] if isinstance(i, int) else xs[:, bass.ds(i, 1), :]
                return at

            def sigmoids(p, m):
                act.wait_ge(s_score, p.times(4, m + 1))
                need(act, s_pv, p.times(4, m + 1 - PROBS))
                for n in range(2):
                    ins = act.activation(prob[m % PROBS][:, 2 * n:2 * n + 2, :, :], bank_s[n], ACT.Sigmoid,
                                         scale=float(HD) ** -0.5)
                ins.then_inc(s_prob, 1)

            def part_hi(dst, ready, p, made):
                q = p.parity
                act.wait_ge(ready, p.done())
                need(act, s_scratch[q], p.dma_done(32, back=2))
                act.activation(parts[q][:, dst, :, :], bank_j, ACT.Copy).then_inc(made, 1)

            def body(t, on):
                a, b_, c, d, e, f = (t - lag for lag in LAG.values())
                if "C" in on:
                    hi(t, "ctx", ct_hi[:, :, :].rearrange("p k (b s) -> p k b s", b=2))
                if "D" in on:
                    sigmoids(d, 0)
                if "C" in on:
                    normed("C", c, stored(c), T_TURNS.count(t - 1, "xc", 1)
                           if t.reg is not None or t.n > LAG["C"] else 0)
                if "C" in on:
                    part_hi(0, s_k, c, s_k_hi)
                if "D" in on:
                    sigmoids(d, 1)
                if "C" in on:
                    hi(t, "xc", xt_hi["C"][:, :, :].rearrange("p k (b s) -> p k b s", b=2))
                if "A" in on:
                    q = a.parity
                    act.wait_ge(s_shift["A"], a.done())
                    need(act, s_x2, a.done(back=2))
                    for b in range(2):
                        act.activation(x1[q][:, b, :], x_in[q][:, b, :], ACT.Identity, bias=shift["A"][q][:, b:b + 1],
                                       scale=ln_gain[:, b:b + 1]).then_inc(s_xn["A"], 1)
                if "D" in on:
                    sigmoids(d, 2)
                if "B" in on:
                    act.wait_ge(s_b, b_.times(B_STEPS, B_DIFF))
                    act.activation(lsig[:, :, :], ldiff[:, :, :], ACT.Sigmoid).then_inc(s_lsig, 1)
                    act.activation(lsig_n[:, :, :], ldiff[:, :, :], ACT.Sigmoid, scale=-1.0).then_inc(s_lsig, 1)
                if "E" in on:
                    need(act, s_scat[e.parity], e.dma_done(16 * 2 * TOP, back=2))
                    normed("E", e, lambda b: stored(e)(b).rearrange("p a d -> p (a d)").unsqueeze(1)
                           .broadcast_to([128, TOP, D]) if e.reg is not None else
                           stored(e)(b).unsqueeze(1).broadcast_to([128, TOP, D]), T_TURNS.count(t - 1, "xe", 1)
                           if t.reg is not None or t.n > LAG["E"] else 0,
                           lambda b: xn_e[e.parity][:, TOP * b:TOP * b + TOP, 0:D])
                if "C" in on:
                    part_hi(2, s_q, c, s_q_hi)
                if "E" in on:
                    hi(t, "xe", xt_hi["E"][:, :, :].rearrange("p k (b s) -> p k b s", b=2))
                if "D" in on:
                    sigmoids(d, 3)
                if "D" in on:
                    act.wait_ge(s_pv, d.done(4))
                    need(act, s_o, d.done(back=1))
                    act.activation(av[:, :, :, :], bank_av, ACT.Copy).then_inc(s_av, 1)
                if "B" in on:
                    act.wait_ge(s_g, G_TURNS.count(t, "down", 1))
                    act.activation(down_t[:, :, :], g_down, ACT.Copy).then_inc(s_g_free, 1)
                if "A" in on:
                    normed("B", a, lambda b: x1[a.parity][:, b, :], T_TURNS.count(t - 1, "xb", 1)
                           if t.reg is not None or t.n > 0 else 0)
                if "C" in on:
                    q = c.parity
                    act.wait_ge(s_v, c.done())
                    act.wait_ge(s_keep, c.done())
                    need(act, s_pv, c.done(4, back=2))
                    if t.reg is None:
                        act.wait_ge(s_iota, N_IOTA)
                    for b in range(2):
                        act.activation(v_wide[q][:, b, :, 0:4:3, :],
                                       bank_j[:, b, :].rearrange("p (n h d) -> p n h d", n=8, h=2),
                                       ACT.Copy, scale=keep[q][:, b:b + 1]).then_inc(s_v_wide, 1)
                if "A" in on:
                    need(act, s_f, a.done(back=1))
                    hi(t, "xb", xt_hi["B"][:, :, :].rearrange("p k (b s) -> p k b s", b=2))
            def matrices(t):
                for n in SPLITS.get(t, ()):
                    act.wait_ge(s_ew[n % 2], 16 * (n // 2 + 1))
                    act.activation((win_hi, wout_hi)[n % 2][:, n // 2, :, :], w_stage[n % 2][:, :, :], ACT.Copy)\
                        .then_inc(s_ew_hi, 1)

            run_bodies(act, body, after_first=setup, beside=matrices)

            act.wait_ge(s_e, E_STEPS * NP)
            act.activation(rsig[:, :, :], rdiff[:, :, :], ACT.Sigmoid).then_inc(s_rsig, 1)
            act.activation(rsig_n[:, :, :], rdiff[:, :, :], ACT.Sigmoid, scale=-1.0).then_inc(s_rsig, 1)

            act.wait_ge(s_eb, 32)
            act.wait_ge(s_plan, PLAN_STEPS)

            def copy_hi(i):
                q = i.n % 2
                act.wait_ge(s_xb_t, i.done())
                if i.reg is not None or i.n >= 2:
                    act.wait_ge(s_h, i.done(back=2))
                act.activation(xb_hi[q][:, :, :], xb_banks[q], ACT.Copy).then_inc(s_xb_hi, 1)

            biases = bin_t[:, :, :].rearrange("p e m -> p (e m)")

            def gelu(i, at):
                q = i.n % 2
                if i.reg is not None or i.n >= 2:
                    need_apart(act, s_h_lo, i.done(back=2), s_tanh)
                need_apart(act, s_h, i.done(), s_tanh)
                for m in range(KT):
                    act.activation(h_f32[q][:, m, :], hid_banks[q][:, m, :], ACT.Gelu_apprx_tanh,
                                   bias=biases[:, bass.ds(at + m, 1)]).then_inc(s_gelu, 1)
                act.wait_ge(s_gelu, i.done(KT))
                if i.reg is not None or i.n >= 2:
                    act.wait_ge(s_y, i.done(back=2))
                act.activation(h_hi[q][:, :, :], h_f32[q][:, :, :], ACT.Copy).then_inc(s_h_hi, 1)

            def act_step(i, bias_at):
                if i.reg is not None or i.n + 2 < BLOCKS:
                    copy_hi(i + 2)
                if i.reg is not None or 0 <= i.n + 1 < BLOCKS:
                    gelu(i + 1, bias_at[(i.n % FAR if i.n >= 0 else i.n) + 1])

            run_blocks(act, act_step, BLOCKS - 1,
                       plan_reader(act, "bias_at", 0, FAR + 1, KT * (NE - 1)), ahead=2)

        @block.tensor
        def _(pe):
            def split_mm(o, lhs, rhs, start=True, stop=True, skip=False):
                terms = [(l, r) for l, r in zip(lhs, rhs)]
                seq = []
                for (lh, ll), (rh, rl_) in terms:
                    seq += [(lh, rh), (lh, rl_), (ll, rh)]
                for i, (l, r) in enumerate(seq):
                    ins = pe.matmul(o, l, r, start=start and i == 0, stop=stop and i == len(seq) - 1,
                                    skip_group_check=skip)
                return ins

            def setup():
                pe.wait_ge(s_const, 16 * N_CONST)
                pe.wait_ge(s_set, 1)
                pe.matmul(P["O"][0:PROJ, 0:NA], ones[:, 0:PROJ], sim_sq[:, :], start=True, stop=True)\
                    .then_inc(s_set_t, 1)
                pe.wait_ge(s_set, 5)
                for k in range(KT):
                    pe.matmul(P["O"][:, 8 * k:8 * k + NA], wp_t[:, 128 * k:128 * k + 128], sim_n[:, :],
                              start=True, stop=True)
                pe.matmul(P["O"][:, 16:16 + NA], bp_wide[:, :], sim_n[:, :], start=True, stop=True)\
                    .then_inc(s_set_t, 1)
                pe.wait_ge(s_set_a, 2)
                pe.wait_ge(s_whi, 2)
                pe.wait_ge(s_wlo, 2)
                pe.wait_ge(s_wo, 16)

            def transposes(t, name, src):
                n = T_TURNS.count(t, name)
                need(pe, s_t_hi, n)
                need(pe, s_t_lo, n)
                for k in range(KT):
                    for b in range(2):
                        ins = pe.transpose(bank_t[:, k, b, :], src[:, b, 128 * k:128 * k + 128], ident[:, :])
                ins.then_inc(s_t, 1)

            def wcols(k, c, n):
                return w_hi[:, k, c:c + n], w_lo[:, k, c:c + n]

            def feature_major(t, name, c, xh, xl):
                for m in range(2):
                    ins = split_mm(bank_j[:, m, :], [wcols(k, c + 128 * m, 128) for k in range(KT)],
                                   [(xh[:, k, :], xl[:, k, :]) for k in range(KT)])
                return ins

            def scores(p, m):
                q, b, k = p.parity, m // 2, m % 2
                cut = slice(128 * b, 128 * b + 128)
                need(pe, s_prob, p.times(4, m))
                for g in range(4):
                    ins = pe.matmul(bank_s[g // 2][:, g % 2, :, :], k_stack[q][:, g, k, cut],
                                    q_stack[q][:, :, g, k, cut], start=True, stop=True)
                ins.then_inc(s_score, 1)

            def weigh(p, m):
                q, b, k = p.parity, m // 2, m % 2
                pe.wait_ge(s_prob, p.times(4, m + 1))
                for h in range(2):
                    for g in range(4):
                        ins = pe.matmul(bank_av[32 * g:32 * g + 32, k, b, :],
                                        v_wide[q][:, b, 4 * k + g, 2 * h:2 * h + 2, :].rearrange("p a d -> p (a d)"),
                                        prob[m % PROBS][:, g, h, :], start=(h == 0), stop=(h == 1))
                ins.then_inc(s_pv, 1)

            def body(t, on):
                a, b_, c, d, e, f = (t - lag for lag in LAG.values())
                if "A" in on:
                    if t.reg is None:
                        pe.wait_ge(s_first, 48)
                    pe.wait_ge(s_kv, a.done())
                    need(pe, s_moved, a.done(2, back=1))
                    pe.matmul(P["R"][:, :], decay_t[:, :], kv[a.parity][:, :, :].rearrange("p b d -> p (b d)"),
                              start=True, stop=True).then_inc(s_scan, 1)
                if "B" in on:
                    pe.wait_ge(s_t_hi, T_TURNS.count(t - 1, "xb", 1))
                    pe.wait_ge(s_t_lo, T_TURNS.count(t - 1, "xb", 1))
                    need(pe, s_g_free, G_TURNS.count(t, "small"))
                    for b in range(2):
                        cut = slice(128 * b, 128 * b + 128)
                        acts = [(xt_hi["B"][:, k, cut], xt_lo["B"][:, k, cut]) for k in range(KT)]
                        ins = split_mm(g_small[:, b, :], acts, [wcols(k, C_SMALL, SMALL) for k in range(KT)])
                    ins.then_inc(s_g, 1)
                if "C" in on:
                    pe.wait_ge(s_c2[c.parity], c.dma_done())
                    transposes(t, "ctx", c_again[c.parity])
                if "B" in on:
                    need(pe, s_x2, b_.done(back=1))
                    for b in range(2):
                        cut = slice(128 * b, 128 * b + 128)
                        acts = [(xt_hi["B"][:, k, cut], xt_lo["B"][:, k, cut]) for k in range(KT)]
                        ins = split_mm(bank_f[:, b, :], acts, [wcols(k, C_BASE, D) for k in range(KT)],
                                       start=(b == 0), stop=False, skip=True)
                    ins.then_inc(s_f, 1)
                if "D" in on:
                    pe.wait_ge(s_stacked[d.parity], d.dma_done(16 * STACK_DMAS))
                    pe.wait_ge(s_v_wide, d.done(2))
                    scores(d, 0)
                if "C" in on:
                    pe.wait_ge(s_t_hi, T_TURNS.count(t, "ctx", 1))
                    pe.wait_ge(s_t_lo, T_TURNS.count(t, "ctx", 1))
                    need(pe, s_v_wide, c.done(2, back=1))
                    feature_major(t, "k", C_K, ct_hi, ct_lo).then_inc(s_k, 1)
                if "F" in on:
                    pe.wait_ge(s_both, f.done())
                    need(pe, s_g_free, G_TURNS.count(t, "rank"))
                    pe.matmul(g_rank[:, 0, :], before_t[:, :], both[:, 0, :], start=True, stop=True)
                    pe.matmul(g_rank[:, 1, :], ones16[:, :], both[:, 0, :], start=True, stop=False)
                    pe.matmul(g_rank[:, 1, :], before_t[:, :], both[:, 1, :], start=False, stop=True)
                    pe.matmul(g_rank[:, 2, :], ones16[:, :], both[:, 0, :], start=True, stop=False)
                    pe.matmul(g_rank[:, 2, :], ones16[:, :], both[:, 1, :], start=False, stop=True).then_inc(s_g, 1)
                if "D" in on:
                    scores(d, 1)
                    need(pe, s_x3, d.done(back=1))
                    weigh(d, 0)
                if "C" in on:
                    pe.wait_ge(s_xn["C"], c.done(2))
                    transposes(t, "xc", xn["C"])
                if "D" in on:
                    scores(d, 2)
                    weigh(d, 1)
                if "C" in on:
                    pe.wait_ge(s_t_hi, T_TURNS.count(t, "xc", 1))
                    pe.wait_ge(s_t_lo, T_TURNS.count(t, "xc", 1))
                    pe.wait_ge(s_k_hi, c.done())
                    pe.wait_ge(s_k_lo, c.done())
                    feature_major(t, "q", C_Q, xt_hi["C"], xt_lo["C"]).then_inc(s_q, 1)
                if "E" in on:
                    pe.wait_ge(s_xn["E"], e.done(2))
                    transposes(t, "xe", xn_e[e.parity][:, 0:2 * TOP:TOP, 0:D])
                if "D" in on:
                    scores(d, 3)
                    weigh(d, 2)
                if "C" in on:
                    pe.wait_ge(s_q_hi, c.done())
                    pe.wait_ge(s_q_lo, c.done())
                    for b in range(2):
                        cut = slice(128 * b, 128 * b + 128)
                        ins = split_mm(bank_j[:, b, :], [(ct_hi[:, k, cut], ct_lo[:, k, cut]) for k in range(KT)],
                                       [wcols(k, C_V, D) for k in range(KT)])
                    ins.then_inc(s_v, 1)
                if "E" in on:
                    pe.wait_ge(s_t_hi, T_TURNS.count(t, "xe", 1))
                    pe.wait_ge(s_t_lo, T_TURNS.count(t, "xe", 1))
                    need(pe, s_g_free, G_TURNS.count(t, "logits"))
                    for b in range(2):
                        cut = slice(128 * b, 128 * b + 128)
                        acts = [(xt_hi["E"][:, k, cut], xt_lo["E"][:, k, cut]) for k in range(KT)]
                        ins = split_mm(g_logits[:, b, :], acts, [wcols(k, C_ROUTER, NE) for k in range(KT)])
                    ins.then_inc(s_g, 1)
                if "D" in on:
                    weigh(d, 3)
                if "B" in on:
                    pe.wait_ge(s_down, b_.done())
                    pe.wait_ge(s_g_free, G_TURNS.count(t, "down"))
                    for b in range(2):
                        ins = pe.transpose(g_down[:, b, :], down_parts[:, b, :], ident16[:, :])
                    ins.then_inc(s_g, 1)
                if "D" in on:
                    pe.wait_ge(s_av, d.done())
                    for b in range(2):
                        for k in range(KT):
                            ins = pe.matmul(bank_o[:, b, :], av[:, k, b, :], wo_t[:, k, :], start=(k == 0),
                                            stop=(k == KT - 1))
                    ins.then_inc(s_o, 1)
                if "B" in on:
                    pe.wait_ge(s_g_free, G_TURNS.count(t, "down", 1))
                    for b in range(2):
                        ins = pe.matmul(bank_f[:, b, :], down_t[:, b, :], wu_parts[:, :], start=False, stop=(b == 1),
                                        skip_group_check=True)
                    ins.then_inc(s_up, 1)
                if "A" in on:
                    pe.wait_ge(s_xn["B"], a.done(2))
                    transposes(t, "xb", xn["B"])
            run_bodies(pe, body, after_first=setup)

            pe.wait_ge(s_plan, PLAN_STEPS)
            pe.wait_ge(s_ew_hi, 2 * NE)
            pe.wait_ge(s_ew_lo, 2 * NE)

            def transpose_block(i):
                q = i.n % 2
                pe.wait_ge(s_xb[i.n % FAR], i.dma_done())
                if i.reg is not None or i.n >= 2:
                    pe.wait_ge(s_xb_lo, i.done(back=2))
                for k in range(KT):
                    ins = pe.transpose(xb_banks[q][:, k, :], xb[i.n % FAR][:, 128 * k:128 * k + 128], ident[:, :])
                ins.then_inc(s_xb_t, 1)

            first_hi, first_lo, second_hi, second_lo = (
                w[:, :, :, :].rearrange("p e k d -> p (e k d)") for w in (win_hi, win_lo, wout_hi, wout_lo))

            copies = []

            def copied(at):
                reg = pe.alloc_register(f"entry_copy{len(copies)}")
                copies.append(reg)
                pe.reg_mov(reg, at)
                return bass.RuntimeValue.of_register_unchecked(reg).with_bounds(min_val=at.min_val, max_val=at.max_val)

            def layer1(i, at):
                q, at = i.n % 2, copied(at)
                pe.wait_ge(s_xb_lo, i.done())
                if i.reg is not None or i.n >= 2:
                    pe.wait_ge(s_gelu, i.done(KT, back=2))
                for m in range(KT):
                    ins = split_mm(hid_banks[q][:, m, :],
                                   [(first_hi[:, bass.ds(at + (D * k + 128 * m), 128)],
                                     first_lo[:, bass.ds(at + (D * k + 128 * m), 128)]) for k in range(KT)],
                                   [(xb_hi[q][:, k, :], xb_lo[q][:, k, :]) for k in range(KT)])
                ins.then_inc(s_h, 1)

            def layer2(i, at):
                q, at = i.n % 2, copied(at)
                pe.wait_ge(s_h_lo, i.done())
                if i.reg is not None or i.n >= 2:
                    pe.wait_ge(s_y_out, i.done(back=2))
                split_mm(y_banks[q], [(h_hi[q][:, k, :], h_lo[q][:, k, :]) for k in range(KT)],
                         [(second_hi[:, bass.ds(at + D * k, D)], second_lo[:, bass.ds(at + D * k, D)])
                          for k in range(KT)])\
                    .then_inc(s_y, 1)

            def pe_step(i, weights_at):
                if i.reg is not None or i.n + 2 < BLOCKS:
                    transpose_block(i + 2)
                if i.reg is not None or 0 <= i.n + 1 < BLOCKS:
                    layer1(i + 1, weights_at[(i.n % FAR if i.n >= 0 else i.n) + 1])
                if i.n >= 0:
                    layer2(i, weights_at[i.n % FAR])

            run_blocks(pe, pe_step, BLOCKS, plan_reader(pe, "weights_at", 0, FAR + 1, KT * D * (NE - 1)), ahead=2)

        @block.vector
        def _(dve):
            dve.memset(small_bias[:, :], 0.0).then_inc(s_zero, 1)
            dve.memset(wu_f32[:, :], 0.0).then_inc(s_zero, 1)
            dve.memset(ones[:, :], 1.0)
            dve.memset(down_parts[:, :, :], 0.0).then_inc(s_zero, 1)
            dve.memset(zeros[:, :], 0.0).then_inc(s_zero, 1)

            def setup():
                dve.wait_ge(s_const, 16 * N_CONST)
                dve.tensor_tensor(sim_sq[:, :], sim_t[:, :], sim_t[:, :], ALU.mult).then_inc(s_set, 1)
                dve.wait_ge(s_set_t, 1)
                dve.tensor_scalar(sim_sq[:, :], P["O"][0:PROJ, 0:NA], 1e-24, None, ALU.max).then_inc(s_set, 1)
                dve.tensor_scalar(temp_e[:, :], temp_t[:, :], CLAMP_MAX, None, ALU.min).then_inc(s_set, 1)
                dve.tensor_scalar(bp_wide[:, :], ones[:, :], bp_col[:, 0:1], None, ALU.mult).then_inc(s_set, 1)
                dve.wait_ge(s_set_p, 2)
                dve.wait_ge(s_set_a, 1)
                dve.scalar_tensor_tensor(out=sim_n[:, :], in0=sim_t[:, :], scalar=temp_e[:, 0:1],
                                         in1=sim_inv[:, :], op0=ALU.mult, op1=ALU.mult).then_inc(s_set, 1)
                dve.tensor_scalar(keep_all[:, :], mask_i[:, :], 0, None, ALU.not_equal)
                dve.tensor_copy(running[:, :], route[:, K_CAP:K_CAP + NE]).then_inc(s_run, 1)
                dve.wait_ge(s_set_t, 2)
                dve.wait_ge(s_wall, 16)
                for k in range(KT):
                    dve.tensor_copy(w_f32[:, k, C_SMALL + PROJ + RSUM:C_ROUTER], P["O"][:, 8 * k:8 * k + NA])
                dve.tensor_copy(small_bias[:, PROJ + RSUM:SMALL], P["O"][:, 16:16 + NA]).then_inc(s_set, 1)
                dve.wait_ge(s_whi, 1)
                dve.tensor_tensor(wu_parts[64:96, :], wu_f32[64:96, :], wu_parts[64:96, :], ALU.subtract)\
                    .then_inc(s_wlo, 1)
                dve.wait_ge(s_set, 6)
                dve.wait_ge(s_whi, 2)
                dve.tensor_tensor(w_lo[:, :, :], w_f32[:, :, :], w_hi[:, :, :], ALU.subtract).then_inc(s_wlo, 1)

            dve.wait_ge(s_tanh, 1)

            def statistics(k, p, src):
                q = p.parity
                for b in range(2):
                    dve.bn_stats(stats[k][:, b, :], src(b)).then_inc(s_stats[k], 1)
                yield
                need_apart(dve, s_stats[k], p.done(2), s_zero)
                for b in range(2):
                    dve.bn_aggr(mv[k][q][:, b, :], stats[k][:, b, :]).then_inc(s_aggr[k], 1)
                yield
                dve.wait_ge(s_aggr[k], p.done(2))
                dve.tensor_scalar(var[k][q][:, :], mv[k][q][:, :, 1], LN_EPS, None, ALU.add).then_inc(s_var[k], 1)

            def shifts(k, p):
                q = p.parity
                dve.wait_ge(s_rstd[k], p.done())
                dve.scalar_tensor_tensor(out=shift[k][q][:, :], in0=mv[k][q][:, :, 0], scalar=-1.0,
                                         in1=rstd[k][q][:, :], op0=ALU.mult, op1=ALU.mult).then_inc(s_shift[k], 1)

            def wait_shift(k, p):
                yield
                shifts(k, p)

            def stored(p):
                def at(b):
                    i = p.times(2, b)
                    return xs[:, i, :] if isinstance(i, int) else xs[:, bass.ds(i, 1), :]
                return at

            def pair_of(tile, p):
                at = p.times(2)
                return tile[:, at:at + 2] if isinstance(at, int) else tile[:, bass.ds(at, 2)]

            def lo(t, name, hi_part, dst):
                n = T_TURNS.count(t, name, 1)
                dve.wait_ge(s_t_hi, n)
                dve.tensor_tensor(dst, bank_t, hi_part, ALU.subtract).then_inc(s_t_lo, 1)

            def part_lo(n, made_hi, p, made):
                q = p.parity
                dve.wait_ge(made_hi, p.done())
                dve.tensor_tensor(parts[q][:, n + 1, :, :], bank_j, parts[q][:, n, :, :], ALU.subtract)\
                    .then_inc(made, 1)

            class Chain:
                def __init__(self, s, p, per):
                    self.s, self.p, self.per, self.n = s, p, per, 0

                def link(self, ins):
                    self.n += 1
                    ins.then_inc(self.s, 1)

                def after(self):
                    dve.wait_ge(self.s, self.p.times(self.per, self.n))

                def after_apart(self):
                    need_apart(dve, self.s, self.p.times(self.per, self.n), s_zero)

            def adapter_norms(t, p):
                dve.wait_ge(s_g, G_TURNS.count(t, "small", 1))
                dve.tensor_tensor(small[:, :, :], g_small, small_bias[:, :].unsqueeze(1)
                                  .broadcast_to([128, 2, SMALL]), ALU.add).then_inc(s_small, 1)
                yield
                dve.wait_ge(s_small, p.done())
                dve.sem_inc(s_g_free, 1)
                for b in range(2):
                    dve.tensor_tensor_reduce(square[:, b, :], small[:, b, 0:PROJ], small[:, b, 0:PROJ], 1.0, 0.0,
                                             ALU.mult, ALU.add, norm2[:, b:b + 1]).then_inc(s_square, 1)
                yield
                dve.wait_ge(s_square, p.done(2))
                dve.tensor_scalar(norm2c[:, :], norm2[:, :], 1e-24, None, ALU.max).then_inc(s_norm, 1)

            def wide(tile, n):
                return tile[:, :].unsqueeze(2).broadcast_to([128, 2, n])

            def adapter_gates(p):
                ch = Chain(s_b, p, B_STEPS)
                dve.wait_ge(s_inv, p.done())
                ch.link(dve.tensor_tensor(lg[:, :, :], small[:, :, PROJ + RSUM:], wide(inv_norm, NA), ALU.mult))
                yield
                ch.after()
                ch.link(dve.tensor_reduce(lmax[:, :], lg[:, :, :], AX, ALU.max))
                yield
                ch.after()
                ch.link(dve.tensor_tensor(ldiff[:, :, :], lg[:, :, :], wide(lmax, NA), ALU.subtract))
                assert ch.n == B_DIFF
                yield
                ch.after()
                ch.link(dve.scalar_tensor_tensor(out=lcode[:, :, :], in0=ldiff[:, :, :], scalar=0.0,
                                                 in1=adapter_wt[:, :, :], op0=ALU.is_ge, op1=ALU.mult))
                yield
                ch.after()
                ch.link(dve.tensor_reduce(lwin[:, :], lcode[:, :, :], AX, ALU.max))
                yield
                ch.after()
                ch.link(dve.tensor_tensor(picked[:, :, :], adapter_id[:, :, :], wide(lwin, RSUM), ALU.is_equal))
                yield
                ch.after()
                ch.link(dve.tensor_tensor(down[:, :, :], picked[:, :, :], small[:, :, PROJ:PROJ + RSUM], ALU.mult))
                yield
                dve.wait_ge(s_lsig, p.done(2))
                ch.link(dve.reciprocal(lrec[:, :, :], lsig_n[:, :, :]))
                yield
                ch.after()
                ch.link(dve.tensor_tensor(lexp[:, :, :], lsig[:, :, :], lrec[:, :, :], ALU.mult))
                yield
                ch.after()
                ch.link(dve.tensor_reduce(lsum[:, :], lexp[:, :, :], AX, ALU.add))
                yield
                ch.after()
                ch.link(dve.reciprocal(ltop[:, :], lsum[:, :]))
                yield
                ch.after()
                ch.link(dve.tensor_tensor(down_g[:, :, :], down[:, :, :], wide(ltop, RSUM), ALU.mult))
                yield
                ch.after()
                ch.link(dve.tensor_copy(down_parts[:, :, 0:RSUM], down_g[:, :, :]))
                yield
                ch.after()
                ch.link(dve.tensor_copy(down_parts[:, :, 64:64 + RSUM], down_parts[:, :, 0:RSUM]))
                assert ch.n == B_STEPS
                yield
                ch.after()
                dve.tensor_tensor(down_parts[:, :, 32:32 + RSUM], down_g[:, :, :], down_parts[:, :, 0:RSUM],
                                  ALU.subtract).then_inc(s_down, 1)

            def ids(n):
                return route[:, K_ID:K_ID + NE].unsqueeze(1).broadcast_to([128, n, NE])

            def picks_of(p):
                at = p.times(2 * TOP)
                return picks[:, at:at + 2 * TOP, :] if isinstance(at, int) else picks[:, bass.ds(at, 2 * TOP), :]

            def router_choices(p, ch):
                need_apart(dve, s_rl, p.done(), s_zero)
                for b in range(2):
                    ch.link(dve.max(rmax[:, b, :], rl[:, b, :]))
                yield
                ch.after()
                ch.link(dve.tensor_tensor(pair_of(rdiff, p), rl[:, :, :], rmax[:, :, 0:1]
                                          .broadcast_to([128, 2, NE]), ALU.subtract))
                yield
                for b in range(2):
                    ch.link(dve.max_index(rindex[:, b, :], rmax[:, b, :], rl[:, b, :]))
                yield
                ch.after()
                ch.link(dve.tensor_copy(chosen[:, :, :], rindex[:, :, 0:TOP]))
                yield
                ch.after()
                ch.link(dve.tensor_tensor(picks_of(p), ids(2 * TOP), chosen[:, :, :]
                                          .rearrange("p b k -> p (b k)").unsqueeze(2)
                                          .broadcast_to([128, 2 * TOP, NE]), ALU.is_equal))
                yield
                ch.after()
                assert ch.n == E_STEPS
                picks4 = picks_of(p).rearrange("p (b k) e -> p b k e", b=2)
                dve.tensor_tensor(both[:, :, :], picks4[:, :, 0, :], picks4[:, :, 1, :], ALU.add).then_inc(s_both, 1)

            def ranks(t, p):
                ch = Chain(s_r, p, RANK_STEPS)
                if p.reg is None and p.n == 0:
                    dve.wait_ge(s_run, 1)
                need(dve, s_r, p.done(RANK_STEPS, back=1) if p.reg is not None or p.n > 0 else 0)
                dve.wait_ge(s_g, G_TURNS.count(t, "rank", 1))
                ch.link(dve.tensor_tensor(rank[:, :, :], g_rank[:, 0:2, :], running[:, :].unsqueeze(1)
                                          .broadcast_to([128, 2, NE]), ALU.add))
                yield
                ch.after()
                ch.link(dve.tensor_tensor(running[:, :], running[:, :], g_rank[:, 2, :], ALU.add))
                yield
                ch.after()
                dve.sem_inc(s_g_free, 1)
                ch.link(dve.tensor_tensor(pick_row[:, :, :, :], picks_of(p)
                                          .rearrange("p (b k) e -> p b k e", b=2), rank[:, :, :].unsqueeze(2)
                                          .broadcast_to([128, 2, TOP, NE]), ALU.mult))
                yield
                ch.after()
                ch.link(dve.tensor_reduce(slot[:, :, :], pick_row[:, :, :, :], AX, ALU.add))
                assert ch.n == RANK_STEPS
                yield
                need_apart(dve, s_scat[p.parity], p.dma_done(16 * 2 * TOP, back=2), s_zero)
                at = p.times(1)
                rows = y_rows[:, at:at + 1, :] if isinstance(at, int) else y_rows[:, bass.ds(at, 1), :]
                dve.tensor_copy(xn_e[p.parity][:, :, D:WIDE], rows.rearrange("p a c -> p (a c)").unsqueeze(2))
                ch.after()
                dve.tensor_copy(slot_u[p.parity][:, :], slot[:, :, :].rearrange("p b k -> p (b k)"))\
                    .then_inc(s_slot, 1)

            def in_turn(*chains):
                chains = list(chains)
                while chains:
                    chains = [c for c in chains if next(c, chains) is not chains]

            def body(t, on):
                a, b_, c, d, e, f = (t - lag for lag in LAG.values())
                def gain():
                    dve.wait_ge(s_rstd["A"], a.done())
                    dve.tensor_scalar(ln_gain[:, :], rstd["A"][a.parity][:, :], tanh_g[:, 0:1], None, ALU.mult)\
                        .then_inc(s_gain, 1)
                    yield
                    dve.wait_ge(s_gain, a.done())
                    dve.scalar_tensor_tensor(out=shift["A"][a.parity][:, :], in0=mv["A"][a.parity][:, :, 0],
                                             scalar=-1.0, in1=ln_gain[:, :], op0=ALU.mult, op1=ALU.mult)\
                        .then_inc(s_shift["A"], 1)

                def stored_statistics(k, p, made):
                    need_apart(dve, made, p.done(), s_zero)
                    yield from statistics(k, p, stored(p))

                def loaded_statistics():
                    need_apart(dve, s_x[a.parity], a.dma_done(), s_zero)
                    yield from statistics("A", a, lambda b: x_in[a.parity][:, b, :])

                def context_lo():
                    for _ in range(3):
                        yield
                    lo(t, "ctx", ct_hi[:, :, :].rearrange("p k (b s) -> p k b s", b=2),
                       ct_lo[:, :, :].rearrange("p k (b s) -> p k b s", b=2))

                router = Chain(s_e, f, E_STEPS)
                in_turn(*([stored_statistics("C", c, s_x2)] if "C" in on else []),
                        *([router_choices(f, router)] if "F" in on else []),
                        *([context_lo()] if "C" in on else []))
                in_turn(*([loaded_statistics()] if "A" in on else []), *([adapter_norms(t, b_)] if "B" in on else []),
                        *([wait_shift("C", c)] if "C" in on else []))
                in_turn(*([stored_statistics("E", e, s_x3)] if "E" in on else []), *([gain()] if "A" in on else []))
                if "C" in on:
                    dve.tensor_copy(keep[c.parity][:, :], pair_of(keep_all, c)).then_inc(s_keep, 1)

                def moves():
                    dve.wait_ge(s_scan, a.done())
                    dve.wait_ge(s_xn["A"], a.done(2))
                    need(dve, s_x1, a.done(2, back=1))
                    for b in range(2):
                        dve.tensor_tensor(moved[:, b, :], x1[a.parity][:, b, :], bank_r[:, b, :], ALU.mult)\
                            .then_inc(s_moved, 1)

                def next_statistics():
                    need_apart(dve, s_x1, a.done(2), s_zero)
                    yield from statistics("B", a, lambda b: x1[a.parity][:, b, :])
                    yield
                    yield
                    shifts("B", a)

                def between():
                    if "C" in on:
                        part_lo(0, s_k_hi, c, s_k_lo)
                    yield
                    if "E" in on:
                        shifts("E", e)
                    yield
                    if "C" in on:
                        lo(t, "xc", xt_hi["C"][:, :, :].rearrange("p k (b s) -> p k b s", b=2),
                           xt_lo["C"][:, :, :].rearrange("p k (b s) -> p k b s", b=2))
                    yield
                    yield
                    yield
                    if "A" in on:
                        moves()

                in_turn(*([ranks(t, f)] if "F" in on else []), *([adapter_gates(b_)] if "B" in on else []),
                        between())

                def copies():
                    if "C" in on:
                        part_lo(2, s_q_hi, c, s_q_lo)
                    yield
                    yield
                    if "E" in on:
                        lo(t, "xe", xt_hi["E"][:, :, :].rearrange("p k (b s) -> p k b s", b=2),
                           xt_lo["E"][:, :, :].rearrange("p k (b s) -> p k b s", b=2))

                in_turn(copies(), *([next_statistics()] if "A" in on else []))
                if "E" in on:
                    dve.wait_ge(s_g, G_TURNS.count(t, "logits", 1))
                    dve.tensor_copy(rl[:, :, :], g_logits).then_inc(s_rl, 1)
                    dve.wait_ge(s_rl, e.done())
                    dve.sem_inc(s_g_free, 1)
                if "D" in on:
                    dve.wait_ge(s_o, d.done())
                    dve.scalar_tensor_tensor(out=pair_of(xs, d), in0=bank_o, scalar=tanh_g[:, 1:2],
                                             in1=pair_of(xs, d), op0=ALU.mult, op1=ALU.add).then_inc(s_x3, 1)
                if "B" in on:
                    dve.wait_ge(s_up, b_.done())
                    dve.scalar_tensor_tensor(out=pair_of(xs, b_), in0=bank_f, scalar=tanh_g[:, 2:3],
                                             in1=x1[b_.parity][:, :, :], op0=ALU.mult, op1=ALU.add)\
                        .then_inc(s_x2, 1)
                if "A" in on:
                    need(dve, s_f, a.done(back=1))
                    lo(t, "xb", xt_hi["B"][:, :, :].rearrange("p k (b s) -> p k b s", b=2),
                       xt_lo["B"][:, :, :].rearrange("p k (b s) -> p k b s", b=2))

            def matrices(t):
                for n in SPLITS.get(t, ()):
                    dve.wait_ge(s_ew_hi, n + 1)
                    dve.tensor_tensor((win_lo, wout_lo)[n % 2][:, n // 2, :, :], w_stage[n % 2][:, :, :],
                                      (win_hi, wout_hi)[n % 2][:, n // 2, :, :], ALU.subtract).then_inc(s_ew_lo, 1)

            run_bodies(dve, body, after_first=setup, beside=matrices)

            steps = 0

            def planned(ins):
                nonlocal steps
                steps += 1
                ins.then_inc(s_plan, 1)
                dve.wait_ge(s_plan, steps)

            def const(c, n):
                return route[:, c:c + n]

            def over_rows(ap, n):
                return ap.unsqueeze(1).broadcast_to([ap.shape[0], n, NE])

            dve.wait_ge(s_r, RANK_STEPS * NP)
            dve.wait_ge(s_slot, NP)
            planned(dve.tensor_copy(pad_rows[:, :], running[0:1, :]))
            assert steps == PAD_STEPS
            planned(dve.tensor_tensor(count[:, :], running[:, :], const(K_CAP, NE), ALU.subtract))
            planned(dve.tensor_tensor(over[:, :, :], const(K_THR, NE * (TOKENS // 128))
                                      .rearrange("p (e j) -> p e j", e=NE), count[:, :].unsqueeze(2)
                                      .broadcast_to([128, NE, TOKENS // 128]), ALU.is_lt))
            planned(dve.tensor_reduce(n_blocks[:, :], over[:, :, :], AX, ALU.add))
            planned(dve.tensor_tensor(ends[:, :, :], const(K_TRI, NE * NE).rearrange("p (a b) -> p a b", a=NE),
                                      over_rows(n_blocks[:, :], NE), ALU.mult))
            planned(dve.tensor_reduce(end[:, :], ends[:, :, :], AX, ALU.add))
            planned(dve.tensor_scalar(skip[:, :], n_blocks[:, :], -128.0, float(CAP), ALU.mult, ALU.add))
            blocks = route[0:1, K_BLK:K_BLK + PLANNED].unsqueeze(2).broadcast_to([1, PLANNED, NE])
            planned(dve.tensor_tensor(passed[:, :, :], over_rows(end[0:1, :], PLANNED), blocks, ALU.is_le))
            planned(dve.tensor_tensor(skipped[:, :, :], passed[:, :, :], over_rows(skip[0:1, :], PLANNED), ALU.mult))
            planned(dve.tensor_reduce(row_sum[:, :], skipped[:, :, :], AX, ALU.add))
            planned(dve.tensor_reduce(owner[:, :], passed[:, :, :], AX, ALU.add))
            planned(dve.scalar_tensor_tensor(out=table[:, 0, :], in0=route[0:1, K_BLK:K_BLK + PLANNED], scalar=128.0,
                                             in1=row_sum[:, :], op0=ALU.mult, op1=ALU.add))
            planned(dve.tensor_scalar(owner[:, :], owner[:, :], float(NE - 1), None, ALU.min))
            for line, scale in (("weights_at", KT * D), ("bias_at", KT), ("out_bias_at", D)):
                planned(dve.tensor_scalar(table[:, LINES.index(line), :], owner[:, :], float(scale), None, ALU.mult))
            assert steps == PLAN_STEPS

            dve.wait_ge(s_rsig, 2)
            dve.reciprocal(rrec[:, :, :], rsig_n[:, :, :]).then_inc(s_gate, 1)
            dve.wait_ge(s_gate, 1)
            dve.tensor_tensor(rexp[:, :, :], rsig[:, :, :], rrec[:, :, :], ALU.mult).then_inc(s_gate, 1)
            dve.wait_ge(s_gate, 2)
            dve.tensor_reduce(rsum[:, :], rexp[:, :, :], AX, ALU.add).then_inc(s_gate, 1)
            dve.tensor_tensor(pick_exp[:, :, :, :], picks[:, :, :].rearrange("p (b k) e -> p b k e", k=TOP),
                              rexp[:, :, :].unsqueeze(2).broadcast_to([128, BATCH, TOP, NE]), ALU.mult)\
                .then_inc(s_gate, 1)
            dve.wait_ge(s_gate, 4)
            dve.reciprocal(rinv[:, :], rsum[:, :]).then_inc(s_gate, 1)
            dve.tensor_reduce(top_exp[:, :, :], pick_exp[:, :, :, :], AX, ALU.add).then_inc(s_gate, 1)
            dve.wait_ge(s_gate, 6)
            dve.tensor_tensor(gate_all[:, :, :], top_exp[:, :, :], rinv[:, :].unsqueeze(2)
                              .broadcast_to([128, BATCH, TOP]), ALU.mult).then_inc(s_gate, 1)
            dve.wait_ge(s_gate, 7)
            dve.tensor_scalar(gate_all[:, :, :], gate_all[:, :, :], tanh_g[:, 3:4], None, ALU.mult).then_inc(s_gate, 1)
            dve.wait_ge(s_eb, 32)

            def copy_lo(i):
                q = i.n % 2
                dve.wait_ge(s_xb_hi, i.done())
                if i.reg is not None or i.n >= 2:
                    dve.wait_ge(s_h, i.done(back=2))
                dve.tensor_tensor(xb_lo[q][:, :, :], xb_banks[q], xb_hi[q][:, :, :], ALU.subtract)\
                    .then_inc(s_xb_lo, 1)

            def take_rows(i):
                n, col = i.n % FAR, i.times(1)
                need_apart(dve, s_xb[n], i.dma_done(), s_plan)
                if i.reg is not None or i.n >= FAR:
                    need_apart(dve, s_y_kept[n], i.dma_done(back=FAR), s_plan)
                dve.tensor_tensor(y_row[n][:, :], xb[n][:, D:WIDE], left_rows[:, col:col + 1] if isinstance(col, int)
                                  else left_rows[:, bass.ds(col, 1)], ALU.max).then_inc(s_y_row, 1)

            def hidden_lo(i):
                q = i.n % 2
                dve.wait_ge(s_h_hi, i.done())
                if i.reg is not None or i.n >= 2:
                    dve.wait_ge(s_y, i.done(back=2))
                dve.tensor_tensor(h_lo[q][:, :, :], h_f32[q][:, :, :], h_hi[q][:, :, :], ALU.subtract)\
                    .then_inc(s_h_lo, 1)

            out_biases = bout_t[:, :, :].rearrange("p e d -> p (e d)")

            def add_bias(i, at):
                n = i.n % FAR
                if i.reg is not None or i.n >= FAR:
                    need_apart(dve, s_y_kept[n], i.dma_done(back=FAR), s_plan)
                dve.wait_ge(s_y, i.done())
                dve.tensor_tensor(y_out[i.n % FAR][:, :], y_banks[i.n % 2], out_biases[:, bass.ds(at, D)],
                                  ALU.add).then_inc(s_y_out, 1)

            def dve_step(i, out_bias_at):
                if i.reg is not None or i.n + 2 < BLOCKS:
                    copy_lo(i + 2)
                    take_rows(i + 2)
                if i.reg is not None or 0 <= i.n + 1 < BLOCKS:
                    hidden_lo(i + 1)
                if i.n >= 0:
                    add_bias(i, out_bias_at[i.n % FAR])

            run_blocks(dve, dve_step, BLOCKS, plan_reader(dve, "out_bias_at", 0, FAR, D * (NE - 1)), ahead=2)

            dve.wait_ge(s_gate, 8)
            for n in range(BATCH):
                pair, b = n // 2, n % 2
                got = y_got[pair % PICK_BUFS]
                dve.wait_ge(s_got[pair % PICK_BUFS], 16 * (pair // PICK_BUFS + 1))
                dve.scalar_tensor_tensor(out=half_sum[b][:, :], in0=got[:, b, 0:D], scalar=gate_all[:, n, 0:1],
                                         in1=xs[:, n, :], op0=ALU.mult, op1=ALU.add).then_inc(s_half, 1)
                dve.wait_ge(s_half, n + 1)
                if pair >= PICK_BUFS:
                    dve.wait_ge(s_out[pair % PICK_BUFS], 16 * (pair // PICK_BUFS))
                dve.scalar_tensor_tensor(out=result[pair % PICK_BUFS][:, b, :], in0=got[:, b, D:TOP * D],
                                         scalar=gate_all[:, n, 1:2], in1=half_sum[b][:, :], op0=ALU.mult,
                                         op1=ALU.add).then_inc(s_fin, 1)


KINDS = ("k_hi", "k_lo", "q_hi", "q_lo")
B_DIFF, B_STEPS = 3, 14
E_STEPS = 7
RANK_STEPS = 4
PAD_STEPS, PLAN_STEPS = 1, 16
LINES = ("row", "weights_at", "bias_at", "out_bias_at")
PICK_BUFS = 4


def kernel(**inputs):
    import numpy as np
    import concourse.bacc as bacc
    from concourse.bass_utils import run_bass_kernel_spmd as run

    a = {k: np.asarray(v) for k, v in inputs.items()}
    f = np.float32
    gap = np.zeros((D, NA), f)
    wall = np.concatenate([a["L0_ffn_W"].T, a["L1_xattn_Wk"], a["L1_xattn_Wv"], a["L1_xattn_Wq"],
                           a["L0_ffn_Wp"].T] + [a[f"L0_ffn_Wd{i}"].T for i in range(NA)] + [gap, a["L1_ffn_router_w"]],
                          axis=1)
    wu = np.concatenate([a[f"L0_ffn_Wu{i}"].T for i in range(NA)], axis=0)
    steps = np.arange(S)
    decay = np.where(steps[None, :] >= steps[:, None], 0.9 ** np.maximum(steps[None, :] - steps[:, None], 0), 0.0)
    ex = np.arange(NE)
    lanes = np.arange(128)[:, None]
    rows = [ex * CAP, ex, (ex[None, :] <= ex[:, None]).ravel(),
            np.tile(128 * np.arange(TOKENS // 128), NE), np.arange(PLANNED)]
    routing = np.concatenate([np.broadcast_to(v, (128, v.shape[-1])) for v in rows], axis=1).astype(f)
    arrays = {
        "x": a["x"], "ctx": a["ctx_1024"], "mask": a["mask_BxS2_ik0"].T,
        "gates": np.stack([a["g_xattn"][0], a["g_xattn"][1], a["g_ffn"][0], a["g_ffn"][1]]),
        "temp": a["L0_ffn_temp"], "bp": a["L0_ffn_bp"], "sim": a["L0_ffn_sim"], "wall": wall, "wp": a["L0_ffn_Wp"],
        "wu": wu, "wo": a["L1_xattn_Wo"].reshape(KT, 128, D).transpose(1, 0, 2),
        "w_in": a["L1_ffn_w_in"], "b_in": a["L1_ffn_b_in"].reshape(NE, KT, 128).transpose(2, 0, 1),
        "w_out": a["L1_ffn_w_out"], "b_out": a["L1_ffn_b_out"],
        "decay": decay.astype(f), "eye": np.eye(128, dtype=f),
        "before": (steps[:, None] < steps[None, :]).astype(np.float16), "routing": routing,
        "y_rows": (LEFT + TOP * (128 * np.arange(BATCH)[None, :, None] + lanes[:, :, None]) + np.arange(TOP))
        .reshape(128, NP, 2 * TOP).astype(f),
        "left_rows": (128 * np.arange(BLOCKS)[None, :] + lanes).astype(f),
    }
    nc = bacc.Bacc("TRN2", target_bir_lowering=False, num_devices=1)
    feed, aps = {}, []
    for name, v in arrays.items():
        v = np.ascontiguousarray(v)
        feed[f"in_{name}"] = v
        aps.append(nc.dram_tensor(f"in_{name}", v.shape, mybir.dt.from_np(v.dtype), kind="ExternalInput").ap())
    o = nc.dram_tensor("out_0", (BATCH, S, D), F32, kind="ExternalOutput").ap()
    build(nc, *aps, o)
    r = run(nc, [feed], core_ids=[0])
    return r.results[0]["out_0"]
```
